# Optimizing a Trainium2 kernel written in Bass

```python
import numpy as np
import jax
import jax.numpy as jnp

def _softmax(x, axis=-1):
    return jax.nn.softmax(x, axis=axis)

def _gelu(x):
    return jax.nn.gelu(x, approximate=True)

def _silu(x):
    return jax.nn.silu(x)

def _sigmoid(x):
    return jax.nn.sigmoid(x)

def _layernorm(x, axis=-1, eps=1e-05):
    m = jnp.mean(x, axis=axis, keepdims=True)
    v = jnp.var(x, axis=axis, keepdims=True)
    return (x - m) / jnp.sqrt(v + eps)

def _scatter_add(tgt, idx, src, axis=0):
    return tgt.at[idx].add(src)

def _segment_sum(src, seg, n):
    return jax.ops.segment_sum(src, seg, n)
kernel_name = 'mk_early_fusion_d2_tok_img256_r4_4693ea'

def setup_inputs(seed: int=0):
    np.random.seed(seed)
    _w = jnp.asarray

    def _rec_inputs():
        import jax
        import jax.numpy as jnp
        _rk = jax.random.key(seed)
        x = -0.000596345 + 1.00056 * jax.random.normal(jax.random.fold_in(_rk, 1), (32, 64, 64, 3), jnp.float32)
        txt = -1.92552e-05 + 0.02 * jax.random.normal(jax.random.fold_in(_rk, 2), (32, 32, 64), jnp.float32)
        return (x, txt)
    x, txt = _rec_inputs()

    def _L0_tok_setup():
        import jax, jax.numpy as jnp
        import numpy as np
        M1 = 20
        M2 = 20

        def _spectral_conv(x, w):
            B, Cin, H, W = x.shape
            x_ft = jnp.fft.rfft2(x, norm='ortho')
            out = jnp.einsum('bixy,ioxy->boxy', x_ft[:, :, :M1, :M2], w.astype(x_ft.dtype))
            out_ft = jnp.zeros((B, w.shape[1], H, W // 2 + 1), dtype=x_ft.dtype)
            out_ft = out_ft.at[:, :, :M1, :M2].set(out)
            return jnp.fft.irfft2(out_ft, s=(H, W), norm='ortho')

        def _gelu(x):
            return jax.nn.gelu(x, approximate=False)
        key = jax.random.key(seed)
        ks = jax.random.split(key, 16)
        B, H, W, width = (16, 64, 64, 32)
        scale = 1.0 / (width * width)
        d = {}
        d['coords'] = jax.random.normal(ks[0], (B, H, W, 3), dtype=jnp.float32)
        d['fc0_w'] = jax.random.normal(ks[1], (3, width), dtype=jnp.float32) * 0.1
        d['fc0_b'] = jnp.zeros((width,), dtype=jnp.float32)
        for i in range(4):
            d[f'sw{i}'] = scale * jax.random.normal(ks[2 + i], (width, width, M1, M2), dtype=jnp.float32)
            d[f'cw{i}'] = jax.random.normal(ks[6 + i], (width, width), dtype=jnp.float32) * 0.1
            d[f'cb{i}'] = jnp.zeros((width,), dtype=jnp.float32)
        d['fc1_w'] = jax.random.normal(ks[10], (width, 64), dtype=jnp.float32) * 0.1
        d['fc1_b'] = jnp.zeros((64,), dtype=jnp.float32)
        d['fc2_w'] = jax.random.normal(ks[11], (64, 1), dtype=jnp.float32) * 0.1
        d['fc2_b'] = jnp.zeros((1,), dtype=jnp.float32)
        return d
    _L0_tok_all = _L0_tok_setup()
    _L0_tok_in = {k: v for k, v in _L0_tok_all.items() if k in ('fc0_w', 'fc0_b', 'sw0', 'cw0', 'cb0', 'sw1', 'cw1', 'cb1', 'sw2', 'cw2', 'cb2', 'sw3', 'cw3', 'cb3', 'fc1_w', 'fc1_b', 'fc2_w', 'fc2_b')}
    del _L0_tok_all

    def _L0_attn_setup():
        import jax, jax.numpy as jnp
        import numpy as np
        key = jax.random.key(seed)
        k1, k2, k3 = jax.random.split(key, 3)
        b, n_t, n, n_h = (8, 256, 64, 8)
        s = jax.random.normal(k1, (b, n_t, n), dtype=jnp.float32)
        Q = jax.random.normal(k2, (n_h, n, n), dtype=jnp.float32) * 0.02
        E = jax.random.normal(k3, (n_h, n, n), dtype=jnp.float32) * 0.02
        return {'s': s, 'Q': Q, 'E': E}
    _L0_attn_all = _L0_attn_setup()
    _L0_attn_in = {k: v for k, v in _L0_attn_all.items() if k in ('Q', 'E')}
    del _L0_attn_all

    def _L0_ffn_setup():
        import jax, jax.numpy as jnp
        import numpy as np
        E, D, H, TOP_K = (6, 64, 64, 2)
        ROUTER_H = D // 2
        key = jax.random.key(seed)
        ks = jax.random.split(key, 12)
        s = 1.0 / np.sqrt(D)
        sh = 1.0 / np.sqrt(H)
        sr = 1.0 / np.sqrt(ROUTER_H)
        return {'features': jax.random.normal(ks[0], (8, 1024, D), dtype=jnp.float32), 'router_w1': jax.random.uniform(ks[1], (D, ROUTER_H), jnp.float32, -s, s), 'router_b1': jnp.zeros((ROUTER_H,), jnp.float32), 'router_w2': jax.random.uniform(ks[2], (ROUTER_H, E), jnp.float32, -sr, sr), 'router_b2': jnp.zeros((E,), jnp.float32), 'expert_w1': jax.random.uniform(ks[3], (E, D, H), jnp.float32, -s, s), 'expert_b1': jnp.zeros((E, H), jnp.float32), 'expert_w2': jax.random.uniform(ks[4], (E, H, H), jnp.float32, -sh, sh), 'expert_b2': jnp.zeros((E, H), jnp.float32), 'expert_w3': jax.random.uniform(ks[5], (E, H, D), jnp.float32, -sh, sh), 'expert_b3': jnp.zeros((E, D), jnp.float32)}
    _L0_ffn_all = _L0_ffn_setup()
    _L0_ffn_in = {k: v for k, v in _L0_ffn_all.items() if k in ('router_w1', 'router_b1', 'router_w2', 'router_b2', 'expert_w1', 'expert_b1', 'expert_w2', 'expert_b2', 'expert_w3', 'expert_b3')}
    del _L0_ffn_all

    def _L1_attn_setup():
        import jax, jax.numpy as jnp
        import numpy as np
        MAX_ADAPTIVE_LR = 0.1

        def _l2n(z):
            n = jnp.linalg.norm(z, axis=-1, keepdims=True)
            return z / jnp.maximum(n, 1e-12)

        def _mlp(params, z):
            W0, W1, P0, P1 = params
            h = z @ W0 + z @ P0
            h = jax.nn.silu(h)
            return h @ W1 + h @ P1
        key = jax.random.key(seed)
        kx, kf, kp0, kp1 = jax.random.split(key, 4)
        B, T, H, E = (4, 64, 64, 4)
        D = H * E
        x = jax.random.normal(kx, (B, T, H), dtype=jnp.float32)
        W_fused = jax.random.normal(kf, (3 * H + 3, H), dtype=jnp.float32) / np.sqrt(H).astype(np.float32)
        W0 = jnp.zeros((H, D), dtype=jnp.float32)
        W1 = jnp.zeros((D, H), dtype=jnp.float32)
        P0 = jax.random.normal(kp0, (H, D), dtype=jnp.float32)
        P1 = jax.random.normal(kp1, (D, H), dtype=jnp.float32)
        return {'x': x, 'W_fused': W_fused, 'W0': W0, 'W1': W1, 'P0': P0, 'P1': P1}
    _L1_attn_all = _L1_attn_setup()
    _L1_attn_in = {k: v for k, v in _L1_attn_all.items() if k in ('W_fused', 'W0', 'W1', 'P0', 'P1')}
    del _L1_attn_all

    def _L1_ffn_setup():
        import math
        import jax, jax.numpy as jnp
        import numpy as np
        CAPACITY_FACTOR = 1.25
        key = jax.random.key(seed)
        ks = jax.random.split(key, 5)
        B, L, D, F, E = (8, 2048, 64, 256, 8)
        h = jax.random.normal(ks[0], (B, L, D), dtype=jnp.float32)
        gate_w = jax.random.normal(ks[1], (D, E), dtype=jnp.float32) * 0.02
        gate_b = jnp.zeros((E,), dtype=jnp.float32)
        w1 = jax.random.normal(ks[2], (E, D, F), dtype=jnp.float32) * (1.0 / math.sqrt(D))
        b1 = jnp.zeros((E, F), dtype=jnp.float32)
        w2 = jax.random.normal(ks[3], (E, F, D), dtype=jnp.float32) * (1.0 / math.sqrt(F))
        b2 = jnp.zeros((E, D), dtype=jnp.float32)
        return {'h': h, 'gate_w': gate_w, 'gate_b': gate_b, 'w1': w1, 'b1': b1, 'w2': w2, 'b2': b2}
    _L1_ffn_all = _L1_ffn_setup()
    _L1_ffn_in = {k: v for k, v in _L1_ffn_all.items() if k in ('gate_w', 'gate_b', 'w1', 'b1', 'w2', 'b2')}
    del _L1_ffn_all
    return {'x': x, 'txt': txt, 'L0_tok_fc0_w': _L0_tok_in['fc0_w'], 'L0_tok_fc0_b': _L0_tok_in['fc0_b'], 'L0_tok_sw0': _L0_tok_in['sw0'], 'L0_tok_cw0': _L0_tok_in['cw0'], 'L0_tok_cb0': _L0_tok_in['cb0'], 'L0_tok_sw1': _L0_tok_in['sw1'], 'L0_tok_cw1': _L0_tok_in['cw1'], 'L0_tok_cb1': _L0_tok_in['cb1'], 'L0_tok_sw2': _L0_tok_in['sw2'], 'L0_tok_cw2': _L0_tok_in['cw2'], 'L0_tok_cb2': _L0_tok_in['cb2'], 'L0_tok_sw3': _L0_tok_in['sw3'], 'L0_tok_cw3': _L0_tok_in['cw3'], 'L0_tok_cb3': _L0_tok_in['cb3'], 'L0_tok_fc1_w': _L0_tok_in['fc1_w'], 'L0_tok_fc1_b': _L0_tok_in['fc1_b'], 'L0_tok_fc2_w': _L0_tok_in['fc2_w'], 'L0_tok_fc2_b': _L0_tok_in['fc2_b'], 'L0_attn_Q': _L0_attn_in['Q'], 'L0_attn_E': _L0_attn_in['E'], 'L0_ffn_router_w1': _L0_ffn_in['router_w1'], 'L0_ffn_router_b1': _L0_ffn_in['router_b1'], 'L0_ffn_router_w2': _L0_ffn_in['router_w2'], 'L0_ffn_router_b2': _L0_ffn_in['router_b2'], 'L0_ffn_expert_w1': _L0_ffn_in['expert_w1'], 'L0_ffn_expert_b1': _L0_ffn_in['expert_b1'], 'L0_ffn_expert_w2': _L0_ffn_in['expert_w2'], 'L0_ffn_expert_b2': _L0_ffn_in['expert_b2'], 'L0_ffn_expert_w3': _L0_ffn_in['expert_w3'], 'L0_ffn_expert_b3': _L0_ffn_in['expert_b3'], 'L1_attn_W_fused': _L1_attn_in['W_fused'], 'L1_attn_W0': _L1_attn_in['W0'], 'L1_attn_W1': _L1_attn_in['W1'], 'L1_attn_P0': _L1_attn_in['P0'], 'L1_attn_P1': _L1_attn_in['P1'], 'L1_ffn_gate_w': _L1_ffn_in['gate_w'], 'L1_ffn_gate_b': _L1_ffn_in['gate_b'], 'L1_ffn_w1': _L1_ffn_in['w1'], 'L1_ffn_b1': _L1_ffn_in['b1'], 'L1_ffn_w2': _L1_ffn_in['w2'], 'L1_ffn_b2': _L1_ffn_in['b2']}

def reference(x, txt, L0_tok_fc0_w, L0_tok_fc0_b, L0_tok_sw0, L0_tok_cw0, L0_tok_cb0, L0_tok_sw1, L0_tok_cw1, L0_tok_cb1, L0_tok_sw2, L0_tok_cw2, L0_tok_cb2, L0_tok_sw3, L0_tok_cw3, L0_tok_cb3, L0_tok_fc1_w, L0_tok_fc1_b, L0_tok_fc2_w, L0_tok_fc2_b, L0_attn_Q, L0_attn_E, L0_ffn_router_w1, L0_ffn_router_b1, L0_ffn_router_w2, L0_ffn_router_b2, L0_ffn_expert_w1, L0_ffn_expert_b1, L0_ffn_expert_w2, L0_ffn_expert_b2, L0_ffn_expert_w3, L0_ffn_expert_b3, L1_attn_W_fused, L1_attn_W0, L1_attn_W1, L1_attn_P0, L1_attn_P1, L1_ffn_gate_w, L1_ffn_gate_b, L1_ffn_w1, L1_ffn_b1, L1_ffn_w2, L1_ffn_b2):
    import jax
    import jax.numpy as jnp

    def _L0_tok_ref(coords, fc0_w, fc0_b, sw0, cw0, cb0, sw1, cw1, cb1, sw2, cw2, cb2, sw3, cw3, cb3, fc1_w, fc1_b, fc2_w, fc2_b):
        import jax, jax.numpy as jnp
        import numpy as np
        M1 = 20
        M2 = 20

        def _spectral_conv(x, w):
            B, Cin, H, W = x.shape
            x_ft = jnp.fft.rfft2(x, norm='ortho')
            out = jnp.einsum('bixy,ioxy->boxy', x_ft[:, :, :M1, :M2], w.astype(x_ft.dtype))
            out_ft = jnp.zeros((B, w.shape[1], H, W // 2 + 1), dtype=x_ft.dtype)
            out_ft = out_ft.at[:, :, :M1, :M2].set(out)
            return jnp.fft.irfft2(out_ft, s=(H, W), norm='ortho')

        def _gelu(x):
            return jax.nn.gelu(x, approximate=False)
        x = coords @ fc0_w + fc0_b
        x = jnp.transpose(x, (0, 3, 1, 2))
        for sw, cw, cb in ((sw0, cw0, cb0), (sw1, cw1, cb1), (sw2, cw2, cb2), (sw3, cw3, cb3)):
            x1 = _spectral_conv(x, sw)
            x2 = jnp.einsum('bchw,oc->bohw', x, cw) + cb[None, :, None, None]
            x = _gelu(x1 + x2)
        x = jnp.transpose(x, (0, 2, 3, 1))
        x = _gelu(x @ fc1_w + fc1_b)
        return (x @ fc2_w + fc2_b)[..., 0]

    def _L0_attn_ref(s, Q, E):
        import jax, jax.numpy as jnp
        import numpy as np
        n_t = s.shape[1]
        qs = jnp.einsum('bti,hij->bhtj', s, Q)
        Omega = jnp.einsum('bhtj,buj->bhtu', qs, s)
        mask = jnp.tril(jnp.ones((n_t, n_t), dtype=s.dtype))
        Omega = Omega * mask
        es = jnp.einsum('hij,buj->bhui', E, s)
        r = jnp.einsum('bhtu,bhui->bti', Omega, es)
        return r

    def _L0_ffn_ref(features, router_w1, router_b1, router_w2, router_b2, expert_w1, expert_b1, expert_w2, expert_b2, expert_w3, expert_b3):
        import jax, jax.numpy as jnp
        import numpy as np
        E, D, H, TOP_K = (6, 64, 64, 2)
        ROUTER_H = D // 2
        rh = jax.nn.relu(features @ router_w1 + router_b1)
        expert_logits = jax.nn.softmax(rh @ router_w2 + router_b2, axis=-1)
        top_w, top_i = jax.lax.top_k(expert_logits, TOP_K)
        routing_weights = jax.nn.softmax(top_w, axis=-1)
        h1 = jax.nn.relu(jnp.einsum('bsd,edh->bseh', features, expert_w1) + expert_b1)
        h2 = jax.nn.relu(jnp.einsum('bseh,ehf->bsef', h1, expert_w2) + expert_b2)
        expert_out = jnp.einsum('bsef,efo->bseo', h2, expert_w3) + expert_b3
        sel = jnp.take_along_axis(expert_out, top_i[:, :, :, None], axis=2)
        combined = jnp.sum(sel * routing_weights[..., None], axis=2)
        return combined

    def _L1_attn_ref(x, W_fused, W0, W1, P0, P1):
        import jax, jax.numpy as jnp
        import numpy as np
        MAX_ADAPTIVE_LR = 0.1

        def _l2n(z):
            n = jnp.linalg.norm(z, axis=-1, keepdims=True)
            return z / jnp.maximum(n, 1e-12)

        def _mlp(params, z):
            W0, W1, P0, P1 = params
            h = z @ W0 + z @ P0
            h = jax.nn.silu(h)
            return h @ W1 + h @ P1
        B, T, H = x.shape
        fp = x @ W_fused.T
        q, k, v, alpha, theta, eta = jnp.split(fp, [H, 2 * H, 3 * H, 3 * H + 1, 3 * H + 2], axis=-1)
        q = _l2n(jax.nn.silu(q))
        k = _l2n(jax.nn.silu(k))
        v = jax.nn.silu(v)
        alpha = jax.nn.sigmoid(alpha)
        theta = jax.nn.sigmoid(theta) * MAX_ADAPTIVE_LR
        eta = jax.nn.sigmoid(eta)
        params0 = (W0, W1, P0, P1)
        bat = lambda p: jnp.broadcast_to(p[None], (B,) + p.shape)
        cur_p = jax.tree_util.tree_map(bat, params0)
        cur_m = jax.tree_util.tree_map(jnp.zeros_like, cur_p)

        def loss_fn(params, kk, vv):
            pred = _mlp(params, kk)
            return jnp.mean((pred - vv) ** 2)

        def step(carry, xs):
            cp, cm = carry
            k_t, v_t, q_t, a_t, th_t, e_t = xs
            g = jax.vmap(jax.grad(loss_fn))(cp, k_t, v_t)
            s = lambda c: c[:, :, None]
            nm = jax.tree_util.tree_map(lambda m, gg: m * s(e_t) - s(th_t) * gg, cm, g)
            np_ = jax.tree_util.tree_map(lambda p, m: p * (1.0 - s(a_t)) + m, cp, nm)
            out_t = jax.vmap(_mlp, in_axes=(0, 0))(np_, q_t)
            new_carry = jax.lax.stop_gradient((np_, nm))
            return (new_carry, out_t)
        tT = lambda a: jnp.swapaxes(a, 0, 1)
        xs = tuple(map(tT, (k, v, q, alpha, theta, eta)))
        _, ys = jax.lax.scan(step, (cur_p, cur_m), xs)
        return jnp.swapaxes(ys, 0, 1)

    def _L1_ffn_ref(h, gate_w, gate_b, w1, b1, w2, b2):
        import math
        import jax, jax.numpy as jnp
        import numpy as np
        CAPACITY_FACTOR = 1.25
        B, L, D = h.shape
        E = gate_w.shape[1]
        T = B * L
        C = max(1, math.ceil(CAPACITY_FACTOR * T / E))
        x = h.reshape(T, D)
        logits = x @ gate_w + gate_b
        probs = jax.nn.softmax(logits, axis=-1)
        idx = jnp.argmax(probs, axis=-1)
        prb = jnp.take_along_axis(probs, idx[:, None], axis=1)[:, 0]
        one_hot = jax.nn.one_hot(idx, E, dtype=jnp.float32)
        pos = (jnp.cumsum(one_hot, axis=0) * one_hot).sum(-1).astype(jnp.int32) - 1
        kept = pos < C
        pos_safe = jnp.where(kept, pos, C)
        buf = jnp.zeros((E, C, D), dtype=h.dtype).at[idx, pos_safe].set(x, mode='drop')
        hmid = jax.nn.relu(jnp.einsum('ecd,edf->ecf', buf, w1) + b1[:, None, :])
        ybuf = jnp.einsum('ecf,efd->ecd', hmid, w2) + b2[:, None, :]
        pos_g = jnp.minimum(pos, C - 1)
        y_tok = ybuf[idx, pos_g] * (prb * kept)[:, None]
        y = y_tok.reshape(B, L, D)
        y = jnp.nan_to_num(y, nan=0.0, posinf=10000.0, neginf=-10000.0)
        return y
    h = _L0_tok_ref(x, L0_tok_fc0_w, L0_tok_fc0_b, L0_tok_sw0, L0_tok_cw0, L0_tok_cb0, L0_tok_sw1, L0_tok_cw1, L0_tok_cb1, L0_tok_sw2, L0_tok_cw2, L0_tok_cb2, L0_tok_sw3, L0_tok_cw3, L0_tok_cb3, L0_tok_fc1_w, L0_tok_fc1_b, L0_tok_fc2_w, L0_tok_fc2_b)
    h = jnp.concatenate([h, txt], axis=1)
    h = h + _L0_attn_ref(_layernorm(h, axis=-1), L0_attn_Q, L0_attn_E)
    h = h + _L0_ffn_ref(_layernorm(h, axis=-1), L0_ffn_router_w1, L0_ffn_router_b1, L0_ffn_router_w2, L0_ffn_router_b2, L0_ffn_expert_w1, L0_ffn_expert_b1, L0_ffn_expert_w2, L0_ffn_expert_b2, L0_ffn_expert_w3, L0_ffn_expert_b3)
    h = h + _L1_attn_ref(_layernorm(h, axis=-1), L1_attn_W_fused, L1_attn_W0, L1_attn_W1, L1_attn_P0, L1_attn_P1)
    h = h + _L1_ffn_ref(_layernorm(h, axis=-1), L1_ffn_gate_w, L1_ffn_gate_b, L1_ffn_w1, L1_ffn_b1, L1_ffn_w2, L1_ffn_b2)
    return h

_drawn_inputs = setup_inputs


def setup_inputs(seed=0):
    import zlib

    import numpy as np

    out = dict(_drawn_inputs(seed))
    spreads = {'L0_tok_fc0_b': (0.0, 0.286),
     'L0_tok_cb0': (0.0, 0.1),
     'L0_tok_cb1': (0.0, 0.1),
     'L0_tok_cb2': (0.0, 0.1),
     'L0_tok_cb3': (0.0, 0.1),
     'L0_tok_fc1_b': (0.0, 0.1),
     'L0_ffn_router_b1': (0.0, 0.1),
     'L0_ffn_router_b2': (0.0, 0.1),
     'L0_ffn_expert_b1': (0.0, 0.1),
     'L0_ffn_expert_b2': (0.0, 0.1),
     'L0_ffn_expert_b3': (0.0, 0.1),
     'L1_attn_W0': (0.0, 0.514),
     'L1_attn_W1': (0.0, 0.508),
     'L1_ffn_gate_b': (0.0, 0.1),
     'L1_ffn_b1': (0.0, 0.8),
     'L1_ffn_b2': (0.0, 0.8)}
    factors = {'L0_tok_sw0': 8.0, 'L0_tok_sw1': 8.0, 'L0_tok_sw2': 8.0, 'L0_tok_sw3': 5.222}
    for name, (base, spread) in spreads.items():
        noise = np.random.default_rng([zlib.crc32(name.encode()), seed]).standard_normal(out[name].shape)
        drawn = base * np.exp(spread * noise) if base else spread * noise
        out[name] = jnp.asarray(drawn.astype(out[name].dtype))
    for name, factor in factors.items():
        out[name] = (out[name] * factor).astype(out[name].dtype)
    return out
```

```python
from contextlib import ExitStack

import numpy as np
import concourse.bass as bass
from concourse import mybir

F32 = mybir.dt.float32
ALU = mybir.AluOpType
ACT = mybir.ActivationFunctionType
AX = mybir.AxisListType

NB = 32
NT = 96
DM = 64
TOK = NB * NT
EPS = 1e-5
MAX_LR = 0.1


def bc(ap, *shape):
    return ap.broadcast_to(list(shape))


class Steps:

    def __init__(self, eng, sem, base=0):
        self.eng, self.sem, self.base, self.n = eng, sem, base, 0

    def mark(self, ins):
        ins.then_inc(self.sem, 1)
        self.n += 1
        return self.n

    def link(self, ins):
        self.mark(ins)
        self.eng.wait_ge(self.sem, self.base + self.n)


C = 32
S = 64
MO = 20
KG, KJ = 5, 4
NL = 4
NGRP = 4


def spectral_constants():
    n = np.arange(S)
    kx = np.array([KG * j + g for g in range(KG) for j in range(KJ)])
    ky = np.arange(MO)
    scale = 1.0 / np.sqrt(S)
    cx, sx = (f(2 * np.pi * np.outer(n, kx) / S) * scale for f in (np.cos, np.sin))
    cy, sy = (f(2 * np.pi * np.outer(n, ky) / S) * scale for f in (np.cos, np.sin))
    d1 = np.zeros((2, S, 2, 2, MO))
    d2 = np.zeros((2, 2, S, MO, 2, 2))
    e1 = np.zeros((2, MO, 2, 2, S))
    e2 = np.zeros((128, 2, S))
    twice = np.where(ky == 0, 1.0, 2.0)[:, None]
    ck, sk = (f(2 * np.pi * np.outer(ky, n) / S) * scale for f in (np.cos, np.sin))
    for b in range(2):
        d1[b, :, b, 0], d1[b, :, b, 1] = cx, -sx
        d2[0, b, :, :, b, 0], d2[0, b, :, :, b, 1] = cy, -sy
        d2[1, b, :, :, b, 0], d2[1, b, :, :, b, 1] = sy, cy
        e1[b, :, 0, b, :], e1[b, :, 1, b, :] = twice * ck, -twice * sk
        e2[b * 40:b * 40 + 20, b], e2[b * 40 + 20:b * 40 + 40, b] = ck, -sk
    e2[96] = 1.0
    f = lambda a, *s: np.ascontiguousarray(a.reshape(s).astype(np.float32))
    return dict(d1=f(d1, 128, 80), d2=f(d2.reshape(2, 128, 80).transpose(1, 0, 2), 128, 160), e1=f(e1, 80, 128), e2=f(e2, 128, 128))


def image_network(nc, x, h_out, ident, consts, fc0_w, fc0_b, sw, cw, cb, fc1_w, fc1_b, fc2_w, fc2_b):
    RING = 6
    PH = 8
    with ExitStack() as ctx:
        sb = lambda n, sh: ctx.enter_context(nc.sbuf_tensor("im_" + n, sh, F32))
        sem = lambda n: ctx.enter_context(nc.semaphore("im_" + n))
        a = sb("a", [128, NGRP, 2 * S * C])
        spec = sb("spec", [128, KG * MO, 32])
        mixed = sb("mixed", [128, KG, NGRP, 2, 2, 80])
        half_t = sb("half_t", [128, 2, 2560])
        u = sb("u", [97, 2 * S * C])
        wbd = sb("wbd", [128, 128, KG * MO])
        chan = sb("chan", [128, 2, 512])
        xi = sb("xi", [128, 2, 2, 192])
        xt = sb("xt", [97, 4, 128])
        fc0 = sb("fc0", [97, 1024])
        d1, d2, e1, e2 = sb("d1", [128, 80]), sb("d2", [128, 2, 80]), sb("e1", [80, 128]), sb("e2", [128, 128])
        cwn, cwt = sb("cwn", [128, 128]), sb("cwt", [128, NL, 128])
        fc1 = sb("fc1", [128, 2, 128])
        fc1b, fc2, fc2b = sb("fc1b", [128, 1]), sb("fc2", [128, 2]), sb("fc2b", [128, 1])
        ho = sb("ho", [128, 2, S])
        gl = half_t[:, :, 0:512]
        ring = ctx.enter_context(nc.psum_tensor("im_ring", [128, RING, 512], F32))
        acc = ctx.enter_context(nc.psum_tensor("im_acc", [128, 2, 512], F32))
        zeroed, loaded, cw_in, cw_turned, cw_ready = sem("zeroed"), sem("loaded"), sem("cw_in"), sem("cw_turned"), sem("cw_ready")
        with nc.Block() as block:
            @block.gpsimd
            def _(pool):
                nc.gpsimd.memset(wbd[:, :, :], 0.0).then_inc(zeroed, 1)

            @block.vector
            def _(dve):
                for t in (u[64:97, :], xt[:, :, :], fc0[:, :], cwn[:, :], fc1[:, :, :], fc2[:, :]):
                    nc.vector.memset(t, 0.0).then_inc(zeroed, 1)
                dve.wait_ge(zeroed, 7)
                nc.vector.memset(xt[96:97, :, :], 1.0).then_inc(zeroed, 1)
                for l in range(NL):
                    dve.wait_ge(cw_turned, l + 1)
                    nc.vector.tensor_copy(cwt[:, l, :], acc[:, l % 2, 0:128]).then_inc(cw_ready, 1)
                dve.wait_ge(cw_ready, NL)
                dve.wait_ge(zeroed, 8)

            @block.tensor
            def _(pe):
                for l in range(NL):
                    pe.wait_ge(cw_in, 64 * (l + 1))
                    if l >= 2:
                        pe.wait_ge(cw_ready, l - 1)
                    nc.tensor.transpose(acc[:, l % 2, 0:128], cwn[:, :], ident[:, :]).then_inc(cw_turned, 1)

            @block.sync
            def _(sp):
                sp.wait_ge(zeroed, 7)
                for l in range(NL):
                    if l:
                        sp.wait_ge(cw_turned, l)
                    for k in range(4):
                        sp.dma_start(cwn[k * C:(k + 1) * C, k * C:(k + 1) * C], cw[l]).then_inc(cw_in, 16)

            @block.scalar
            def _(act):
                n = 0
                act.wait_ge(zeroed, 7)
                with nc.allow_non_contiguous_dma(reason="small weights"):
                    for dst, src in ((d1[:, :], consts["d1"]), (d2[:, :, :].rearrange("p a c -> p (a c)"), consts["d2"]), (e1[:, :], consts["e1"]), (e2[:, :], consts["e2"]),
                                     (fc0[96:97, :].rearrange("p (w c) -> p w c", c=C), fc0_b.rearrange("(a b c) -> a b c", a=1, b=1).broadcast_to([1, 32, C])),
                                     (fc2b[:, :], fc2_b.rearrange("(a b) -> a b", a=1).broadcast_to([128, 1]))):
                        act.dma_start(dst, src).then_inc(loaded, 16)
                        n += 1
                    for k in range(4):
                        act.dma_start(fc1[k * C:(k + 1) * C, k // 2, k % 2 * 64:(k % 2 + 1) * 64], fc1_w).then_inc(loaded, 16)
                    for k in range(2):
                        act.dma_start(fc1b[k * 64:(k + 1) * 64, :], fc1_b.rearrange("(p a) -> p a", a=1)).then_inc(loaded, 16)
                        act.dma_start(fc2[k * 64:(k + 1) * 64, k:k + 1], fc2_w).then_inc(loaded, 16)
                    for k in range(32):
                        act.dma_start(fc0[3 * k:3 * k + 3, k * C:(k + 1) * C], fc0_w).then_inc(loaded, 16)
                    n += 4 + 4 + 32
                act.wait_ge(loaded, 16 * n)

        filled, drained = sem("filled"), sem("drained")
        acc_full, acc_read = sem("acc_full"), sem("acc_read")
        w_in, bias_in, xi_in = sem("w_in"), sem("bias_in"), [sem("xi_in0"), sem("xi_in1")]
        ho_ready, ho_stored = sem("ho_ready"), sem("ho_stored")
        FC0_FILLS, LAYER_FILLS, FC_FILLS = 4 * 9, 4 * 8 + 10 + 4 * 21, 4 * 10
        HALF_FILLS = FC0_FILLS + NL * LAYER_FILLS + FC_FILLS
        LAYER_ACC, HALF_ACC = 4 * PH, NL * 4 * PH + 4 * PH * 2
        assert LAYER_FILLS % RING == 0
        MIXED_AT = 4 * 8 + 10
        img = x.rearrange("(n b c) h w k -> n b h c (w k)", b=2, c=2)
        out_img = h_out.rearrange("(n b c) h w -> n b h c w", b=2, c=2)

        class Fills:
            def __init__(self, start, base=0):
                self.n, self.bank, self.base = start, start % RING, base
            def next(self):
                n, bank = self.n, self.bank
                self.n, self.bank = n + 1, (bank + 1) % RING
                return self.base + n, bank

        with nc.Block() as block:
            @block.sync
            def _(sp):
                for half in range(2):
                    base = half * HALF_FILLS
                    for l in range(NL):
                        r = NL * half + l
                        if r:
                            sp.wait_ge(filled, base + FC0_FILLS + (l - 1) * LAYER_FILLS + MIXED_AT if l else base - FC_FILLS - LAYER_FILLS + MIXED_AT)
                        for j in range(KJ):
                            o = slice(j * C, (j + 1) * C)
                            sp.dma_start(wbd[o, o, :], sw[l][:, :, KG * j:KG * (j + 1), :].rearrange("i o x y -> i o (x y)")).then_inc(w_in, 16)
                        if r:
                            sp.wait_ge(acc_full, half * HALF_ACC + l * LAYER_ACC if l else half * HALF_ACC - 4 * PH * 2)
                        sp.dma_start(u[96:97, :].rearrange("p (w c) -> p w c", c=C),
                                     cb[l].rearrange("(a b c) -> a b c", a=1, b=1).broadcast_to([1, 2 * S, C])).then_inc(bias_in, 16)

            @block.gpsimd
            def _(pool):
                def load_image(n):
                    if n >= 2:
                        pool.wait_ge(filled, (n - 2) // NGRP * HALF_FILLS + (n - 2) % NGRP * 9 + 1)
                    for b2 in range(2):
                        pool.dma_start(xi[b2 * S:(b2 + 1) * S, n % 2, :, :], img[n, b2]).then_inc(xi_in[n % 2], 16)

                def store_result(n):
                    pool.wait_ge(ho_ready, n + 1)
                    for b2 in range(2):
                        pool.dma_start(out_img[n, b2], ho[b2 * S:(b2 + 1) * S, :, :]).then_inc(ho_stored, 16)

                for n in range(NGRP + 2):
                    load_image(n)
                for n in range(NGRP):
                    store_result(n)
                for n in range(NGRP + 2, 2 * NGRP):
                    load_image(n)
                for n in range(NGRP, 2 * NGRP):
                    store_result(n)
                pool.wait_ge(ho_stored, 32 * 2 * NGRP)

            def second_layer(pe, MM, item, start):
                n, p, v = item
                if p + v == 0:
                    pe.wait_ge(drained, start + 4 + 1)
                pe.wait_ge(acc_read, n + 3)
                for m in range(4):
                    col = p * 16 + m * 4 + v * 2
                    mm = MM(ring[:, (start + 4) % RING, col:col + 2], gl[:, v, m * 128:(m + 1) * 128], fc2[:, :], start=True, stop=True)
                return mm

            @block.tensor
            def _(pe):
                T, MM = nc.tensor.transpose, nc.tensor.matmul

                def fill(f):
                    n, bank = f.next()
                    pe.wait_ge(drained, n + 1)
                    return ring[:, bank, :]

                def have(n):
                    pe.wait_ge(drained, n + RING)

                def input_layer(f, half):
                    for g in range(NGRP):
                        n = half * NGRP + g
                        pe.wait_ge(xi_in[n % 2], 32 * (n // 2 + 1))
                        ps = fill(f)
                        for k in range(4):
                            mm = T(ps[0:96, k * 128:(k + 1) * 128], xi[:, n % 2, k // 2, k % 2 * 96:(k % 2 + 1) * 96], ident[:, :])
                        mm.then_inc(filled, 1)
                        have(f.n)
                        for p in range(PH):
                            ps = fill(f)
                            MM(ps, xt[:, p // 2, :], fc0[:, p % 2 * 512:(p % 2 + 1) * 512], start=True, stop=True).then_inc(filled, 1)

                def rows_transform(f, g):
                    for q in range(0, C, 6):
                        ps = fill(f)
                        for i, c in enumerate(range(q, min(q + 6, C))):
                            mm = MM(ps[:, i * 80:(i + 1) * 80], a[:, g, c:2 * S * C:C], d1[:, :], start=True, stop=True)
                        mm.then_inc(filled, 1)

                def columns_transform(f, g):
                    for b2 in range(2):
                        ps = fill(f)
                        for k in range(KG):
                            for r in range(2):
                                o = (b2 * 2 + r) * 640 + k * 128
                                mm = MM(ps[:, k * 80:(k + 1) * 80], half_t[:, g % 2, o:o + 128], d2[:, r, :], start=r == 0, stop=r == 1)
                        mm.then_inc(filled, 1)

                def mixing(f, r):
                    pe.wait_ge(w_in, 64 * r + 64)
                    for k in range(KG):
                        for y in range(0, MO, 10):
                            ps = fill(f)[:, 0:320].rearrange("p (b y r) -> p b y r", b=16, r=2)
                            for i in range(10):
                                m = k * MO + y + i
                                mm = MM(ps[:, :, i, :], wbd[:, :, m], spec[:, m, :].rearrange("p (b r) -> p b r", r=2), start=True, stop=True)
                            mm.then_inc(filled, 1)

                def turn_mixed(f, g):
                    for k in range(KG):
                        ps = fill(f)
                        for q in range(4):
                            mm = T(ps[0:80, q * 128:(q + 1) * 128], mixed[:, k, g, q // 2, q % 2, :], ident[:, :])
                        mm.then_inc(filled, 1)

                def columns_inverse(f, g):
                    for q in range(0, C, 4):
                        ps = fill(f)
                        for i in range(4):
                            mm = MM(ps[0:80, i * 128:(i + 1) * 128], half_t[0:80, g % 2, q + i:2560:C], e1[:, :], start=True, stop=True)
                        mm.then_inc(filled, 1)

                def turn_activations(f, g, p):
                    ps = fill(f)
                    for m in range(4):
                        o = p * 512 + m * 128
                        mm = T(ps[:, m * 128:(m + 1) * 128], a[:, g, o:o + 128], ident[:, :])
                    mm.then_inc(filled, 1)
                    return f.n

                for half in range(2):
                    at, acc_at = half * HALF_FILLS, half * HALF_ACC
                    if half == 0:
                        pe.sem_inc(drained, RING)
                        pe.sem_inc(acc_read, 2)
                    input_layer(Fills(at), half)
                    at += FC0_FILLS
                    with pe.Fori(0, NL) as l:
                        f = Fills(at, l * LAYER_FILLS)
                        first, acc_base = f.n, acc_at + l * LAYER_ACC
                        pe.wait_ge(acc_read, acc_base + 2)
                        have(f.base + f.n)
                        marks = {}
                        for g in range(NGRP):
                            rows_transform(f, g)
                            marks[g] = f.n
                            if g:
                                have(f.base + marks[g - 1])
                                columns_transform(f, g - 1)
                        have(f.base + marks[NGRP - 1])
                        columns_transform(f, NGRP - 1)
                        have(f.base + f.n)
                        mixing(f, NL * half + l)
                        have(f.base + f.n)
                        turn_mixed(f, 0)
                        for g in range(NGRP):
                            have(f.base + f.n)
                            columns_inverse(f, g)
                            if g + 1 < NGRP:
                                turn_mixed(f, g + 1)
                            chan_at = turn_activations(f, g, 0)
                            for p in range(PH):
                                n = acc_base + g * PH + p
                                nxt = turn_activations(f, g, p + 1) if p + 1 < PH else None
                                have(f.base + chan_at)
                                if g + p == 0:
                                    pe.wait_ge(bias_in, 16 * (NL * half + l) + 16)
                                pe.wait_ge(acc_read, n + 1)
                                MM(acc[:, p % 2, :], e2[0:97, :], u[:, p * 512:(p + 1) * 512], start=True, stop=True, skip_group_check=True)
                                for m in range(4):
                                    mm = MM(acc[:, p % 2, m * 128:(m + 1) * 128], chan[:, p % 2, m * 128:(m + 1) * 128],
                                            cwt[:, bass.ds(l, 1), :].rearrange("p a c -> p (a c)"), start=False, stop=True, skip_group_check=True)
                                mm.then_inc(acc_full, 1)
                                chan_at = nxt
                        assert f.n == first + LAYER_FILLS
                    at += NL * LAYER_FILLS
                    acc_at += NL * LAYER_ACC
                    pe.wait_ge(acc_read, acc_at + 2)
                    f = Fills(at)
                    for g in range(NGRP):
                        for q in range(2):
                            start = f.n
                            turn_activations(f, g, 4 * q)
                            pend = []
                            for p in range(4):
                                if p < 3:
                                    turn_activations(f, g, 4 * q + p + 1)
                                have(start + p + 1)
                                for v in range(2):
                                    n = acc_at + ((g * 2 + q) * 4 + p) * 2 + v
                                    pe.wait_ge(acc_read, n + 1)
                                    MM(acc[:, v, :], fc1[:, v, :], chan[:, p % 2, :], start=True, stop=True).then_inc(acc_full, 1)
                                    pend.append((n, p, v))
                                    if len(pend) == 2:
                                        second_layer(pe, MM, pend.pop(0), start)
                            second_layer(pe, MM, pend.pop(0), start).then_inc(filled, 1)
                            f.next()

            @block.vector
            def _(dve):
                V = nc.vector

                def drain(f):
                    n, bank = f.next()
                    dve.wait_ge(filled, n + 1)
                    return ring[:, bank, :]

                for half in range(2):
                    at = half * HALF_FILLS
                    f = Fills(at)
                    for g in range(NGRP):
                        V.tensor_copy(xt[0:96, :, :].rearrange("p a c -> p (a c)"), drain(f)[0:96, :]).then_inc(drained, 1)
                        for p in range(PH):
                            V.tensor_copy(a[:, g, p * 512:(p + 1) * 512], drain(f)).then_inc(drained, 1)
                    at += FC0_FILLS
                    with dve.Fori(0, NL) as l:
                        f = Fills(at, l * LAYER_FILLS)

                        def rows(g):
                            for q in range(0, C, 6):
                                w = min(6, C - q)
                                src = drain(f)[:, 0:w * 80].rearrange("p (c n) -> p c n", n=80)
                                V.tensor_copy(half_t[:, g % 2, :].rearrange("p (n c) -> p c n", c=C)[:, q:q + w, :], src).then_inc(drained, 1)

                        def columns(g):
                            for b2 in range(2):
                                o = (g * 2 + b2) * 4
                                V.tensor_copy(spec[:, :, o:o + 4], drain(f)[:, 0:400].rearrange("p (m n) -> p m n", n=4)).then_inc(drained, 1)

                        for g in range(NGRP):
                            rows(g)
                            if g:
                                columns(g - 1)
                        columns(NGRP - 1)
                        for k in range(KG):
                            for y in range(0, MO, 10):
                                src = drain(f)[:, 0:320].rearrange("p (n b m) -> p n b m", n=8, b=2)
                                dst = mixed[:, k, :, :, :, :].rearrange("p g b r (c y) -> p (g b) r c y", c=2)
                                V.tensor_copy(dst[:, :, 0, :, 2 * y:2 * y + 20], src)
                                V.tensor_copy(dst[:, :, 1, :, 2 * y:2 * y + 20:2], src[:, :, :, 1:20:2])
                                V.tensor_scalar(dst[:, :, 1, :, 2 * y + 1:2 * y + 20:2], src[:, :, :, 0:20:2], -1.0, None, ALU.mult).then_inc(drained, 1)

                        def turned(g):
                            for k in range(KG):
                                src = drain(f)[0:80, :].rearrange("p (n o) -> p n o", o=C)
                                V.tensor_copy(half_t[0:80, g % 2, :].rearrange("p (n k o) -> p n k o", k=KG, o=C)[:, :, k, :], src).then_inc(drained, 1)

                        turned(0)
                        for g in range(NGRP):
                            for q in range(0, C, 4):
                                src = drain(f)[0:80, :].rearrange("p (o w) -> p o w", o=4)
                                V.tensor_copy(u[0:80, :].rearrange("p (w o) -> p o w", o=C)[:, q:q + 4, :], src).then_inc(drained, 1)
                            if g + 1 < NGRP:
                                turned(g + 1)
                            for p in range(PH):
                                V.tensor_copy(chan[:, p % 2, :], drain(f)).then_inc(drained, 1)
                    at += NL * LAYER_FILLS
                    f = Fills(at)
                    for g in range(NGRP):
                        for q in range(2):
                            for p in range(4):
                                V.tensor_copy(chan[:, p % 2, :], drain(f)).then_inc(drained, 1)
                            n = half * NGRP + g
                            if q == 0 and n >= 1:
                                dve.wait_ge(ho_stored, 32 * n)
                            V.tensor_scalar(ho[:, q, :], drain(f)[:, 0:S], fc2b[:, 0:1], None, ALU.add).then_inc(drained, 1)
                        dve.wait_ge(drained, f.n + RING)
                        V.sem_inc(ho_ready, 1)

            @block.scalar
            def _(act):
                for half in range(2):
                    with act.Fori(0, NL) as l:
                        for g in range(NGRP):
                            for p in range(PH):
                                act.wait_ge(acc_full, half * HALF_ACC + l * LAYER_ACC + g * PH + p + 1)
                                nc.scalar.activation(a[:, g, p * 512:(p + 1) * 512], acc[:, p % 2, :], ACT.Gelu).then_inc(acc_read, 1)
                    for n in range(4 * PH * 2):
                        act.wait_ge(acc_full, half * HALF_ACC + NL * LAYER_ACC + n + 1)
                        nc.scalar.activation(gl[:, n % 2, :], acc[:, n % 2, :], ACT.Gelu, bias=fc1b[:, 0:1]).then_inc(acc_read, 1)


def layernorm_semaphores(nc, ctx):
    return {n: ctx.enter_context(nc.semaphore("ln_" + n))
            for n in ("step", "var_ready", "root_ready", "normed", "turned", "copied_a", "copied_v")}


def layernorm_transposed(nc, sems, turn, H, XN, sq, XT, ident):
    G = 4
    with ExitStack() as ctx:
        st = ctx.enter_context(nc.sbuf_tensor(f"ln_st{turn}", [NT, 8, NB], F32))
        ps = ctx.enter_context(nc.psum_tensor(f"ln_ps{turn}", [DM, 4, 512], F32))
        step, var_ready, root_ready, normed = sems["step"], sems["var_ready"], sems["root_ready"], sems["normed"]
        turned, copied_a, copied_v = sems["turned"], sems["copied_a"], sems["copied_v"]
        LINKS, FILLS, HALF = 10, NB // G, NB // G // 2
        sums, mean, var, root, inv, other = (st[:, i, :] for i in range(6))
        wide = lambda s: bc(s.unsqueeze(2), NT, NB, DM)
        with nc.Block() as block:
            @block.vector
            def _(dve):
                s = Steps(dve, step, turn * LINKS)
                s.link(nc.vector.reduce_sum(sums, H[:, :, :], AX.X))
                s.link(nc.vector.tensor_scalar(mean, sums, 1.0 / DM, None, ALU.mult))
                s.link(nc.vector.tensor_tensor(XN[:, :, :], H[:, :, :], wide(mean), ALU.subtract))
                s.link(nc.vector.tensor_tensor(sq[:, :, :], XN[:, :, :], XN[:, :, :], ALU.mult))
                s.link(nc.vector.reduce_sum(sums, sq[:, :, :], AX.X))
                nc.vector.tensor_scalar(var, sums, 1.0 / DM, EPS, ALU.mult, ALU.add).then_inc(var_ready, 1)
                dve.wait_ge(var_ready, turn + 1)
                dve.wait_ge(root_ready, turn + 1)
                s.link(nc.vector.reciprocal(inv, root))
                s.link(nc.vector.tensor_tensor(other, var, inv, ALU.mult))
                s.link(nc.vector.tensor_tensor(sums, other, root, ALU.add))
                s.link(nc.vector.tensor_scalar(other, sums, 0.5, None, ALU.mult))
                s.link(nc.vector.reciprocal(inv, other))
                nc.vector.tensor_tensor(XN[:, :, :], XN[:, :, :], wide(inv), ALU.mult).then_inc(normed, 1)
                for g in range(1, NB // G, 2):
                    dve.wait_ge(turned, turn * FILLS + g + 1)
                    nc.vector.tensor_copy(XT[:, g * G * NT:(g + 1) * G * NT], ps[:, g % 4, 0:G * NT]).then_inc(copied_v, 1)
                dve.wait_ge(copied_v, (turn + 1) * HALF)
                assert s.n == LINKS

            @block.scalar
            def _(act):
                act.wait_ge(var_ready, turn + 1)
                nc.scalar.activation(root, var, ACT.Sqrt).then_inc(root_ready, 1)
                for g in range(0, NB // G, 2):
                    act.wait_ge(turned, turn * FILLS + g + 1)
                    nc.scalar.activation(XT[:, g * G * NT:(g + 1) * G * NT], ps[:, g % 4, 0:G * NT], ACT.Copy).then_inc(copied_a, 1)
                act.wait_ge(copied_a, (turn + 1) * HALF)

            @block.tensor
            def _(pe):
                pe.wait_ge(normed, turn + 1)
                for g in range(NB // G):
                    if g >= 4:
                        pe.wait_ge(copied_a if g % 2 == 0 else copied_v, turn * HALF + (g - 4) // 2 + 1)
                    for j in range(G):
                        mm = nc.tensor.transpose(ps[:, g % 4, j * NT:(j + 1) * NT], XN[:, g * G + j, :], ident[0:NT, 0:NT])
                    mm.then_inc(turned, 1)


def linear_attention(nc, H, XT, ident, Q, E):
    NH = 8
    with ExitStack() as ctx:
        sb = lambda n, sh: ctx.enter_context(nc.sbuf_tensor(n, sh, F32))
        pb = lambda n, sh: ctx.enter_context(nc.psum_tensor(n, sh, F32))
        sem = lambda n: ctx.enter_context(nc.semaphore(n))
        q_w = sb("at_q_w", [DM, NH, DM])
        e_w = sb("at_e_w", [DM, NH, DM])
        e_t = sb("at_e_t", [DM, NH, DM])
        causal = sb("at_causal", [NT, NT])
        s_t = sb("at_s_t", [DM, 2, NT])
        es = sb("at_es", [NT, 2, NH * DM])
        qs = sb("at_qs", [DM, 2, NH * NT])
        om = sb("at_om", [NT, 2, NH, NT])
        psE = pb("at_psE", [NT, 2, 512])
        psQ = pb("at_psQ", [DM, 2, 512])
        psO = pb("at_psO", [NT, 2, 512])
        psR = pb("at_psR", [NT, 2, 512])
        HH = NH // 2 * NT
        loaded, ones, mask_ready = sem("at_loaded"), sem("at_ones"), sem("at_mask_ready")
        e_turned, e_ready = sem("at_e_turned"), sem("at_e_ready")
        staged, es_done, es_ready = sem("at_staged"), sem("at_es_done"), sem("at_es_ready")
        qs_done, qs_ready = sem("at_qs_done"), sem("at_qs_ready")
        om_done, om_ready, r_done, r_added = sem("at_om_done"), sem("at_om_ready"), sem("at_r_done"), sem("at_r_added")
        with nc.Block() as block:
            @block.sync
            def _(sp):
                sp.dma_start(q_w[:, :, :], Q.rearrange("h i j -> i h j")).then_inc(loaded, 16)
                sp.dma_start(e_w[:, :, :], E.rearrange("h i j -> i h j")).then_inc(loaded, 16)

            @block.gpsimd
            def _(pool):
                nc.gpsimd.memset(causal[:, :], 1.0).then_inc(ones, 1)
                pool.wait_ge(ones, 1)
                nc.gpsimd.affine_select(out=causal[:, :], in_=causal[:, :], compare_op=ALU.is_ge, fill=0.0,
                                        base=0, pattern=[[1, NT]], channel_multiplier=-1).then_inc(mask_ready, 1)
                for k in range(2):
                    nc.gpsimd.tensor_copy(s_t[:, k, :], XT[:, k * NT:(k + 1) * NT]).then_inc(staged, 1)
                with pool.Fori(0, NB // 2 - 1) as p:
                    for k in range(2):
                        pool.wait_ge(om_done, 2 * p + k + 1)
                        nc.gpsimd.tensor_copy(s_t[:, k, :], XT[:, bass.ds((2 * p + 2 + k) * NT, NT)]).then_inc(staged, 1)

            @block.tensor
            def _(pe):
                pe.wait_ge(loaded, 32)
                for h in range(NH):
                    mm = nc.tensor.transpose(psQ[:, 0, h * DM:(h + 1) * DM], e_w[:, h, :], ident[0:DM, 0:DM])
                mm.then_inc(e_turned, 1)
                pe.wait_ge(e_ready, 1)

                def products_es(k, n):
                    pe.wait_ge(staged, n + 1)
                    nc.tensor.matmul(psE[:, k, :], s_t[:, k, :], e_t[:, :, :].rearrange("j h i -> j (h i)"),
                                     start=True, stop=True).then_inc(es_done, 1)

                def products_qs(k, n):
                    for h in range(NH):
                        mm = nc.tensor.matmul(psQ[:, h // 4, h % 4 * NT:(h % 4 + 1) * NT], q_w[:, h, :], s_t[:, k, :],
                                              start=True, stop=True)
                    mm.then_inc(qs_done, 1)

                def products_om(k, n):
                    pe.wait_ge(qs_ready, n + 1)
                    for half in range(2):
                        mm = nc.tensor.matmul(psO[:, half, 0:HH], s_t[:, k, :], qs[:, k, half * HH:(half + 1) * HH],
                                              start=True, stop=True)
                    mm.then_inc(om_done, 1)

                def products_r(k, n):
                    pe.wait_ge(es_ready, n + 1)
                    pe.wait_ge(om_ready, n + 1)
                    for h in range(NH):
                        mm = nc.tensor.matmul(psR[:, k, 0:DM], om[:, k, h, :], es[:, k, h * DM:(h + 1) * DM],
                                              start=h == 0, stop=h == NH - 1)
                    mm.then_inc(r_done, 1)

                with pe.Fori(0, NB // 2) as p:
                    products_es(0, 2 * p)
                    products_qs(0, 2 * p)
                    products_es(1, 2 * p + 1)
                    products_om(0, 2 * p)
                    products_qs(1, 2 * p + 1)
                    products_r(0, 2 * p)
                    products_om(1, 2 * p + 1)
                    products_r(1, 2 * p + 1)

            @block.scalar
            def _(act):
                with act.Fori(0, NB // 2) as p:
                    for k in range(2):
                        act.wait_ge(qs_done, 2 * p + k + 1)
                        nc.scalar.activation(qs[:, k, :].rearrange("j (a c) -> j a c", a=2), psQ[:, :, 0:HH], ACT.Copy).then_inc(qs_ready, 1)
                        act.wait_ge(es_done, 2 * p + k + 1)
                        nc.scalar.activation(es[:, k, :], psE[:, k, :], ACT.Copy).then_inc(es_ready, 1)

            @block.vector
            def _(dve):
                dve.wait_ge(e_turned, 1)
                nc.vector.tensor_copy(e_t[:, :, :].rearrange("j h i -> j (h i)"), psQ[:, 0, :]).then_inc(e_ready, 1)
                dve.wait_ge(mask_ready, 1)

                def add(k, n):
                    dve.wait_ge(r_done, n + 1)
                    nc.vector.tensor_tensor(H[:, bass.ds(n, 1), :], H[:, bass.ds(n, 1), :], psR[:, k:k + 1, 0:DM], ALU.add).then_inc(r_added, 1)

                with dve.Fori(0, NB // 2) as p:
                    for k in range(2):
                        dve.wait_ge(om_done, 2 * p + k + 1)
                        for half in range(2):
                            ins = nc.vector.tensor_tensor(om[:, k, 4 * half:4 * half + 4, :], psO[:, half, 0:HH].rearrange("u (h t) -> u h t", h=4),
                                                          bc(causal[:, :].unsqueeze(1), NT, 4, NT), ALU.mult)
                        ins.then_inc(om_ready, 1)
                    for k in range(2):
                        add(k, 2 * p + k)
                dve.wait_ge(r_added, NB)


def top_two_experts(nc, H, XT, router_w1, router_b1, router_w2, router_b2, w1, b1, w2, b2, w3, b3):
    NE, RH, NP = 6, 32, 3
    G = 4
    N = G * NT
    NG = NB // G
    with ExitStack() as ctx:
        sb = lambda n, sh: ctx.enter_context(nc.sbuf_tensor("ff_" + n, sh, F32))
        pb = lambda n, sh: ctx.enter_context(nc.psum_tensor("ff_" + n, sh, F32))
        sem = lambda n: ctx.enter_context(nc.semaphore("ff_" + n))
        rw1, rb1, rw2, rb2 = sb("rw1", [DM, RH]), sb("rb1", [RH, 1]), sb("rw2", [RH, NE]), sb("rb2", [NT, NE])
        w1s = sb("w1s", [DM, NE, DM])
        w2s = sb("w2s", [128, NP, 128])
        w3s = sb("w3s", [128, NP, 128])
        b1s, b2s = sb("b1s", [128, NP]), sb("b2s", [128, NP])
        b3s = sb("b3s", [NT, NE * DM])
        prio = sb("prio", [NT, NE])
        rh = sb("rh", [RH, 2, N])
        pr = sb("pr", [NT, NB, NE])
        first = sb("first", [NT, NB, NE])
        second = sb("second", [NT, NB, NE])
        score = sb("score", [NT, NB, NE])
        mx = sb("mx", [NT, 4, NB])
        mix = sb("mix", [NT, NB, NE])
        h1 = sb("h1", [128, NP, N])
        h2 = sb("h2", [128, 2, NP, N])
        eo = sb("eo", [NT, 2, NE * DM])
        ew = sb("ew", [NT, 2, NE * DM])
        es = sb("es", [NT, 2, DM])
        psA = pb("psA", [128, 3, 512])
        psB = pb("psB", [128, 3, 512])
        psC = pb("psC", [NT, 2, 512])
        loaded, blocks_zero, prio_ready = sem("loaded"), sem("blocks_zero"), sem("prio_ready")
        diag_loaded = sem("diag_loaded")
        rh_done, rh_ready, lg_done, lg_ready = sem("rh_done"), sem("rh_ready"), sem("lg_done"), sem("lg_ready")
        centred, exp_ready, gap_ready, ratio_ready = sem("centred"), sem("exp_ready"), sem("gap_ready"), sem("ratio_ready")
        step = sem("step")
        h1_done, h1_ready, h2_done, h2_ready = sem("h1_done"), sem("h1_ready"), sem("h2_done"), sem("h2_ready")
        eo_done, eo_read, added, vstep = sem("eo_done"), sem("eo_read"), sem("added"), sem("vstep")
        staged = sem("staged")
        xs = sb("xs", [DM, N])
        lg = psC[:, 0, 0:NB * NE].rearrange("t (b e) -> t b e", e=NE)
        with nc.Block() as block:
            @block.sync
            def _(sp):
                with nc.allow_non_contiguous_dma(reason="small weights"):
                    sp.dma_start(rw1[:, :], router_w1).then_inc(loaded, 16)
                    sp.dma_start(rb1[:, :], router_b1.rearrange("(k a) -> k a", a=1)).then_inc(loaded, 16)
                    sp.dma_start(rw2[:, :], router_w2).then_inc(loaded, 16)
                    sp.dma_start(rb2[:, :], router_b2.rearrange("(a k) -> a k", a=1).broadcast_to([NT, NE])).then_inc(loaded, 16)
                    sp.dma_start(w1s[:, :, :], w1.rearrange("e d h -> d e h")).then_inc(loaded, 16)
                    sp.dma_start(b1s[:, :], b1.rearrange("(p e) h -> (e h) p", e=2)).then_inc(loaded, 16)
                    sp.dma_start(b2s[:, :], b2.rearrange("(p e) h -> (e h) p", e=2)).then_inc(loaded, 16)
                    sp.dma_start(b3s[:, :], b3.rearrange("(a e) d -> a (e d)", a=1).broadcast_to([NT, NE * DM])).then_inc(loaded, 16)
                    sp.wait_ge(blocks_zero, 2)
                    for dst, src in ((w2s, w2), (w3s, w3)):
                        for e in range(2):
                            sp.dma_start(dst[e * DM:(e + 1) * DM, :, e * DM:(e + 1) * DM],
                                         src.rearrange("(p e) h f -> e h p f", e=2)[e]).then_inc(diag_loaded, 16)

            @block.gpsimd
            def _(pool):
                nc.gpsimd.memset(w2s[:, :, :], 0.0).then_inc(blocks_zero, 1)
                nc.gpsimd.memset(w3s[:, :, :], 0.0).then_inc(blocks_zero, 1)
                for e in range(NE):
                    ins = nc.gpsimd.memset(prio[:, e:e + 1], float(NE - e))
                ins.then_inc(prio_ready, 1)
                nc.gpsimd.tensor_copy(xs[:, :], XT[:, 0:N]).then_inc(staged, 1)
                with pool.Fori(1, NG) as g:
                    pool.wait_ge(h1_done, NP * g)
                    nc.gpsimd.tensor_copy(xs[:, :], XT[:, bass.ds(g * N, N)]).then_inc(staged, 1)

            @block.tensor
            def _(pe):
                pe.wait_ge(loaded, 8 * 16)
                for g in range(NG):
                    if g >= 2:
                        pe.wait_ge(rh_ready, g - 1)
                    nc.tensor.matmul(psA[0:RH, g % 2, 0:N], rw1[:, :], XT[:, g * N:(g + 1) * N], start=True, stop=True).then_inc(rh_done, 1)
                    pe.wait_ge(rh_ready, g + 1)
                    for j in range(G):
                        b = g * G + j
                        mm = nc.tensor.matmul(psC[:, 0, b * NE:(b + 1) * NE], rh[:, g % 2, j * NT:(j + 1) * NT], rw2[:, :], start=True, stop=True)
                    mm.then_inc(lg_done, 1)
                pe.wait_ge(diag_loaded, 4 * 16)
                pe.wait_ge(lg_ready, 1)

                with pe.Fori(0, NG) as g:
                    pe.wait_ge(staged, g + 1)
                    for p in range(NP):
                        nc.tensor.matmul(psA[:, p, 0:N], w1s[:, 2 * p:2 * p + 2, :].rearrange("d e h -> d (e h)"), xs[:, :],
                                         start=True, stop=True).then_inc(h1_done, 1)
                    for p in range(NP):
                        pe.wait_ge(h1_ready, NP * g + p + 1)
                        nc.tensor.matmul(psB[:, p, 0:N], w2s[:, p, :], h1[:, p, :], start=True, stop=True).then_inc(h2_done, 1)
                    pe.wait_ge(h2_ready, NP * g + NP)
                    for j in range(G):
                        pe.wait_ge(eo_read, G * g + j + 1)
                        for p in range(NP):
                            mm = nc.tensor.matmul(psC[:, j % 2, p * 128:(p + 1) * 128], h2[:, 0, p, j * NT:(j + 1) * NT], w3s[:, p, :], start=True, stop=True)
                        mm.then_inc(eo_done, 1)

            @block.scalar
            def _(act):
                act.wait_ge(loaded, 8 * 16)
                for g in range(NG):
                    act.wait_ge(rh_done, g + 1)
                    if g >= 2:
                        act.wait_ge(lg_done, g - 1)
                    nc.scalar.activation(rh[:, g % 2, :], psA[0:RH, g % 2, 0:N], ACT.Relu, bias=rb1[:, 0:1]).then_inc(rh_ready, 1)
                act.wait_ge(centred, 1)
                nc.scalar.activation(pr[:, :, :], pr[:, :, :], ACT.Exp).then_inc(exp_ready, 1)
                act.wait_ge(gap_ready, 1)
                nc.scalar.activation(mx[:, 1, :], mx[:, 1, :], ACT.Exp).then_inc(ratio_ready, 1)
                with act.Fori(0, NG) as g:
                    for p in range(NP):
                        act.wait_ge(h1_done, NP * g + p + 1)
                        nc.scalar.activation(h1[:, p, :], psA[:, p, 0:N], ACT.Relu, bias=b1s[:, p:p + 1]).then_inc(h1_ready, 1)
                    for p in range(NP):
                        act.wait_ge(h2_done, NP * g + p + 1)
                        ins = nc.scalar.activation(h2[:, 0, p, :], psB[:, p, 0:N], ACT.Relu, bias=b2s[:, p:p + 1])
                        ins.then_inc(h2_ready, 1)

            @block.vector
            def _(dve):
                s = Steps(dve, step)
                V = nc.vector
                wide = lambda m: bc(m.unsqueeze(2), NT, NB, NE)
                across = lambda m: bc(m.unsqueeze(1), NT, NB, NE)
                dve.wait_ge(lg_done, NG)
                dve.wait_ge(loaded, 8 * 16)
                V.tensor_tensor(pr[:, :, :], lg, across(rb2[:, :]), ALU.add).then_inc(lg_ready, 1)
                dve.wait_ge(lg_ready, 1)
                s.link(V.reduce_max(mx[:, 0, :], pr[:, :, :], AX.X))
                V.tensor_tensor(pr[:, :, :], pr[:, :, :], wide(mx[:, 0, :]), ALU.subtract).then_inc(centred, 1)
                dve.wait_ge(exp_ready, 1)
                s.link(V.reduce_sum(mx[:, 0, :], pr[:, :, :], AX.X))
                s.link(V.reciprocal(mx[:, 1, :], mx[:, 0, :]))
                s.link(V.tensor_tensor(pr[:, :, :], pr[:, :, :], wide(mx[:, 1, :]), ALU.mult))
                dve.wait_ge(prio_ready, 1)

                def pick(chosen, best, probs):
                    s.link(V.reduce_max(best, probs, AX.X))
                    s.link(V.tensor_tensor(score[:, :, :], probs, wide(best), ALU.is_equal))
                    s.link(V.tensor_tensor(score[:, :, :], score[:, :, :], across(prio[:, :]), ALU.mult))
                    s.link(V.reduce_max(mx[:, 3, :], score[:, :, :], AX.X))
                    s.link(V.tensor_tensor(chosen, score[:, :, :], wide(mx[:, 3, :]), ALU.is_equal))

                pick(first[:, :, :], mx[:, 0, :], pr[:, :, :])
                s.link(V.scalar_tensor_tensor(pr[:, :, :], first[:, :, :], -2.0, pr[:, :, :], ALU.mult, ALU.add))
                pick(second[:, :, :], mx[:, 1, :], pr[:, :, :])
                V.tensor_tensor(mx[:, 1, :], mx[:, 1, :], mx[:, 0, :], ALU.subtract).then_inc(gap_ready, 1)
                dve.wait_ge(ratio_ready, 1)
                s.link(V.tensor_scalar(mx[:, 0, :], mx[:, 1, :], 1.0, None, ALU.add))
                s.link(V.reciprocal(mx[:, 2, :], mx[:, 0, :]))
                s.link(V.tensor_tensor(mx[:, 3, :], mx[:, 2, :], mx[:, 1, :], ALU.mult))
                s.link(V.tensor_tensor(first[:, :, :], first[:, :, :], wide(mx[:, 2, :]), ALU.mult))
                s.link(V.tensor_tensor(second[:, :, :], second[:, :, :], wide(mx[:, 3, :]), ALU.mult))
                s.link(V.tensor_tensor(mix[:, :, :], first[:, :, :], second[:, :, :], ALU.add))
                V.sem_inc(eo_read, 2)
                with dve.Fori(0, NG) as g:
                    t = Steps(dve, vstep, g * (3 * G))
                    for j in range(G):
                        b, k = g * G + j, j % 2
                        dve.wait_ge(eo_done, G * g + j + 1)
                        V.tensor_tensor(eo[:, k, :], psC[:, k, 0:NE * DM], b3s[:, :], ALU.add).then_inc(eo_read, 1)
                        dve.wait_ge(eo_read, G * g + j + 3)
                        t.link(V.tensor_tensor(ew[:, k, :].rearrange("t (e d) -> t e d", e=NE), eo[:, k, :].rearrange("t (e d) -> t e d", e=NE),
                                               bc(mix[:, bass.ds(b, 1), :].rearrange("t a e -> t (a e)").unsqueeze(2), NT, NE, DM), ALU.mult))
                        t.link(V.reduce_sum(es[:, k, :], ew[:, k, :].rearrange("t (e d) -> t d e", e=NE), AX.X))
                        t.link(V.tensor_tensor(H[:, bass.ds(b, 1), :], H[:, bass.ds(b, 1), :], es[:, k:k + 1, :], ALU.add))


def best_expert(nc, H, XT, ident, gate_w, gate_b, w1, b1, w2, b2):
    NE, F = 8, 256
    CAP = -(-5 * TOK // (4 * NE))
    KT = F // 128
    G = 4
    N = G * NT
    NG = NB // G
    with ExitStack() as ctx:
        sb = lambda n, sh: ctx.enter_context(nc.sbuf_tensor("sw_" + n, sh, F32))
        pb = lambda n, sh: ctx.enter_context(nc.psum_tensor("sw_" + n, sh, F32))
        sem = lambda n: ctx.enter_context(nc.semaphore("sw_" + n))
        gw, gb = sb("gw", [DM, NE]), sb("gb", [NT, NE])
        w1s = sb("w1s", [DM, NE, F])
        b1s = sb("b1s", [128, NE, KT])
        w2s = sb("w2s", [128, NE, KT, DM])
        b2s = sb("b2s", [NT, NE * DM])
        prio = sb("prio", [NT, NE])
        pr, score, chosen = sb("pr", [NT, NB, NE]), sb("score", [NT, NB, NE]), sb("chosen", [NT, NB, NE])
        mx = sb("mx", [NT, 4, NB])
        chT = sb("chT", [NE, TOK])
        ones = sb("ones", [NE, TOK])
        count = sb("count", [NE, TOK])
        gate = sb("gate", [NT, NB, NE])
        hid = sb("hid", [128, NE, KT, N])
        eo = sb("eo", [NT, 2, NE * DM])
        ew = sb("ew", [NT, 2, NE * DM])
        es = sb("es", [NT, 2, DM])
        fix = sb("fix", [NT, NB, DM])
        flag = ctx.enter_context(nc.sbuf_tensor("sw_flag", [NT, NB, DM], mybir.dt.uint32))
        const = sb("const", [NT, 3])
        staged = sem("staged")
        xs = sb("xs", [DM, N])
        psA = pb("psA", [128, 4, 512])
        psC = pb("psC", [NT, 2, 512])
        loaded, prio_ready, lg_done, lg_ready = sem("loaded"), sem("prio_ready"), sem("lg_done"), sem("lg_ready")
        centred, exp_ready, step = sem("centred"), sem("exp_ready"), sem("step")
        ch_ready, turned, taken, counted, back, gate_ready = sem("ch_ready"), sem("turned"), sem("taken"), sem("counted"), sem("back"), sem("gate_ready")
        hid_done, hid_a, hid_v = sem("hid_done"), sem("hid_a"), sem("hid_v")
        eo_done, eo_read, vstep = sem("eo_done"), sem("eo_read"), sem("vstep")
        lg = psC[:, 0, 0:NB * NE].rearrange("t (b e) -> t b e", e=NE)
        back_ps = psC[:, 1, 0:NB * NE].rearrange("t (b e) -> t b e", e=NE)
        with nc.Block() as block:
            @block.sync
            def _(sp):
                with nc.allow_non_contiguous_dma(reason="small weights"):
                    sp.dma_start(gw[:, :], gate_w).then_inc(loaded, 16)
                    sp.dma_start(gb[:, :], gate_b.rearrange("(a k) -> a k", a=1).broadcast_to([NT, NE])).then_inc(loaded, 16)
                    sp.dma_start(w1s[:, :, :], w1.rearrange("e d f -> d e f")).then_inc(loaded, 16)
                    sp.dma_start(b1s[:, :, :], b1.rearrange("e (k p) -> p e k", p=128)).then_inc(loaded, 16)
                    for k in range(KT):
                        sp.dma_start(w2s[:, :, k, :], w2[:, k * 128:(k + 1) * 128, :].rearrange("e p d -> p e d")).then_inc(loaded, 16)
                    sp.dma_start(b2s[:, :], b2.rearrange("(a e) d -> a (e d)", a=1).broadcast_to([NT, NE * DM])).then_inc(loaded, 16)
            LOADED = 7 * 16

            @block.gpsimd
            def _(pool):
                for e in range(NE):
                    nc.gpsimd.memset(prio[:, e:e + 1], float(NE - e))
                nc.gpsimd.memset(const[:, 0:1], 0.0)
                nc.gpsimd.memset(const[:, 1:2], 10000.0)
                nc.gpsimd.memset(const[:, 2:3], -10000.0)
                nc.gpsimd.memset(ones[:, :], 1.0).then_inc(prio_ready, 1)
                nc.gpsimd.tensor_copy(xs[:, :], XT[:, 0:N]).then_inc(staged, 1)
                with pool.Fori(1, NG) as g:
                    pool.wait_ge(hid_done, NE * KT * g)
                    nc.gpsimd.tensor_copy(xs[:, :], XT[:, bass.ds(g * N, N)]).then_inc(staged, 1)

            @block.tensor
            def _(pe):
                pe.wait_ge(loaded, LOADED)
                for b in range(NB):
                    mm = nc.tensor.matmul(lg[:, b, :], XT[:, b * NT:(b + 1) * NT], gw[:, :], start=True, stop=True)
                mm.then_inc(lg_done, 1)
                pe.wait_ge(ch_ready, 1)
                for g in range(NG):
                    if g >= 4:
                        pe.wait_ge(taken, g - 3)
                    for j in range(G):
                        mm = nc.tensor.transpose(psA[0:NE, g % 4, j * NT:(j + 1) * NT], chosen[:, g * G + j, :], ident[0:NT, 0:NT])
                    mm.then_inc(turned, 1)
                pe.wait_ge(counted, 1)
                for b in range(NB):
                    mm = nc.tensor.transpose(back_ps[:, b, :], chT[:, b * NT:(b + 1) * NT], ident[0:NE, 0:NE])
                mm.then_inc(back, 1)
                pe.wait_ge(gate_ready, 1)
                pe.sem_inc(eo_done, 1)

                with pe.Fori(0, NG) as g:
                    pe.wait_ge(staged, g + 1)
                    for e in range(NE):
                        for k in range(KT):
                            n = e * KT + k
                            if n >= 4:
                                pe.wait_ge(hid_a if n % 2 == 0 else hid_v, (NE * KT // 2) * g + (n - 4) // 2 + 1)
                            nc.tensor.matmul(psA[:, n % 4, 0:N], w1s[:, e, k * 128:(k + 1) * 128], xs[:, :],
                                             start=True, stop=True).then_inc(hid_done, 1)
                    pe.wait_ge(hid_a, (NE * KT // 2) * (g + 1))
                    pe.wait_ge(hid_v, (NE * KT // 2) * (g + 1))
                    for j in range(G):
                        pe.wait_ge(eo_read, G * g + j + 1)
                        for e in range(NE):
                            for k in range(KT):
                                mm = nc.tensor.matmul(psC[:, j % 2, e * DM:(e + 1) * DM], hid[:, e, k, j * NT:(j + 1) * NT], w2s[:, e, k, :],
                                                      start=k == 0, stop=k == KT - 1)
                        mm.then_inc(eo_done, 1)

            @block.scalar
            def _(act):
                act.wait_ge(loaded, LOADED)
                act.wait_ge(centred, 1)
                nc.scalar.activation(pr[:, :, :], pr[:, :, :], ACT.Exp).then_inc(exp_ready, 1)
                with act.Fori(0, NG) as g:
                    for n in range(0, NE * KT, 2):
                        if n == 0:
                            act.wait_ge(eo_done, G * g + 1)
                        act.wait_ge(hid_done, NE * KT * g + n + 1)
                        nc.scalar.activation(hid[:, n // KT, n % KT, :], psA[:, n % 4, 0:N], ACT.Relu, bias=b1s[:, n // KT, n % KT:n % KT + 1]).then_inc(hid_a, 1)

            @block.vector
            def _(dve):
                s = Steps(dve, step)
                V = nc.vector
                wide = lambda m: bc(m.unsqueeze(2), NT, NB, NE)
                across = lambda m: bc(m.unsqueeze(1), NT, NB, NE)
                dve.wait_ge(lg_done, 1)
                dve.wait_ge(loaded, LOADED)
                dve.wait_ge(prio_ready, 1)
                V.tensor_tensor(pr[:, :, :], lg, across(gb[:, :]), ALU.add).then_inc(lg_ready, 1)
                dve.wait_ge(lg_ready, 1)
                s.link(V.reduce_max(mx[:, 0, :], pr[:, :, :], AX.X))
                V.tensor_tensor(pr[:, :, :], pr[:, :, :], wide(mx[:, 0, :]), ALU.subtract).then_inc(centred, 1)
                dve.wait_ge(exp_ready, 1)
                s.link(V.reduce_sum(mx[:, 0, :], pr[:, :, :], AX.X))
                s.link(V.reciprocal(mx[:, 1, :], mx[:, 0, :]))
                s.link(V.tensor_tensor(pr[:, :, :], pr[:, :, :], wide(mx[:, 1, :]), ALU.mult))
                s.link(V.reduce_max(mx[:, 2, :], pr[:, :, :], AX.X))
                s.link(V.tensor_tensor(score[:, :, :], pr[:, :, :], wide(mx[:, 2, :]), ALU.is_equal))
                s.link(V.tensor_tensor(score[:, :, :], score[:, :, :], across(prio[:, :]), ALU.mult))
                s.link(V.reduce_max(mx[:, 3, :], score[:, :, :], AX.X))
                V.tensor_tensor(chosen[:, :, :], score[:, :, :], wide(mx[:, 3, :]), ALU.is_equal).then_inc(ch_ready, 1)
                for g in range(NG):
                    dve.wait_ge(turned, g + 1)
                    V.tensor_copy(chT[:, g * N:(g + 1) * N], psA[0:NE, g % 4, 0:N]).then_inc(taken, 1)
                dve.wait_ge(taken, NG)
                s.link(V.tensor_tensor_scan(count[:, :], ones[:, :], chT[:, :], 0.0, ALU.mult, ALU.add))
                s.link(V.tensor_scalar(count[:, :], count[:, :], float(CAP), None, ALU.is_le))
                V.tensor_tensor(chT[:, :], chT[:, :], count[:, :], ALU.mult).then_inc(counted, 1)
                dve.wait_ge(back, 1)
                V.tensor_tensor(gate[:, :, :], back_ps, wide(mx[:, 2, :]), ALU.mult).then_inc(gate_ready, 1)
                dve.wait_ge(gate_ready, 1)
                V.sem_inc(eo_read, 2)
                with dve.Fori(0, NG) as g:
                    t = Steps(dve, vstep, g * (2 * G))
                    for n in range(1, NE * KT, 2):
                        if n == 1:
                            dve.wait_ge(eo_done, G * g + 1)
                        dve.wait_ge(hid_done, NE * KT * g + n + 1)
                        V.tensor_scalar(hid[:, n // KT, n % KT, :], psA[:, n % 4, 0:N], b1s[:, n // KT, n % KT:n % KT + 1], 0.0, ALU.add, ALU.max).then_inc(hid_v, 1)
                    for j in range(G):
                        b, k = g * G + j, j % 2
                        dve.wait_ge(eo_done, G * g + j + 2)
                        V.tensor_tensor(eo[:, k, :], psC[:, k, :], b2s[:, :], ALU.add).then_inc(eo_read, 1)
                        dve.wait_ge(eo_read, G * g + j + 3)
                        t.link(V.tensor_tensor(ew[:, k, :].rearrange("t (e d) -> t e d", e=NE), eo[:, k, :].rearrange("t (e d) -> t e d", e=NE),
                                               bc(gate[:, bass.ds(b, 1), :].rearrange("t a e -> t (a e)").unsqueeze(2), NT, NE, DM), ALU.mult))
                        t.link(V.reduce_sum(fix[:, bass.ds(b, 1), :].rearrange("t a d -> t (a d)"), ew[:, k, :].rearrange("t (e d) -> t d e", e=NE), AX.X))
                BIG = 3.4028234663852886e38
                whole = lambda i: bc(const[:, i:i + 1].unsqueeze(2), NT, NB, DM)
                s.link(V.tensor_tensor(flag[:, :, :], fix[:, :, :], fix[:, :, :], ALU.not_equal))
                s.link(V.copy_predicated(fix[:, :, :], flag[:, :, :], whole(0)))
                s.link(V.tensor_scalar(flag[:, :, :], fix[:, :, :], BIG, None, ALU.is_gt))
                s.link(V.copy_predicated(fix[:, :, :], flag[:, :, :], whole(1)))
                s.link(V.tensor_scalar(flag[:, :, :], fix[:, :, :], -BIG, None, ALU.is_lt))
                s.link(V.copy_predicated(fix[:, :, :], flag[:, :, :], whole(2)))
                s.link(V.tensor_tensor(H[:, :, :], H[:, :, :], fix[:, :, :], ALU.add))


FH = 256
NC = 16
HB = NB // 2


def memory_tensors(nc, ctx):
    sb = lambda n, sh: ctx.enter_context(nc.sbuf_tensor("mem_" + n, sh, F32))
    dr = lambda n, sh: nc.dram_tensor("mem_" + n + "_dram", sh, F32).ap()
    return dict(
        a0=sb("a0", [DM, FH]),
        b0=sb("b0", [128, 2, 2, 128]),
        b0t=sb("b0t", [128, 2, FH]),
        z_base=sb("z_base", [128, 2, NB, NT]),
        g_t=sb("g_t", [NT, NB, NT]),
        c_f=sb("c_f", [128, NB, NT]),
        c_y=sb("c_y", [128, HB, NT]),
        v_y=sb("v_y", [128, HB, NT]),
        w_rows=dr("w_rows", [NT, NB, NT]),
        g_rows=dr("g_rows", [NT, NB, NC]),
        w_t=dr("w_t", [NT, TOK]),
        k_t=dr("k_t", [DM, TOK]), q_t=dr("q_t", [DM, TOK]), qc_t=dr("qc_t", [DM, TOK]),
        c_now=dr("c_now", [128, TOK]),
    )


def memory_setup(nc, M, XT, ident, inject, W_fused, W0, W1, P0, P1):
    NQ = 3 * DM
    G = 4
    N = G * NT
    NG = NB // G
    with ExitStack() as ctx:
        sb = lambda n, sh: ctx.enter_context(nc.sbuf_tensor("ms_" + n, sh, F32))
        pb = lambda n, sh: ctx.enter_context(nc.psum_tensor("ms_" + n, sh, F32))
        sem = lambda n: ctx.enter_context(nc.semaphore("ms_" + n))
        wf = sb("wf", [128, 2, DM])
        wft = sb("wft", [DM, 2, 128])
        gcol = sb("gcol", [DM, 3, 128])
        p0, w1, p1 = sb("p0", [DM, FH]), sb("w1", [128, 2, DM]), sb("p1", [128, 2, DM])
        fp = sb("fp", [NT, NB, NQ])
        sg = sb("sg", [NT, 2, 2, NQ])
        nrm = sb("nrm", [NT, 4, 2 * NB])
        keep, eta, theta, work = sb("keep", [128, NB, NT]), sb("eta", [128, NB, NT]), sb("theta", [128, NB, NT]), sb("work", [128, NB, NT])
        diag = sb("diag", [NT, NT])
        vv = sb("vv", [NT, HB, 128])
        kT, qT = sb("kT", [DM, TOK]), sb("qT", [DM, TOK])
        psG, psF, psT = pb("psG", [128, 2, 512]), pb("psF", [NT, 2, 512]), pb("psT", [128, 4, 512])
        flat = lambda t: t[:, :, :].rearrange("p b t -> p (b t)")
        loaded, turned, taken, wft_ready = sem("loaded"), sem("turned"), sem("taken"), sem("wft_ready")
        k_stored = sem("k_stored")
        step, zeroed, b0_ready = sem("step"), sem("zeroed"), sem("b0_ready")
        gate_done, gate_ready = sem("gate_done"), sem("gate_ready")
        fp_done, sig_ready, fp_ready = sem("fp_done"), sem("sig_ready"), sem("fp_ready")
        sq_ready, root_ready, kq_ready = sem("sq_ready"), sem("root_ready"), sem("kq_ready")
        w_ready, base_ready, z_done, z_ready = sem("w_ready"), sem("base_ready"), sem("z_done"), sem("z_ready")
        gram_done, gram_read, stored = sem("gram_done"), sem("gram_read"), sem("stored")
        kt_ready, wt_ready, qc_ready, rows_ready, g_ready, c_ready = sem("kt_ready"), sem("wt_ready"), sem("qc_ready"), sem("rows_ready"), sem("g_ready"), sem("c_ready")
        with nc.Block() as block:
            @block.sync
            def _(sp):
                sp.dma_start(diag[:, :], inject).then_inc(loaded, 16)
                sp.dma_start(wf[:, 0, :], W_fused[0:128, :]).then_inc(loaded, 16)
                sp.dma_start(wf[0:NQ + 3 - 128, 1, :], W_fused[128:NQ + 3, :]).then_inc(loaded, 16)
                sp.dma_start(M["a0"][:, :], W0).then_inc(loaded, 16)
                sp.dma_start(p0[:, :], P0).then_inc(loaded, 16)
                sp.dma_start(w1[:, :, :], W1.rearrange("(k p) d -> p k d", p=128)).then_inc(loaded, 16)
                sp.dma_start(p1[:, :, :], P1.rearrange("(k p) d -> p k d", p=128)).then_inc(loaded, 16)
                sp.wait_ge(wt_ready, 1)
                sp.dma_start(M["w_t"], flat(work)[0:NT]).then_inc(stored, 16)
                sp.wait_ge(kt_ready, 1)
                sp.dma_start(M["k_t"], kT[:, :]).then_inc(k_stored, 16)
                sp.dma_start(M["q_t"], qT[:, :]).then_inc(stored, 16)
                sp.wait_ge(rows_ready, 1)
                sp.dma_start(M["w_rows"], eta[0:NT, :, :]).then_inc(stored, 16)
                sp.wait_ge(c_ready, 1)
                sp.dma_start(M["c_now"], flat(keep)).then_inc(stored, 16)
                sp.wait_ge(qc_ready, 1)
                sp.dma_start(M["qc_t"], fp[0:DM, 0:16, :].rearrange("p a c -> p (a c)")).then_inc(stored, 16)
                sp.wait_ge(g_ready, 1)
                for c in range(NT // NC):
                    o = slice(c * NC, (c + 1) * NC)
                    sp.dma_start(M["g_rows"][o, :, :], theta[o, :, o]).then_inc(stored, 16)
                sp.wait_ge(stored, 16 * (5 + NT // NC))
                sp.wait_ge(k_stored, 16)

            @block.gpsimd
            def _(pool):
                nc.gpsimd.memset(M["b0"][:, :, :, :], 0.0).then_inc(zeroed, 1)

            @block.tensor
            def _(pe):
                T, MM = nc.tensor.transpose, nc.tensor.matmul
                pe.wait_ge(loaded, 7 * 16)
                T(psT[0:DM, 0, 0:128], wf[:, 0, :], ident[:, :])
                T(psT[0:DM, 0, 128:128 + NQ + 3 - 128], wf[0:NQ + 3 - 128, 1, :], ident[0:NQ + 3 - 128, 0:NQ + 3 - 128]).then_inc(turned, 1)
                pe.wait_ge(b0_ready, 1)
                for b2 in range(2):
                    for k in range(2):
                        mm = T(psT[:, 1, (2 * b2 + k) * 128:(2 * b2 + k + 1) * 128], M["b0"][:, k, b2, :], ident[:, :])
                mm.then_inc(turned, 1)
                pe.wait_ge(wft_ready, 1)
                for j in range(3 * 6):
                    if j >= 2:
                        pe.wait_ge(gate_ready, j - 1)
                    MM(psG[:, j % 2, :], gcol[:, j // 6, :], XT[:, j % 6 * 512:(j % 6 + 1) * 512], start=True, stop=True).then_inc(gate_done, 1)
                for j in range(NB // 2):
                    if j >= 2:
                        pe.wait_ge(fp_ready, j - 1)
                    for i in range(2):
                        b = 2 * j + i
                        mm = MM(psF[:, j % 2, i * NQ:(i + 1) * NQ], XT[:, b * NT:(b + 1) * NT], wft[:, :, :].rearrange("d a c -> d (a c)")[:, 0:NQ], start=True, stop=True)
                    mm.then_inc(fp_done, 1)
                pe.wait_ge(kq_ready, 1)
                n = 2
                for what in range(4):
                    if what == 3:
                        pe.wait_ge(w_ready, 1)
                    for g in range(NG if what != 2 else NG // 2):
                        pe.wait_ge(taken, n - 5) if n >= 6 else None
                        for j in range(G):
                            b = g * G + j
                            if what < 2:
                                mm = T(psT[0:DM, n % 4, j * NT:(j + 1) * NT], fp[:, b, (1 - what) * DM:(2 - what) * DM], ident[0:NT, 0:NT])
                            elif what == 2:
                                mm = T(psT[:, n % 4, j * NT:(j + 1) * NT], vv[:, b, :], ident[0:NT, 0:NT])
                            else:
                                mm = T(psT[0:NT, n % 4, j * NT:(j + 1) * NT], theta[0:NT, b, :], ident[0:NT, 0:NT])
                        mm.then_inc(turned, 1)
                        n += 1
                pe.wait_ge(taken, n - 2)
                for g in range(NG):
                    if g >= 4:
                        pe.wait_ge(gram_read, g - 3)
                    for j in range(G):
                        b = g * G + j
                        mm = MM(psT[0:NT, g % 4, j * NT:(j + 1) * NT], kT[:, b * NT:(b + 1) * NT], kT[:, b * NT:(b + 1) * NT], start=True, stop=True)
                    mm.then_inc(gram_done, 1)
                pe.wait_ge(base_ready, 1)
                for j in range(12):
                    if j >= 2:
                        pe.wait_ge(z_ready, j - 1)
                    MM(psG[:, j % 2, :], M["a0"][:, j // 6 * 128:(j // 6 + 1) * 128], kT[:, j % 6 * 512:(j % 6 + 1) * 512], start=True, stop=True).then_inc(z_done, 1)

            @block.scalar
            def _(act):
                A = nc.scalar.activation
                for j in range(3 * 6):
                    act.wait_ge(gate_done, j + 1)
                    A(flat((keep, theta, eta)[j // 6])[:, j % 6 * 512:(j % 6 + 1) * 512], psG[:, j % 2, :], ACT.Sigmoid,
                      scale=(-1.0 if j < 6 else 1.0)).then_inc(gate_ready, 1)
                for j in range(NB // 2):
                    act.wait_ge(fp_done, j + 1)
                    if j >= 2:
                        act.wait_ge(fp_ready, j - 1)
                    A(sg[:, j % 2, :, :].rearrange("t a c -> t (a c)"), psF[:, j % 2, 0:2 * NQ], ACT.Sigmoid).then_inc(sig_ready, 1)
                act.wait_ge(sq_ready, 1)
                A(nrm[:, 1, :], nrm[:, 0, :], ACT.Sqrt).then_inc(root_ready, 1)
                for j in range(12):
                    act.wait_ge(z_done, j + 1)
                    A(M["z_base"][:, j // 6, :, :].rearrange("p b t -> p (b t)")[:, j % 6 * 512:(j % 6 + 1) * 512], psG[:, j % 2, :], ACT.Copy).then_inc(z_ready, 1)
                act.wait_ge(z_ready, 12)

            @block.vector
            def _(dve):
                V = nc.vector
                s = Steps(dve, step)
                dve.wait_ge(loaded, 7 * 16)
                s.link(V.tensor_tensor(M["a0"][:, :], M["a0"][:, :], p0[:, :], ALU.add))
                dve.wait_ge(zeroed, 1)
                for b2 in range(2):
                    ins = V.tensor_tensor(M["b0"][:, :, b2, b2 * DM:(b2 + 1) * DM], w1[:, :, :], p1[:, :, :], ALU.add)
                ins.then_inc(b0_ready, 1)
                dve.wait_ge(turned, 1)
                s.link(V.tensor_copy(wft[:, :, :].rearrange("d a c -> d (a c)")[:, 0:NQ + 3], psT[0:DM, 0, 0:NQ + 3]))
                V.tensor_copy(gcol[:, :, :], bc(wft[:, 1, NQ - 128:NQ - 128 + 3].unsqueeze(2), DM, 3, 128)).then_inc(wft_ready, 1)
                dve.wait_ge(turned, 2)
                s.link(V.tensor_copy(M["b0t"][:, :, :].rearrange("p a f -> p (a f)"), psT[:, 1, :]))
                for j in range(NB // 2):
                    dve.wait_ge(sig_ready, j + 1)
                    V.tensor_tensor(fp[:, 2 * j:2 * j + 2, :], psF[:, j % 2, 0:2 * NQ].rearrange("t (a c) -> t a c", a=2), sg[:, j % 2, :, :], ALU.mult).then_inc(fp_ready, 1)
                dve.wait_ge(fp_ready, NB // 2)
                qk = fp[:, :, 0:2 * DM].rearrange("t b (a d) -> t b a d", a=2)
                dve.wait_ge(gate_ready, 18)
                for a in range(2):
                    sq = work[0:NT, :, 0:DM]
                    s.link(V.tensor_tensor(sq, qk[:, :, a, :], qk[:, :, a, :], ALU.mult))
                    ins = V.reduce_sum(nrm[:, 0, a * NB:(a + 1) * NB], sq, AX.X)
                    if a == 0:
                        s.link(ins)
                ins.then_inc(sq_ready, 1)
                dve.wait_ge(root_ready, 1)
                s.link(V.tensor_scalar(nrm[:, 1, :], nrm[:, 1, :], 1e-12, None, ALU.max))
                s.link(V.reciprocal(nrm[:, 2, :], nrm[:, 1, :]))
                s.link(V.tensor_tensor(nrm[:, 3, :], nrm[:, 2, :], nrm[:, 0, :], ALU.mult))
                s.link(V.tensor_tensor(nrm[:, 2, :], nrm[:, 3, :], nrm[:, 1, :], ALU.add))
                s.link(V.tensor_scalar(nrm[:, 3, :], nrm[:, 2, :], 0.5, 1e-12, ALU.mult, ALU.max))
                s.link(V.reciprocal(nrm[:, 1, :], nrm[:, 3, :]))
                for a in range(2):
                    V.tensor_copy(vv[:, :, a * DM:(a + 1) * DM], fp[:, a * HB:(a + 1) * HB, 2 * DM:3 * DM])
                for a in range(2):
                    ins = V.tensor_tensor(qk[:, :, a, :], qk[:, :, a, :], bc(nrm[:, 1, a * NB:(a + 1) * NB].unsqueeze(2), NT, NB, DM), ALU.mult)
                ins.then_inc(kq_ready, 1)
                s.link(V.memset(work[:, :, :], 0.0))
                s.link(V.tensor_copy(work[:, :, 0:1], keep[:, :, 0:1]))
                s.link(V.memset(keep[:, :, 0:1], 0.0))
                s.link(V.memset(eta[:, :, 0:1], 0.0))
                s.link(V.tensor_tensor_scan(flat(work), flat(keep), flat(work), 0.0, ALU.mult, ALU.add))
                s.link(V.memset(M["c_f"][:, :, 0:1], 1.0))
                s.link(V.tensor_copy(M["c_f"][:, :, 1:NT], work[:, :, 0:NT - 1]))
                for b2 in range(2):
                    V.tensor_copy(M["c_y"][b2 * DM:(b2 + 1) * DM, :, :], M["c_f"][b2 * DM:(b2 + 1) * DM, b2 * HB:(b2 + 1) * HB, :])
                s.link(V.tensor_tensor(theta[0:NT, :, :], theta[0:NT, :, :], bc(diag[:, :].unsqueeze(1), NT, NB, NT), ALU.mult))
                s.link(V.tensor_tensor_scan(flat(eta)[0:NT], flat(eta)[0:NT], flat(theta)[0:NT], 0.0, ALU.mult, ALU.add))
                s.link(V.tensor_tensor_scan(flat(eta)[0:NT], flat(keep)[0:NT], flat(eta)[0:NT], 0.0, ALU.mult, ALU.add))
                s.link(V.memset(theta[0:NT, :, 0:1], 0.0))
                V.tensor_copy(theta[0:NT, :, 1:NT], eta[0:NT, :, 0:NT - 1]).then_inc(w_ready, 1)
                V.tensor_copy(keep[:, :, :], work[:, :, :]).then_inc(c_ready, 1)
                dve.wait_ge(c_ready, 1)
                V.tensor_copy(work[0:NT, :, :], eta[0:NT, :, :]).then_inc(wt_ready, 1)
                dve.wait_ge(wt_ready, 1)
                n = 2
                for what in range(4):
                    for g in range(NG if what != 2 else NG // 2):
                        dve.wait_ge(turned, n + 1)
                        src = psT[:, n % 4, 0:N]
                        if what < 2:
                            ins = V.tensor_copy((kT, qT)[what][:, g * N:(g + 1) * N], src[0:DM])
                        elif what == 2:
                            ins = V.tensor_copy(M["v_y"][:, g * G:(g + 1) * G, :].rearrange("p b t -> p (b t)"), src)
                        else:
                            ins = V.tensor_copy(flat(eta)[0:NT, g * N:(g + 1) * N], src[0:NT])
                        ins.then_inc(taken, 1)
                        n += 1
                    if what == 1:
                        dve.wait_ge(taken, n - 2)
                        V.sem_inc(kt_ready, 1)
                dve.wait_ge(taken, n - 2)
                V.sem_inc(rows_ready, 1)
                qc = fp[0:DM, 0:16, :].rearrange("p a c -> p (a c)")
                V.tensor_tensor(qc, qT[:, :], flat(keep)[0:DM], ALU.mult).then_inc(qc_ready, 1)
                for g in range(NG):
                    dve.wait_ge(gram_done, g + 1)
                    src = psT[0:NT, g % 4, 0:N].rearrange("p (b t) -> p b t", t=NT)
                    o = slice(g * G, (g + 1) * G)
                    s.link(V.tensor_tensor(M["g_t"][:, o, :], src, theta[0:NT, o, :], ALU.mult))
                    s.link(V.tensor_tensor(theta[0:NT, o, :], src, eta[0:NT, o, :], ALU.mult))
                    V.sem_inc(gram_read, 1)
                V.sem_inc(g_ready, 1)
                dve.wait_ge(k_stored, 16)
                V.tensor_tensor(kT[:, :], kT[:, :], flat(M["c_f"])[0:DM], ALU.mult).then_inc(base_ready, 1)
                dve.wait_ge(base_ready, 1)


def memory_scan(nc, M, hist_h, hist_dz, hist_y, ident, cols_in, rows_in):
    NCH = NT // NC
    GB = HB // 2
    with ExitStack() as ctx:
        sb = lambda n, sh: ctx.enter_context(nc.sbuf_tensor("sc_" + n, sh, F32))
        pb = lambda n, sh: ctx.enter_context(nc.psum_tensor("sc_" + n, sh, F32))
        sem = lambda n: ctx.enter_context(nc.semaphore("sc_" + n))
        prod = sb("prod", [128, 2, 2, 2 * GB * NT])
        z_prod = sb("z_prod", [128, 2, NB, NC])
        y_prod = sb("y_prod", [128, 2, GB * NT])
        y_w = sb("y_w", [128, HB * NT])
        w_row = sb("w_row", [128, 2, HB * NT])
        g_row = sb("g_row", [128, 2, NB, NC])
        zsum, z, sg, slope, hs, hg = (sb(n, [128, 2, NB]) for n in ("zsum", "z", "sg", "slope", "hs", "hg"))
        first_part, dh = sb("first_part", [128, 2, NB]), sb("dh", [128, 2, NB])
        pred, off, ysum = (sb(n, [128, HB]) for n in ("pred", "off", "ysum"))
        dz_in, dz_t, g_in = sb("dz_in", [128, 2, 2, NT]), sb("dz_t", [NT, 2, FH]), sb("g_in", [NT, 2, NC])
        cols = sb("cols", [128, 2, 128])
        rows_ = sb("rows", [128, 2, 128])
        ones_in = sem("ones_in")
        wide = pb("wide", [128, 2, 3 * 512])
        small = pb("small", [128, 2, 512])
        ps_pred = lambda g: small[:, g, 0:GB]
        ps_back = lambda g: small[:, g, 64:64 + 4 * GB].rearrange("p (a b) -> p a b", a=4)
        flat_wide = wide[:, :, :].rearrange("p g c -> p (g c)")
        grp = lambda x, g: x[:, :, :].rearrange("p a (c b) -> p (a c) b", c=2)[:, :, GB * g:GB * (g + 1)]
        grp_at = lambda x, g, t: x[:, :, :, bass.ds(t, 1)].rearrange("p a (c b) s -> p (a c) (b s)", c=2)[:, :, GB * g:GB * (g + 1)]
        cols_at = lambda x, g, t: x[:, GB * g:GB * (g + 1), bass.ds(t, 1)].rearrange("p b s -> p (b s)")
        w_in, g_rows_in = [sem("w_in0"), sem("w_in1")], [sem("g_in0"), sem("g_in1")]
        zeroed, step = sem("zeroed"), sem("step")
        z_ready, sg_ready, h_ready, slope_ready = sem("z_ready"), sem("sg_ready"), sem("h_ready"), sem("slope_ready")
        p1_ready, hh_done, yw_ready, dy_ready, p2_ready, yy_done = (sem(n) for n in ("p1_ready", "hh_done", "yw_ready", "dy_ready", "p2_ready", "yy_done"))
        dz_ready, pool_step = sem("dz_ready"), sem("pool_step")
        staged, dz_turned, dzt_ready, base_done, base_added = (sem(n) for n in ("staged", "dz_turned", "dzt_ready", "base_done", "base_added"))
        K = 14
        with nc.Block() as block:
            @block.sync
            def _(sp):
                sp.dma_start(cols[:, :, :], cols_in).then_inc(ones_in, 16)
                sp.dma_start(rows_[:, :, :], rows_in).then_inc(ones_in, 16)
                for c in range(NCH):
                    L = (c + 1) * NC

                    def rows(k, t, turn):
                        if turn is not None:
                            sp.wait_ge(yw_ready, 2 * turn)
                            sp.wait_ge(z_ready, 2 * turn)
                        for b2 in range(2):
                            sp.dma_start(w_row[b2 * DM:(b2 + 1) * DM, k, 0:HB * L].rearrange("p (b s) -> p b s", s=L),
                                         M["w_rows"][bass.ds(t, 1), b2 * HB:(b2 + 1) * HB, 0:L].broadcast_to([DM, HB, L])).then_inc(w_in[k], 16)
                        sp.dma_start(g_row[:, k, :, :].rearrange("p b s -> p (b s)"),
                                     M["g_rows"][bass.ds(t, 1), :, :].rearrange("t b s -> t (b s)").broadcast_to([128, NB * NC])).then_inc(g_rows_in[k], 16)

                    if c == 0:
                        for k in range(2):
                            rows(k, k, None)
                        with sp.Fori(1, NC // 2) as i:
                            for k in range(2):
                                rows(k, 2 * i + k, 2 * i + k - 1)
                    else:
                        with sp.Fori(0, NC // 2) as i:
                            for k in range(2):
                                rows(k, c * NC + 2 * i + k, c * NC + 2 * i + k - 1)

            @block.gpsimd
            def _(pool):
                P = nc.gpsimd
                for t in (hist_h, hist_dz):
                    P.memset(t[:, :, :, :], 0.0).then_inc(zeroed, 1)
                P.memset(hist_y[:, :, :], 0.0).then_inc(zeroed, 1)
                P.memset(dz_in[:, :, :, :], 0.0).then_inc(zeroed, 1)
                pool.wait_ge(zeroed, 4)
                for c in range(NCH):
                    L = (c + 1) * NC
                    if c >= 1:
                        S = c * NC
                        pool.wait_ge(dz_ready, 2 * S)
                        with pool.Fori(0, NB // 2) as i:
                            for k in range(2):
                                b = 2 * i + k
                                pool.wait_ge(base_done, (c - 1) * NB + b + 1)
                                P.tensor_copy(dz_in[:, k, :, 0:S], hist_dz[:, :, bass.ds(b, 1), 0:S].rearrange("p a b s -> p (a b) s"))
                                P.tensor_copy(g_in[0:S, k, :], M["g_t"][0:S, bass.ds(b, 1), S:S + NC].rearrange("p a s -> p (a s)")).then_inc(staged, 1)
                    with pool.Fori(0, NC // 2) as i:
                        for k in range(2):
                            t = c * NC + 2 * i + k
                            pool.wait_ge(w_in[k], (c * NC + 2 * i) * 16 + 32)
                            for g in range(2):
                                pool.wait_ge(p2_ready, 2 * t + g + 1)
                                o = slice(g * GB * L, (g + 1) * GB * L)
                                P.tensor_tensor(y_w[:, o].rearrange("p (b s) -> p b s", s=L), w_row[:, k, o].rearrange("p (b s) -> p b s", s=L),
                                                hist_y[:, g * GB:(g + 1) * GB, 0:L], ALU.mult).then_inc(yw_ready, 1)
                            for g in range(2):
                                pool.wait_ge(h_ready, 2 * t + g + 1)
                                h = grp_at(hist_h, g, t)
                                P.tensor_tensor(grp(hg, g), h, grp(sg, g), ALU.mult)
                                P.tensor_tensor(grp(hs, g), h, grp(sg, g), ALU.add).then_inc(pool_step, 1)
                                pool.wait_ge(pool_step, 2 * t + g + 1)
                                P.tensor_tensor(grp(slope, g), grp(hs, g), grp(hg, g), ALU.subtract).then_inc(slope_ready, 1)

            @block.scalar
            def _(act):
                for c in range(NCH):
                    if c >= 1:
                        S = c * NC
                        with act.Fori(0, NB // 2) as i:
                            for k in range(2):
                                act.wait_ge(dz_turned, (c - 1) * NB + 2 * i + k + 1)
                                nc.scalar.activation(dz_t[0:S, k, :], flat_wide[0:S, k * 512:k * 512 + FH], ACT.Copy).then_inc(dzt_ready, 1)
                    with act.Fori(0, NC) as i:
                        for g in range(2):
                            act.wait_ge(z_ready, 2 * (c * NC + i) + g + 1)
                            nc.scalar.activation(grp(sg, g), grp(z, g), ACT.Sigmoid).then_inc(sg_ready, 1)

            @block.tensor
            def _(pe):
                MM = nc.tensor.matmul
                pe.sem_inc(base_done, 2)
                pe.wait_ge(ones_in, 32)
                for c in range(NCH):
                    L = (c + 1) * NC
                    W = GB * L

                    def parts(start):
                        cuts = [start, *[o for o in range(512, 1536, 512) if start < o < start + W], start + W]
                        return list(zip(cuts, cuts[1:]))

                    if c >= 1:
                        S = c * NC
                        with pe.Fori(0, NB // 2) as i:
                            for k in range(2):
                                n = (c - 1) * NB + 2 * i + k
                                pe.wait_ge(staged, n + 1)
                                for a in range(2):
                                    mm = nc.tensor.transpose(flat_wide[0:NT, k * 512 + a * 128:k * 512 + (a + 1) * 128], dz_in[:, k, a, :], ident[:, :])
                                mm.then_inc(dz_turned, 1)
                            for k in range(2):
                                n = (c - 1) * NB + 2 * i + k
                                pe.wait_ge(dzt_ready, n + 1)
                                pe.wait_ge(base_added, n + 1)
                                for a in range(2):
                                    mm = MM(flat_wide[:, 1024 + k * 512 + a * NC:1024 + k * 512 + (a + 1) * NC], dz_t[0:S, k, a * 128:(a + 1) * 128], g_in[0:S, k, :], start=True, stop=True)
                                mm.then_inc(base_done, 1)
                    with pe.Fori(0, NC) as i:
                        t = c * NC + i

                        def forward(g):
                            pe.wait_ge(h_ready, 2 * t + g + 1)
                            for a in range(2):
                                for b2 in range(2):
                                    o = b2 * HB + g * GB
                                    MM(ps_pred(g), M["b0"][:, a, b2, :], hist_h[:, a, o:o + GB, bass.ds(t, 1)].rearrange("p b s -> p (b s)"),
                                       start=a + b2 == 0, stop=a + b2 == 2)
                            for a in range(2):
                                pe.wait_ge(p1_ready, 4 * t + 2 * g + a + 1)
                                for b2 in range(2):
                                    for o, e in parts(0):
                                        mm = MM(wide[:, g, o:e], cols[:, b2, :], prod[:, g, a, b2 * W + o:b2 * W + e], start=a + b2 == 0, stop=a + b2 == 2)
                            mm.then_inc(hh_done, 1)

                        def backward(g):
                            pe.wait_ge(dy_ready, 2 * t + g + 1)
                            for a in range(2):
                                for b2 in range(2):
                                    MM(ps_back(g)[:, 2 * a + b2, :], M["b0t"][:, b2, a * 128:(a + 1) * 128], cols_at(hist_y, g, t), start=True, stop=True)
                            pe.wait_ge(p2_ready, 2 * t + g + 3)
                            for b2 in range(2):
                                for o, e in parts(b2 * W):
                                    mm = MM(wide[:, g, o:e], rows_[:, b2, :], y_prod[:, g, o - b2 * W:e - b2 * W], start=True, stop=True)
                            mm.then_inc(yy_done, 1)

                        forward(0)
                        forward(1)
                        backward(0)
                        backward(1)

            @block.vector
            def _(dve):
                V = nc.vector
                V.sem_inc(base_added, 2)
                V.sem_inc(p2_ready, 2)
                dve.wait_ge(zeroed, 4)
                for c in range(NCH):
                    L = (c + 1) * NC
                    W = GB * L
                    if c >= 1:
                        S = c * NC
                        with dve.Fori(0, NB // 2) as i:
                            for k in range(2):
                                n = (c - 1) * NB + 2 * i + k
                                dve.wait_ge(base_done, n + 3)
                                part = M["z_base"][:, :, bass.ds(2 * i + k, 1), S:S + NC].rearrange("p a b s -> p (a b) s")
                                V.tensor_tensor(part, part, flat_wide[:, 1024 + k * 512:1024 + k * 512 + 2 * NC].rearrange("p (a s) -> p a s", a=2), ALU.add).then_inc(base_added, 1)
                        dve.wait_ge(base_added, c * NB + 2)
                    with dve.Fori(0, NC // 2) as i:
                        for k in range(2):
                            t = c * NC + 2 * i + k
                            s = Steps(dve, step, t * K)
                            dve.wait_ge(g_rows_in[k], (c * NC + 2 * i) * 8 + 16)
                            bs = lambda x: x.rearrange("p (b s) -> p b s", s=L)
                            hist = lambda x, a, g, o, e: x[:, a, :, o:e].rearrange("p (c b) s -> p c b s", c=2)[:, :, GB * g:GB * (g + 1), :]
                            g_part = lambda g: g_row[:, k, :, :].rearrange("p (c b) s -> p c b s", c=2)[:, :, GB * g:GB * (g + 1), :]
                            z_part = lambda a, g: z_prod[:, a, 2 * GB * g:2 * GB * (g + 1), :]
                            for g in range(2):
                                for a in range(2):
                                    ins = V.tensor_tensor(z_part(a, g).rearrange("p (c b) s -> p c b s", c=2), hist(hist_dz, a, g, c * NC, (c + 1) * NC), g_part(g), ALU.mult)
                                s.link(ins)
                                for a in range(2):
                                    ins = V.reduce_sum(zsum[:, a, :].rearrange("p (c b) -> p c b", c=2)[:, :, GB * g:GB * (g + 1)], z_part(a, g).rearrange("p (c b) s -> p c b s", c=2), AX.X)
                                s.link(ins)
                                V.tensor_tensor(grp(z, g), grp(zsum, g), grp_at(M["z_base"], g, t), ALU.add).then_inc(z_ready, 1)
                            for g in range(2):
                                dve.wait_ge(sg_ready, 2 * t + g + 1)
                                V.tensor_tensor(grp_at(hist_h, g, t), grp(z, g), grp(sg, g), ALU.mult).then_inc(h_ready, 1)
                                dve.wait_ge(h_ready, 2 * t + g + 1)
                                for a in range(2):
                                    now = hist_h[:, a, :, bass.ds(t, 1)].rearrange("p (c b) s -> p c b s", c=2)[:, :, GB * g:GB * (g + 1), :]
                                    V.tensor_tensor(prod[:, g, a, 0:2 * W].rearrange("p (c b s) -> p c b s", c=2, s=L), hist(hist_h, a, g, 0, L),
                                                    bc(now, 128, 2, GB, L), ALU.mult).then_inc(p1_ready, 1)
                            for g in range(2):
                                dve.wait_ge(hh_done, 2 * t + g + 1)
                                dve.wait_ge(yw_ready, 2 * t + g + 1)
                                yw, yp = y_w[:, g * W:(g + 1) * W], y_prod[:, g, 0:W]
                                q = slice(GB * g, GB * (g + 1))
                                V.tensor_tensor(yp, wide[:, g, 0:W], yw, ALU.mult)
                                s.link(V.scalar_tensor_tensor(pred[:, q], ps_pred(g), 2.0 / DM, cols_at(M["c_y"], g, t), ALU.mult, ALU.mult))
                                V.scalar_tensor_tensor(off[:, q], cols_at(M["v_y"], g, t), -2.0 / DM, pred[:, q], ALU.mult, ALU.add)
                                s.link(V.reduce_sum(ysum[:, q], bs(yp), AX.X))
                                V.scalar_tensor_tensor(cols_at(hist_y, g, t), ysum[:, q], 2.0 / DM, off[:, q], ALU.mult, ALU.add).then_inc(dy_ready, 1)
                                dve.wait_ge(dy_ready, 2 * t + g + 1)
                                V.tensor_tensor(bs(yp), bs(yw), bc(hist_y[:, q, bass.ds(t, 1)], 128, GB, L), ALU.mult).then_inc(p2_ready, 1)
                            for g in range(2):
                                dve.wait_ge(yy_done, 2 * t + g + 1)
                                four = lambda x: x.rearrange("p (c b s) -> p c b s", c=2, s=L)
                                for a in range(2):
                                    ins = V.tensor_tensor(four(prod[:, g, a, 0:2 * W]), hist(hist_h, a, g, 0, L), four(wide[:, g, 0:2 * W]), ALU.mult)
                                for a in range(2):
                                    V.tensor_tensor(first_part[:, a, :].rearrange("p (c b) -> p c b", c=2)[:, :, GB * g:GB * (g + 1)], ps_back(g)[:, 2 * a:2 * a + 2, :],
                                                    M["c_f"][:, :, bass.ds(t, 1)].rearrange("p (c b) s -> p c (b s)", c=2)[:, :, GB * g:GB * (g + 1)], ALU.mult)
                                s.link(ins)
                                for a in range(2):
                                    ins = V.reduce_sum(dh[:, a, :].rearrange("p (c b) -> p c b", c=2)[:, :, GB * g:GB * (g + 1)], four(prod[:, g, a, 0:2 * W]), AX.X)
                                s.link(ins)
                                s.link(V.tensor_tensor(grp(dh, g), grp(dh, g), grp(first_part, g), ALU.add))
                                dve.wait_ge(slope_ready, 2 * t + g + 1)
                                V.tensor_tensor(grp_at(hist_dz, g, t), grp(dh, g), grp(slope, g), ALU.mult).then_inc(dz_ready, 1)
                            for g in range(2):
                                dve.wait_ge(dz_ready, 2 * t + g + 1)
                            assert s.n == K, s.n


def memory_outputs(nc, M, H, hist_h, hist_dz, hist_y, ident):
    NS = 4
    NR = HB // 2
    with ExitStack() as ctx:
        sb = lambda n, sh: ctx.enter_context(nc.sbuf_tensor("mo_" + n, sh, F32))
        sem = lambda n: ctx.enter_context(nc.semaphore("mo_" + n))
        kq = sb("kq", [DM, NS, 3, NT])
        w = sb("w", [NT, NS, NT])
        cn = sb("cn", [128, NS, NT])
        dz, hs = sb("dz", [128, NS, 2, NT]), sb("hs", [128, NS, 2, NT])
        dzt = sb("dzt", [NT, NS, FH])
        dyt = sb("dyt", [NT, HB, 128])
        s1, s2 = sb("s1", [NT, NS, NT]), sb("s2", [NT, NS, NT])
        sg, hq, hqc = (sb(n, [128, NS, 2, NT]) for n in ("sg", "hq", "hqc"))
        psA = ctx.enter_context(nc.psum_tensor("mo_psA", [128, NS, 512], F32))
        psB = ctx.enter_context(nc.psum_tensor("mo_psB", [128, NS, 512], F32))
        loaded = [sem(f"loaded{k}") for k in range(NS)]
        dy_turned, dyt_ready, staged, dz_turned, dzt_ready = sem("dy_turned"), sem("dyt_ready"), sem("staged"), sem("dz_turned"), sem("dzt_ready")
        s1_done, s1_ready, z_done, sg_ready, hq_ready = sem("s1_done"), sem("s1_ready"), sem("z_done"), sem("sg_ready"), sem("hq_ready")
        hqc_ready, s2_done, s2_ready, out_done, added = sem("hqc_ready"), sem("s2_done"), sem("s2_ready"), sem("out_done"), sem("added")
        batch = lambda i, k: 2 * i + k // 2 + HB * (k % 2)
        zq = lambda k: psA[:, k, 256:256 + 2 * NT].rearrange("p (a t) -> p a t", a=2)
        with nc.Block() as block:
            @block.sync
            def _(sp):
                def load(i, k):
                    cols = bass.ds(batch(i, k) * NT, NT)
                    for j, n in enumerate(("k_t", "q_t", "qc_t")):
                        sp.dma_start(kq[:, k, j, :], M[n][:, cols]).then_inc(loaded[k], 16)
                    sp.dma_start(w[:, k, :], M["w_t"][:, cols]).then_inc(loaded[k], 16)
                    sp.dma_start(cn[:, k, :], M["c_now"][:, cols]).then_inc(loaded[k], 16)

                for k in range(NS):
                    load(0, k)
                with sp.Fori(1, NR) as i:
                    for k in range(NS):
                        sp.wait_ge(out_done, NS * i - NS + k + 1)
                        load(i, k)

            @block.gpsimd
            def _(pool):
                P = nc.gpsimd

                def stage(i, k):
                    b = batch(i, k)
                    P.tensor_copy(dz[:, k, :, :], hist_dz[:, :, bass.ds(b, 1), :].rearrange("p a b s -> p (a b) s"))
                    P.tensor_copy(hs[:, k, :, :], hist_h[:, :, bass.ds(b, 1), :].rearrange("p a b s -> p (a b) s")).then_inc(staged, 1)

                def scale(i, k):
                    pool.wait_ge(hq_ready, NS * i + k + 1)
                    P.tensor_tensor(hqc[:, k, :, :], hq[:, k, :, :], bc(cn[:, k:k + 1, :], 128, 2, NT), ALU.mult).then_inc(hqc_ready, 1)

                for k in range(NS):
                    stage(0, k)
                with pool.Fori(0, NR - 1) as i:
                    for k in range(NS):
                        scale(i, k)
                    for k in range(NS):
                        pool.wait_ge(s2_done, NS * i + k + 1)
                        stage(i + 1, k)
                for k in range(NS):
                    scale(NR - 1, k)

            @block.tensor
            def _(pe):
                T, MM = nc.tensor.transpose, nc.tensor.matmul
                for b in range(HB):
                    mm = T(psA[0:NT, b // 4, b % 4 * 128:(b % 4 + 1) * 128], hist_y[:, b, :], ident[:, :])
                    if b % 4 == 3:
                        mm.then_inc(dy_turned, 1)
                pe.wait_ge(dyt_ready, 4)
                with pe.Fori(0, NR) as i:
                    for k in range(NS):
                        pe.wait_ge(staged, NS * i + k + 1)
                        for a in range(2):
                            mm = T(psA[0:NT, k, a * 128:(a + 1) * 128], dz[:, k, a, :], ident[:, :])
                        mm.then_inc(dz_turned, 1)
                        pe.wait_ge(added, NS * i + k + 1)
                        pe.wait_ge(loaded[k], 80 * i + 80)
                        MM(psB[0:NT, k, 0:NT], kq[:, k, 0, :], kq[:, k, 1, :], start=True, stop=True).then_inc(s1_done, 1)
                    for k in range(NS):
                        pe.wait_ge(dzt_ready, NS * i + k + 1)
                        pe.wait_ge(s1_ready, NS * i + k + 1)
                        for a in range(2):
                            o = slice(a * 128, (a + 1) * 128)
                            MM(psA[:, k, 256 + a * NT:256 + (a + 1) * NT], dzt[:, k, o], s1[:, k, :], start=True, stop=False)
                            mm = MM(psA[:, k, 256 + a * NT:256 + (a + 1) * NT], M["a0"][:, o], kq[:, k, 2, :], start=False, stop=True)
                        mm.then_inc(z_done, 1)
                    for k in range(NS):
                        pe.wait_ge(hq_ready, NS * i + k + 1)
                        for a in range(2):
                            mm = MM(psB[0:NT, k, 128:128 + NT], hs[:, k, a, :], hq[:, k, a, :], start=a == 0, stop=a == 1)
                        mm.then_inc(s2_done, 1)
                    for k in range(NS):
                        pe.wait_ge(hqc_ready, NS * i + k + 1)
                        pe.wait_ge(s2_ready, NS * i + k + 1)
                        for a in range(2):
                            MM(psB[0:NT, k, 256:256 + DM], hqc[:, k, a, :], M["b0"][:, a, 0, 0:DM], start=a == 0, stop=False)
                        MM(psB[0:NT, k, 256:256 + DM], s2[:, k, :], dyt[:, bass.ds(2 * i + k // 2, 1), k % 2 * DM:(k % 2 + 1) * DM].rearrange("p b d -> p (b d)"),
                           start=False, stop=True).then_inc(out_done, 1)

            @block.scalar
            def _(act):
                with act.Fori(0, NR) as i:
                    for k in range(NS):
                        act.wait_ge(dz_turned, NS * i + k + 1)
                        nc.scalar.activation(dzt[:, k, :], psA[0:NT, k, 0:FH], ACT.Copy).then_inc(dzt_ready, 1)
                    for k in range(NS):
                        act.wait_ge(z_done, NS * i + k + 1)
                        nc.scalar.activation(sg[:, k, :, :], zq(k), ACT.Sigmoid).then_inc(sg_ready, 1)

            @block.vector
            def _(dve):
                V = nc.vector
                V.sem_inc(added, NS)
                for j in range(4):
                    dve.wait_ge(dy_turned, j + 1)
                    V.tensor_copy(dyt[:, 4 * j:4 * j + 4, :].rearrange("p b c -> p (b c)"), psA[0:NT, j, :]).then_inc(dyt_ready, 1)
                with dve.Fori(0, NR) as i:
                    for k in range(NS):
                        dve.wait_ge(s1_done, NS * i + k + 1)
                        V.tensor_tensor(s1[:, k, :], psB[0:NT, k, 0:NT], w[:, k, :], ALU.mult).then_inc(s1_ready, 1)
                    for k in range(NS):
                        dve.wait_ge(sg_ready, NS * i + k + 1)
                        V.tensor_tensor(hq[:, k, :, :], zq(k), sg[:, k, :, :], ALU.mult).then_inc(hq_ready, 1)
                    for k in range(NS):
                        dve.wait_ge(s2_done, NS * i + k + 1)
                        V.tensor_tensor(s2[:, k, :], psB[0:NT, k, 128:128 + NT], w[:, k, :], ALU.mult).then_inc(s2_ready, 1)
                    for k in range(NS):
                        dve.wait_ge(out_done, NS * i + k + 1)
                        row = H[:, bass.ds(batch(i, k), 1), :].rearrange("t b d -> t (b d)")
                        V.tensor_tensor(row, row, psB[0:NT, k, 256:256 + DM], ALU.add).then_inc(added, 1)
                dve.wait_ge(added, NB + NS)


def early_fusion(nc, out, A):
    with ExitStack() as ctx:
        sb = lambda n, sh: ctx.enter_context(nc.sbuf_tensor(n, sh, F32))
        ident = sb("ident", [128, 128])
        constants_in = ctx.enter_context(nc.semaphore("constants_in"))
        h_in = ctx.enter_context(nc.semaphore("h_in"))
        h_out = ctx.enter_context(nc.semaphore("h_out"))
        image = nc.dram_tensor("image_rows", [NB, S, S], F32).ap()
        with nc.Block() as block:
            @block.sync
            def _(sp):
                sp.dma_start(ident[:, :], A["c_ident"]).then_inc(constants_in, 16)
                sp.wait_ge(constants_in, 16)

        t = lambda n: A["L0_tok_" + n]
        image_network(nc, A["x"], image, ident, {n: A["c_" + n] for n in ("d1", "d2", "e1", "e2")},
                      t("fc0_w"), t("fc0_b"), [t(f"sw{i}") for i in range(NL)], [t(f"cw{i}") for i in range(NL)],
                      [t(f"cb{i}") for i in range(NL)], t("fc1_w"), t("fc1_b"), t("fc2_w"), t("fc2_b"))

        H = sb("H", [NT, NB, DM])
        ln = layernorm_semaphores(nc, ctx)
        with nc.Block() as block:
            @block.sync
            def _(sp):
                sp.dma_start(H[0:S, :, :], image.rearrange("b t d -> t b d")).then_inc(h_in, 16)
                sp.dma_start(H[S:NT, :, :], A["txt"].rearrange("b t d -> t b d")).then_inc(h_in, 16)
                sp.wait_ge(h_in, 32)

        def normed(tag, stage):
            XT = stage.enter_context(nc.sbuf_tensor("XT_" + tag, [DM, TOK], F32))
            with ExitStack() as own:
                XN, squares = (own.enter_context(nc.sbuf_tensor(n + tag, [NT, NB, DM], F32)) for n in ("XN_", "squares_"))
                layernorm_transposed(nc, ln, "abcd".index(tag), H, XN, squares, XT, ident)
            return XT

        with ExitStack() as stage:
            XT = normed("a", stage)
            linear_attention(nc, H, XT, ident, A["L0_attn_Q"], A["L0_attn_E"])
        with ExitStack() as stage:
            XT = normed("b", stage)
            f = lambda n: A["L0_ffn_" + n]
            top_two_experts(nc, H, XT, f("router_w1"), f("router_b1"), f("router_w2"), f("router_b2"), f("expert_w1"), f("expert_b1"),
                            f("expert_w2"), f("expert_b2"), f("expert_w3"), f("expert_b3"))
        with ExitStack() as mem:
            M = memory_tensors(nc, mem)
            m = lambda n: A["L1_attn_" + n]
            with ExitStack() as stage:
                XT = normed("c", stage)
                memory_setup(nc, M, XT, ident, A["c_inject"], m("W_fused"), m("W0"), m("W1"), m("P0"), m("P1"))
            msb = lambda n, sh: mem.enter_context(nc.sbuf_tensor(n, sh, F32))
            hist_h, hist_dz, hist_y = msb("hist_h", [128, 2, NB, NT]), msb("hist_dz", [128, 2, NB, NT]), msb("hist_y", [128, HB, NT])
            memory_scan(nc, M, hist_h, hist_dz, hist_y, ident, A["c_cols"], A["c_rows"])
            memory_outputs(nc, M, H, hist_h, hist_dz, hist_y, ident)
        with ExitStack() as stage:
            XT = normed("d", stage)
            w = lambda n: A["L1_ffn_" + n]
            best_expert(nc, H, XT, ident, w("gate_w"), w("gate_b"), w("w1"), w("b1"), w("w2"), w("b2"))
        with nc.Block() as block:
            @block.sync
            def _(sp):
                sp.dma_start(out.rearrange("b t d -> t b d"), H[:, :, :]).then_inc(h_out, 16)
                sp.wait_ge(h_out, 16)


def shape_constants():
    half = np.zeros((128, 2, 128), np.float32)
    half[:, 0, 0:64] = 1.0
    half[:, 1, 64:128] = 1.0
    return dict(spectral_constants(), ident=np.eye(128, dtype=np.float32), inject=(-2 * MAX_LR * np.eye(NT)).astype(np.float32),
                cols=half, rows=np.ascontiguousarray(half.transpose(2, 1, 0)))


_INS = ['x', 'txt', 'L0_tok_fc0_w', 'L0_tok_fc0_b', 'L0_tok_sw0', 'L0_tok_cw0', 'L0_tok_cb0', 'L0_tok_sw1', 'L0_tok_cw1', 'L0_tok_cb1',
        'L0_tok_sw2', 'L0_tok_cw2', 'L0_tok_cb2', 'L0_tok_sw3', 'L0_tok_cw3', 'L0_tok_cb3', 'L0_tok_fc1_w', 'L0_tok_fc1_b', 'L0_tok_fc2_w',
        'L0_tok_fc2_b', 'L0_attn_Q', 'L0_attn_E', 'L0_ffn_router_w1', 'L0_ffn_router_b1', 'L0_ffn_router_w2', 'L0_ffn_router_b2',
        'L0_ffn_expert_w1', 'L0_ffn_expert_b1', 'L0_ffn_expert_w2', 'L0_ffn_expert_b2', 'L0_ffn_expert_w3', 'L0_ffn_expert_b3',
        'L1_attn_W_fused', 'L1_attn_W0', 'L1_attn_W1', 'L1_attn_P0', 'L1_attn_P1', 'L1_ffn_gate_w', 'L1_ffn_gate_b', 'L1_ffn_w1',
        'L1_ffn_b1', 'L1_ffn_w2', 'L1_ffn_b2']


def kernel(**inputs):
    import concourse.bacc as bacc
    from concourse.bass_utils import run_bass_kernel_spmd

    nc = bacc.Bacc("TRN2", target_bir_lowering=False, num_devices=1)
    arrays, A = {}, {}
    for name, a in [*((n, inputs[n]) for n in _INS), *(("c_" + n, a) for n, a in shape_constants().items())]:
        a = np.ascontiguousarray(a)
        arrays[f"in_{name}_dram"] = a
        A[name] = nc.dram_tensor(f"in_{name}_dram", a.shape, mybir.dt.from_np(a.dtype), kind="ExternalInput").ap()
    out = nc.dram_tensor("out_0_dram", (NB, NT, DM), F32, kind="ExternalOutput").ap()
    early_fusion(nc, out, A)
    r = run_bass_kernel_spmd(nc, [arrays], core_ids=[0])
    return r.results[0]["out_0_dram"]
```

```python
from contextlib import ExitStack

import numpy as np
import concourse.bass as bass
from concourse import mybir

F32 = mybir.dt.float32
ALU = mybir.AluOpType
ACT = mybir.ActivationFunctionType
AX = mybir.AxisListType

NB = 32
NT = 96
DM = 64
TOK = NB * NT
EPS = 1e-5
MAX_LR = 0.1


def bc(ap, *shape):
    return ap.broadcast_to(list(shape))


class Steps:

    def __init__(self, eng, sem, base=0):
        self.eng, self.sem, self.base, self.n = eng, sem, base, 0

    def mark(self, ins):
        ins.then_inc(self.sem, 1)
        self.n += 1
        return self.n

    def link(self, ins):
        self.mark(ins)
        self.eng.wait_ge(self.sem, self.base + self.n)


C = 32
S = 64
MO = 20
KG, KJ = 5, 4
NL = 4
NGRP = 4


def spectral_constants():
    n = np.arange(S)
    kx = np.array([KG * j + g for g in range(KG) for j in range(KJ)])
    ky = np.arange(MO)
    scale = 1.0 / np.sqrt(S)
    cx, sx = (f(2 * np.pi * np.outer(n, kx) / S) * scale for f in (np.cos, np.sin))
    cy, sy = (f(2 * np.pi * np.outer(n, ky) / S) * scale for f in (np.cos, np.sin))
    d1 = np.zeros((2, S, 2, 2, MO))
    d2 = np.zeros((2, 2, S, MO, 2, 2))
    e1 = np.zeros((2, MO, 2, 2, S))
    e2 = np.zeros((128, 2, S))
    twice = np.where(ky == 0, 1.0, 2.0)[:, None]
    ck, sk = (f(2 * np.pi * np.outer(ky, n) / S) * scale for f in (np.cos, np.sin))
    for b in range(2):
        d1[b, :, b, 0], d1[b, :, b, 1] = cx, -sx
        d2[0, b, :, :, b, 0], d2[0, b, :, :, b, 1] = cy, -sy
        d2[1, b, :, :, b, 0], d2[1, b, :, :, b, 1] = sy, cy
        e1[b, :, 0, b, :], e1[b, :, 1, b, :] = twice * ck, -twice * sk
        e2[b * 40:b * 40 + 20, b], e2[b * 40 + 20:b * 40 + 40, b] = ck, -sk
    e2[96] = 1.0
    f = lambda a, *s: np.ascontiguousarray(a.reshape(s).astype(np.float32))
    return dict(d1=f(d1, 128, 80), d2=f(d2.reshape(2, 128, 80).transpose(1, 0, 2), 128, 160), e1=f(e1, 80, 128), e2=f(e2, 128, 128))


def image_network(nc, x, h_out, ident, consts, fc0_w, fc0_b, sw, cw, cb, fc1_w, fc1_b, fc2_w, fc2_b):
    RING = 6
    PH = 8
    with ExitStack() as ctx:
        sb = lambda n, sh: ctx.enter_context(nc.sbuf_tensor("im_" + n, sh, F32))
        sem = lambda n: ctx.enter_context(nc.semaphore("im_" + n))
        a = sb("a", [128, NGRP, 2 * S * C])
        spec = sb("spec", [128, KG * MO, 32])
        mixed = sb("mixed", [128, KG, NGRP, 2, 2, 80])
        half_t = sb("half_t", [128, 2, 2560])
        u = sb("u", [97, 2 * S * C])
        wbd = sb("wbd", [128, 128, KG * MO])
        chan = sb("chan", [128, 2, 512])
        xi = sb("xi", [128, 2, 2, 192])
        xt = sb("xt", [97, 4, 128])
        fc0 = sb("fc0", [97, 1024])
        d1, d2, e1, e2 = sb("d1", [128, 80]), sb("d2", [128, 2, 80]), sb("e1", [80, 128]), sb("e2", [128, 128])
        cwn, cwt = sb("cwn", [128, 128]), sb("cwt", [128, NL, 128])
        fc1 = sb("fc1", [128, 2, 128])
        fc1b, fc2, fc2b = sb("fc1b", [128, 1]), sb("fc2", [128, 2]), sb("fc2b", [128, 1])
        ho = sb("ho", [128, 2, S])
        gl = half_t[:, :, 0:512]
        ring = ctx.enter_context(nc.psum_tensor("im_ring", [128, RING, 512], F32))
        acc = ctx.enter_context(nc.psum_tensor("im_acc", [128, 2, 512], F32))
        zeroed, loaded, cw_in, cw_turned, cw_ready = sem("zeroed"), sem("loaded"), sem("cw_in"), sem("cw_turned"), sem("cw_ready")
        with nc.Block() as block:
            @block.gpsimd
            def _(pool):
                nc.gpsimd.memset(wbd[:, :, :], 0.0).then_inc(zeroed, 1)

            @block.vector
            def _(dve):
                for t in (u[64:97, :], xt[:, :, :], fc0[:, :], cwn[:, :], fc1[:, :, :], fc2[:, :]):
                    nc.vector.memset(t, 0.0).then_inc(zeroed, 1)
                dve.wait_ge(zeroed, 7)
                nc.vector.memset(xt[96:97, :, :], 1.0).then_inc(zeroed, 1)
                for l in range(NL):
                    dve.wait_ge(cw_turned, l + 1)
                    nc.vector.tensor_copy(cwt[:, l, :], acc[:, l % 2, 0:128]).then_inc(cw_ready, 1)
                dve.wait_ge(cw_ready, NL)
                dve.wait_ge(zeroed, 8)

            @block.tensor
            def _(pe):
                for l in range(NL):
                    pe.wait_ge(cw_in, 64 * (l + 1))
                    if l >= 2:
                        pe.wait_ge(cw_ready, l - 1)
                    nc.tensor.transpose(acc[:, l % 2, 0:128], cwn[:, :], ident[:, :]).then_inc(cw_turned, 1)

            @block.sync
            def _(sp):
                sp.wait_ge(zeroed, 7)
                for l in range(NL):
                    if l:
                        sp.wait_ge(cw_turned, l)
                    for k in range(4):
                        sp.dma_start(cwn[k * C:(k + 1) * C, k * C:(k + 1) * C], cw[l]).then_inc(cw_in, 16)

            @block.scalar
            def _(act):
                n = 0
                act.wait_ge(zeroed, 7)
                with nc.allow_non_contiguous_dma(reason="small weights"):
                    for dst, src in ((d1[:, :], consts["d1"]), (d2[:, :, :].rearrange("p a c -> p (a c)"), consts["d2"]), (e1[:, :], consts["e1"]), (e2[:, :], consts["e2"]),
                                     (fc0[96:97, :].rearrange("p (w c) -> p w c", c=C), fc0_b.rearrange("(a b c) -> a b c", a=1, b=1).broadcast_to([1, 32, C])),
                                     (fc2b[:, :], fc2_b.rearrange("(a b) -> a b", a=1).broadcast_to([128, 1]))):
                        act.dma_start(dst, src).then_inc(loaded, 16)
                        n += 1
                    for k in range(4):
                        act.dma_start(fc1[k * C:(k + 1) * C, k // 2, k % 2 * 64:(k % 2 + 1) * 64], fc1_w).then_inc(loaded, 16)
                    for k in range(2):
                        act.dma_start(fc1b[k * 64:(k + 1) * 64, :], fc1_b.rearrange("(p a) -> p a", a=1)).then_inc(loaded, 16)
                        act.dma_start(fc2[k * 64:(k + 1) * 64, k:k + 1], fc2_w).then_inc(loaded, 16)
                    for k in range(32):
                        act.dma_start(fc0[3 * k:3 * k + 3, k * C:(k + 1) * C], fc0_w).then_inc(loaded, 16)
                    n += 4 + 4 + 32
                act.wait_ge(loaded, 16 * n)

        filled, drained = sem("filled"), sem("drained")
        acc_full, acc_read = sem("acc_full"), sem("acc_read")
        w_in, bias_in, xi_in = sem("w_in"), sem("bias_in"), [sem("xi_in0"), sem("xi_in1")]
        ho_ready, ho_stored = sem("ho_ready"), sem("ho_stored")
        FC0_FILLS, LAYER_FILLS, FC_FILLS = 4 * 9, 4 * 8 + 10 + 4 * 21, 4 * 10
        HALF_FILLS = FC0_FILLS + NL * LAYER_FILLS + FC_FILLS
        LAYER_ACC, HALF_ACC = 4 * PH, NL * 4 * PH + 4 * PH * 2
        assert LAYER_FILLS % RING == 0
        MIXED_AT = 4 * 8 + 10
        img = x.rearrange("(n b c) h w k -> n b h c (w k)", b=2, c=2)
        out_img = h_out.rearrange("(n b c) h w -> n b h c w", b=2, c=2)

        class Fills:
            def __init__(self, start, base=0):
                self.n, self.bank, self.base = start, start % RING, base
            def next(self):
                n, bank = self.n, self.bank
                self.n, self.bank = n + 1, (bank + 1) % RING
                return self.base + n, bank

        with nc.Block() as block:
            @block.sync
            def _(sp):
                for half in range(2):
                    base = half * HALF_FILLS
                    for l in range(NL):
                        r = NL * half + l
                        if r:
                            sp.wait_ge(filled, base + FC0_FILLS + (l - 1) * LAYER_FILLS + MIXED_AT if l else base - FC_FILLS - LAYER_FILLS + MIXED_AT)
                        for j in range(KJ):
                            o = slice(j * C, (j + 1) * C)
                            sp.dma_start(wbd[o, o, :], sw[l][:, :, KG * j:KG * (j + 1), :].rearrange("i o x y -> i o (x y)")).then_inc(w_in, 16)
                        if r:
                            sp.wait_ge(acc_full, half * HALF_ACC + l * LAYER_ACC if l else half * HALF_ACC - 4 * PH * 2)
                        sp.dma_start(u[96:97, :].rearrange("p (w c) -> p w c", c=C),
                                     cb[l].rearrange("(a b c) -> a b c", a=1, b=1).broadcast_to([1, 2 * S, C])).then_inc(bias_in, 16)

            @block.gpsimd
            def _(pool):
                def load_image(n):
                    if n >= 2:
                        pool.wait_ge(filled, (n - 2) // NGRP * HALF_FILLS + (n - 2) % NGRP * 9 + 1)
                    for b2 in range(2):
                        pool.dma_start(xi[b2 * S:(b2 + 1) * S, n % 2, :, :], img[n, b2]).then_inc(xi_in[n % 2], 16)

                def store_result(n):
                    pool.wait_ge(ho_ready, n + 1)
                    for b2 in range(2):
                        pool.dma_start(out_img[n, b2], ho[b2 * S:(b2 + 1) * S, :, :]).then_inc(ho_stored, 16)

                for n in range(NGRP + 2):
                    load_image(n)
                for n in range(NGRP):
                    store_result(n)
                for n in range(NGRP + 2, 2 * NGRP):
                    load_image(n)
                for n in range(NGRP, 2 * NGRP):
                    store_result(n)
                pool.wait_ge(ho_stored, 32 * 2 * NGRP)

            def second_layer(pe, MM, item, start):
                n, p, v = item
                if p + v == 0:
                    pe.wait_ge(drained, start + 4 + 1)
                pe.wait_ge(acc_read, n + 3)
                for m in range(4):
                    col = p * 16 + m * 4 + v * 2
                    mm = MM(ring[:, (start + 4) % RING, col:col + 2], gl[:, v, m * 128:(m + 1) * 128], fc2[:, :], start=True, stop=True)
                return mm

            @block.tensor
            def _(pe):
                T, MM = nc.tensor.transpose, nc.tensor.matmul

                def fill(f):
                    n, bank = f.next()
                    pe.wait_ge(drained, n + 1)
                    return ring[:, bank, :]

                def have(n):
                    pe.wait_ge(drained, n + RING)

                def input_layer(f, half):
                    for g in range(NGRP):
                        n = half * NGRP + g
                        pe.wait_ge(xi_in[n % 2], 32 * (n // 2 + 1))
                        ps = fill(f)
                        for k in range(4):
                            mm = T(ps[0:96, k * 128:(k + 1) * 128], xi[:, n % 2, k // 2, k % 2 * 96:(k % 2 + 1) * 96], ident[:, :])
                        mm.then_inc(filled, 1)
                        have(f.n)
                        for p in range(PH):
                            ps = fill(f)
                            MM(ps, xt[:, p // 2, :], fc0[:, p % 2 * 512:(p % 2 + 1) * 512], start=True, stop=True).then_inc(filled, 1)

                def rows_transform(f, g):
                    for q in range(0, C, 6):
                        ps = fill(f)
                        for i, c in enumerate(range(q, min(q + 6, C))):
                            mm = MM(ps[:, i * 80:(i + 1) * 80], a[:, g, c:2 * S * C:C], d1[:, :], start=True, stop=True)
                        mm.then_inc(filled, 1)

                def columns_transform(f, g):
                    for b2 in range(2):
                        ps = fill(f)
                        for k in range(KG):
                            for r in range(2):
                                o = (b2 * 2 + r) * 640 + k * 128
                                mm = MM(ps[:, k * 80:(k + 1) * 80], half_t[:, g % 2, o:o + 128], d2[:, r, :], start=r == 0, stop=r == 1)
                        mm.then_inc(filled, 1)

                def mixing(f, r):
                    pe.wait_ge(w_in, 64 * r + 64)
                    for k in range(KG):
                        for y in range(0, MO, 10):
                            ps = fill(f)[:, 0:320].rearrange("p (b y r) -> p b y r", b=16, r=2)
                            for i in range(10):
                                m = k * MO + y + i
                                mm = MM(ps[:, :, i, :], wbd[:, :, m], spec[:, m, :].rearrange("p (b r) -> p b r", r=2), start=True, stop=True)
                            mm.then_inc(filled, 1)

                def turn_mixed(f, g):
                    for k in range(KG):
                        ps = fill(f)
                        for q in range(4):
                            mm = T(ps[0:80, q * 128:(q + 1) * 128], mixed[:, k, g, q // 2, q % 2, :], ident[:, :])
                        mm.then_inc(filled, 1)

                def columns_inverse(f, g):
                    for q in range(0, C, 4):
                        ps = fill(f)
                        for i in range(4):
                            mm = MM(ps[0:80, i * 128:(i + 1) * 128], half_t[0:80, g % 2, q + i:2560:C], e1[:, :], start=True, stop=True)
                        mm.then_inc(filled, 1)

                def turn_activations(f, g, p):
                    ps = fill(f)
                    for m in range(4):
                        o = p * 512 + m * 128
                        mm = T(ps[:, m * 128:(m + 1) * 128], a[:, g, o:o + 128], ident[:, :])
                    mm.then_inc(filled, 1)
                    return f.n

                for half in range(2):
                    at, acc_at = half * HALF_FILLS, half * HALF_ACC
                    if half == 0:
                        pe.sem_inc(drained, RING)
                        pe.sem_inc(acc_read, 2)
                    input_layer(Fills(at), half)
                    at += FC0_FILLS
                    with pe.Fori(0, NL) as l:
                        f = Fills(at, l * LAYER_FILLS)
                        first, acc_base = f.n, acc_at + l * LAYER_ACC
                        pe.wait_ge(acc_read, acc_base + 2)
                        have(f.base + f.n)
                        marks = {}
                        for g in range(NGRP):
                            rows_transform(f, g)
                            marks[g] = f.n
                            if g:
                                have(f.base + marks[g - 1])
                                columns_transform(f, g - 1)
                        have(f.base + marks[NGRP - 1])
                        columns_transform(f, NGRP - 1)
                        have(f.base + f.n)
                        mixing(f, NL * half + l)
                        have(f.base + f.n)
                        turn_mixed(f, 0)
                        for g in range(NGRP):
                            have(f.base + f.n)
                            columns_inverse(f, g)
                            if g + 1 < NGRP:
                                turn_mixed(f, g + 1)
                            chan_at = turn_activations(f, g, 0)
                            for p in range(PH):
                                n = acc_base + g * PH + p
                                nxt = turn_activations(f, g, p + 1) if p + 1 < PH else None
                                have(f.base + chan_at)
                                if g + p == 0:
                                    pe.wait_ge(bias_in, 16 * (NL * half + l) + 16)
                                pe.wait_ge(acc_read, n + 1)
                                MM(acc[:, p % 2, :], e2[0:97, :], u[:, p * 512:(p + 1) * 512], start=True, stop=True, skip_group_check=True)
                                for m in range(4):
                                    mm = MM(acc[:, p % 2, m * 128:(m + 1) * 128], chan[:, p % 2, m * 128:(m + 1) * 128],
                                            cwt[:, bass.ds(l, 1), :].rearrange("p a c -> p (a c)"), start=False, stop=True, skip_group_check=True)
                                mm.then_inc(acc_full, 1)
                                chan_at = nxt
                        assert f.n == first + LAYER_FILLS
                    at += NL * LAYER_FILLS
                    acc_at += NL * LAYER_ACC
                    pe.wait_ge(acc_read, acc_at + 2)
                    f = Fills(at)
                    for g in range(NGRP):
                        for q in range(2):
                            start = f.n
                            turn_activations(f, g, 4 * q)
                            pend = []
                            for p in range(4):
                                if p < 3:
                                    turn_activations(f, g, 4 * q + p + 1)
                                have(start + p + 1)
                                for v in range(2):
                                    n = acc_at + ((g * 2 + q) * 4 + p) * 2 + v
                                    pe.wait_ge(acc_read, n + 1)
                                    MM(acc[:, v, :], fc1[:, v, :], chan[:, p % 2, :], start=True, stop=True).then_inc(acc_full, 1)
                                    pend.append((n, p, v))
                                    if len(pend) == 2:
                                        second_layer(pe, MM, pend.pop(0), start)
                            second_layer(pe, MM, pend.pop(0), start).then_inc(filled, 1)
                            f.next()

            @block.vector
            def _(dve):
                V = nc.vector

                def drain(f):
                    n, bank = f.next()
                    dve.wait_ge(filled, n + 1)
                    return ring[:, bank, :]

                for half in range(2):
                    at = half * HALF_FILLS
                    f = Fills(at)
                    for g in range(NGRP):
                        V.tensor_copy(xt[0:96, :, :].rearrange("p a c -> p (a c)"), drain(f)[0:96, :]).then_inc(drained, 1)
                        for p in range(PH):
                            V.tensor_copy(a[:, g, p * 512:(p + 1) * 512], drain(f)).then_inc(drained, 1)
                    at += FC0_FILLS
                    with dve.Fori(0, NL) as l:
                        f = Fills(at, l * LAYER_FILLS)

                        def rows(g):
                            for q in range(0, C, 6):
                                w = min(6, C - q)
                                src = drain(f)[:, 0:w * 80].rearrange("p (c n) -> p c n", n=80)
                                V.tensor_copy(half_t[:, g % 2, :].rearrange("p (n c) -> p c n", c=C)[:, q:q + w, :], src).then_inc(drained, 1)

                        def columns(g):
                            for b2 in range(2):
                                o = (g * 2 + b2) * 4
                                V.tensor_copy(spec[:, :, o:o + 4], drain(f)[:, 0:400].rearrange("p (m n) -> p m n", n=4)).then_inc(drained, 1)

                        for g in range(NGRP):
                            rows(g)
                            if g:
                                columns(g - 1)
                        columns(NGRP - 1)
                        for k in range(KG):
                            for y in range(0, MO, 10):
                                src = drain(f)[:, 0:320].rearrange("p (n b m) -> p n b m", n=8, b=2)
                                dst = mixed[:, k, :, :, :, :].rearrange("p g b r (c y) -> p (g b) r c y", c=2)
                                V.tensor_copy(dst[:, :, 0, :, 2 * y:2 * y + 20], src)
                                V.tensor_copy(dst[:, :, 1, :, 2 * y:2 * y + 20:2], src[:, :, :, 1:20:2])
                                V.tensor_scalar(dst[:, :, 1, :, 2 * y + 1:2 * y + 20:2], src[:, :, :, 0:20:2], -1.0, None, ALU.mult).then_inc(drained, 1)

                        def turned(g):
                            for k in range(KG):
                                src = drain(f)[0:80, :].rearrange("p (n o) -> p n o", o=C)
                                V.tensor_copy(half_t[0:80, g % 2, :].rearrange("p (n k o) -> p n k o", k=KG, o=C)[:, :, k, :], src).then_inc(drained, 1)

                        turned(0)
                        for g in range(NGRP):
                            for q in range(0, C, 4):
                                src = drain(f)[0:80, :].rearrange("p (o w) -> p o w", o=4)
                                V.tensor_copy(u[0:80, :].rearrange("p (w o) -> p o w", o=C)[:, q:q + 4, :], src).then_inc(drained, 1)
                            if g + 1 < NGRP:
                                turned(g + 1)
                            for p in range(PH):
                                V.tensor_copy(chan[:, p % 2, :], drain(f)).then_inc(drained, 1)
                    at += NL * LAYER_FILLS
                    f = Fills(at)
                    for g in range(NGRP):
                        for q in range(2):
                            for p in range(4):
                                V.tensor_copy(chan[:, p % 2, :], drain(f)).then_inc(drained, 1)
                            n = half * NGRP + g
                            if q == 0 and n >= 1:
                                dve.wait_ge(ho_stored, 32 * n)
                            V.tensor_scalar(ho[:, q, :], drain(f)[:, 0:S], fc2b[:, 0:1], None, ALU.add).then_inc(drained, 1)
                        dve.wait_ge(drained, f.n + RING)
                        V.sem_inc(ho_ready, 1)

            @block.scalar
            def _(act):
                for half in range(2):
                    with act.Fori(0, NL) as l:
                        for g in range(NGRP):
                            for p in range(PH):
                                act.wait_ge(acc_full, half * HALF_ACC + l * LAYER_ACC + g * PH + p + 1)
                                nc.scalar.activation(a[:, g, p * 512:(p + 1) * 512], acc[:, p % 2, :], ACT.Gelu).then_inc(acc_read, 1)
                    for n in range(4 * PH * 2):
                        act.wait_ge(acc_full, half * HALF_ACC + NL * LAYER_ACC + n + 1)
                        nc.scalar.activation(gl[:, n % 2, :], acc[:, n % 2, :], ACT.Gelu, bias=fc1b[:, 0:1]).then_inc(acc_read, 1)


def layernorm_semaphores(nc, ctx):
    return {n: ctx.enter_context(nc.semaphore("ln_" + n))
            for n in ("step", "var_ready", "root_ready", "normed", "turned", "copied_a", "copied_v")}


def layernorm_transposed(nc, sems, turn, H, XN, sq, XT, ident):
    G = 4
    with ExitStack() as ctx:
        st = ctx.enter_context(nc.sbuf_tensor(f"ln_st{turn}", [NT, 8, NB], F32))
        ps = ctx.enter_context(nc.psum_tensor(f"ln_ps{turn}", [DM, 4, 512], F32))
        step, var_ready, root_ready, normed = sems["step"], sems["var_ready"], sems["root_ready"], sems["normed"]
        turned, copied_a, copied_v = sems["turned"], sems["copied_a"], sems["copied_v"]
        LINKS, FILLS, HALF = 10, NB // G, NB // G // 2
        sums, mean, var, root, inv, other = (st[:, i, :] for i in range(6))
        wide = lambda s: bc(s.unsqueeze(2), NT, NB, DM)
        with nc.Block() as block:
            @block.vector
            def _(dve):
                s = Steps(dve, step, turn * LINKS)
                s.link(nc.vector.reduce_sum(sums, H[:, :, :], AX.X))
                s.link(nc.vector.tensor_scalar(mean, sums, 1.0 / DM, None, ALU.mult))
                s.link(nc.vector.tensor_tensor(XN[:, :, :], H[:, :, :], wide(mean), ALU.subtract))
                s.link(nc.vector.tensor_tensor(sq[:, :, :], XN[:, :, :], XN[:, :, :], ALU.mult))
                s.link(nc.vector.reduce_sum(sums, sq[:, :, :], AX.X))
                nc.vector.tensor_scalar(var, sums, 1.0 / DM, EPS, ALU.mult, ALU.add).then_inc(var_ready, 1)
                dve.wait_ge(var_ready, turn + 1)
                dve.wait_ge(root_ready, turn + 1)
                s.link(nc.vector.reciprocal(inv, root))
                s.link(nc.vector.tensor_tensor(other, var, inv, ALU.mult))
                s.link(nc.vector.tensor_tensor(sums, other, root, ALU.add))
                s.link(nc.vector.tensor_scalar(other, sums, 0.5, None, ALU.mult))
                s.link(nc.vector.reciprocal(inv, other))
                nc.vector.tensor_tensor(XN[:, :, :], XN[:, :, :], wide(inv), ALU.mult).then_inc(normed, 1)
                for g in range(1, NB // G, 2):
                    dve.wait_ge(turned, turn * FILLS + g + 1)
                    nc.vector.tensor_copy(XT[:, g * G * NT:(g + 1) * G * NT], ps[:, g % 4, 0:G * NT]).then_inc(copied_v, 1)
                dve.wait_ge(copied_v, (turn + 1) * HALF)
                assert s.n == LINKS

            @block.scalar
            def _(act):
                act.wait_ge(var_ready, turn + 1)
                nc.scalar.activation(root, var, ACT.Sqrt).then_inc(root_ready, 1)
                for g in range(0, NB // G, 2):
                    act.wait_ge(turned, turn * FILLS + g + 1)
                    nc.scalar.activation(XT[:, g * G * NT:(g + 1) * G * NT], ps[:, g % 4, 0:G * NT], ACT.Copy).then_inc(copied_a, 1)
                act.wait_ge(copied_a, (turn + 1) * HALF)

            @block.tensor
            def _(pe):
                pe.wait_ge(normed, turn + 1)
                for g in range(NB // G):
                    if g >= 4:
                        pe.wait_ge(copied_a if g % 2 == 0 else copied_v, turn * HALF + (g - 4) // 2 + 1)
                    for j in range(G):
                        mm = nc.tensor.transpose(ps[:, g % 4, j * NT:(j + 1) * NT], XN[:, g * G + j, :], ident[0:NT, 0:NT])
                    mm.then_inc(turned, 1)


def linear_attention(nc, H, XT, ident, rows_in, Q, E):
    NH = 8
    with ExitStack() as ctx:
        sb = lambda n, sh: ctx.enter_context(nc.sbuf_tensor(n, sh, F32))
        pb = lambda n, sh: ctx.enter_context(nc.psum_tensor(n, sh, F32))
        sem = lambda n: ctx.enter_context(nc.semaphore(n))
        q_w = sb("at_q_w", [DM, NH, DM])
        e_w = sb("at_e_w", [DM, NH, DM])
        e_t = sb("at_e_t", [DM, NH, DM])
        causal = sb("at_causal", [NT, NT])
        s_t = sb("at_s_t", [128, 2, 2, NT])
        xt_2 = sb("at_xt_2", [128, TOK])
        half = sb("at_half", [128, 2])
        es = sb("at_es", [NT, 2, NH * DM])
        qs = sb("at_qs", [128, NH // 2, TOK])
        om = sb("at_om", [NT, 2, NH, NT])
        psE = pb("at_psE", [NT, 2, 512])
        psO = pb("at_psO", [128, 2, 2, 512])
        psR = pb("at_psR", [NT, 2, 512])
        HH = NH // 2 * NT
        PIECES = TOK // 512
        NQS = NH // 2 * PIECES
        loaded, ones, mask_ready = sem("at_loaded"), sem("at_ones"), sem("at_mask_ready")
        e_turned, e_ready = sem("at_e_turned"), sem("at_e_ready")
        staged, es_done, es_ready = sem("at_staged"), sem("at_es_done"), sem("at_es_ready")
        qs_done, qs_act, qs_dve = sem("at_qs_done"), sem("at_qs_act"), sem("at_qs_dve")
        om_done, om_ready, r_done, r_added = sem("at_om_done"), sem("at_om_ready"), sem("at_r_done"), sem("at_r_added")
        bank = lambda n: psO[:, n % 4 // 2, n % 2, :]
        piece = lambda n: qs[:, n // PIECES, n % PIECES * 512:(n % PIECES + 1) * 512]
        with nc.Block() as block:
            @block.sync
            def _(sp):
                sp.dma_start(q_w[:, :, :], Q.rearrange("h i j -> i h j")).then_inc(loaded, 16)
                sp.dma_start(e_w[:, :, :], E.rearrange("h i j -> i h j")).then_inc(loaded, 16)
                for k in range(2):
                    sp.dma_start(xt_2[k * DM:(k + 1) * DM, :], XT[:, :]).then_inc(loaded, 16)
                with nc.allow_non_contiguous_dma(reason="a column"):
                    sp.dma_start(half[:, :], rows_in[:, :, 0:1].rearrange("k a m -> k (a m)")).then_inc(loaded, 16)

            @block.gpsimd
            def _(pool):
                P = nc.gpsimd

                def stage(k, n):
                    P.tensor_tensor(s_t[:, k, :, :], bc(xt_2[:, bass.ds(n * NT, NT)].unsqueeze(1), 128, 2, NT),
                                    bc(half[:, :].unsqueeze(2), 128, 2, NT), ALU.mult).then_inc(staged, 1)

                P.memset(causal[:, :], 1.0).then_inc(ones, 1)
                pool.wait_ge(ones, 1)
                P.affine_select(out=causal[:, :], in_=causal[:, :], compare_op=ALU.is_ge, fill=0.0,
                                base=0, pattern=[[1, NT]], channel_multiplier=-1).then_inc(mask_ready, 1)
                pool.wait_ge(mask_ready, 1)
                pool.wait_ge(loaded, 80)
                for k in range(2):
                    stage(k, k)
                with pool.Fori(0, NB // 2 - 1) as p:
                    for k in range(2):
                        pool.wait_ge(om_done, 2 * p + k + 1)
                        stage(k, 2 * p + 2 + k)

            @block.tensor
            def _(pe):
                MM = nc.tensor.matmul
                pe.sem_inc(r_done, 2)
                pe.wait_ge(loaded, 80)
                for h in range(NH):
                    mm = nc.tensor.transpose(psR[0:DM, 0, h * DM:(h + 1) * DM], e_w[:, h, :], ident[0:DM, 0:DM])
                mm.then_inc(e_turned, 1)
                for n in range(NQS):
                    if n >= 4:
                        pe.wait_ge((qs_act, qs_dve)[n % 2], (n - 4) // 2 + 1)
                    MM(bank(n), q_w[:, n // PIECES * 2:n // PIECES * 2 + 2, :].rearrange("i h j -> i (h j)"), XT[:, n % PIECES * 512:(n % PIECES + 1) * 512],
                       start=True, stop=True).then_inc(qs_done, 1)
                pe.wait_ge(e_ready, 1)
                pe.wait_ge(qs_act, NQS // 2)
                pe.wait_ge(qs_dve, NQS // 2)

                def products(k, n):
                    pe.wait_ge(staged, n + 1)
                    pe.wait_ge(es_ready, n + 1)
                    pe.wait_ge(om_ready, n + 1)
                    MM(psE[:, k, :], s_t[0:DM, k, 0, :], e_t[:, :, :].rearrange("j h i -> j (h i)"), start=True, stop=True).then_inc(es_done, 1)
                    for h2 in range(2):
                        mm = MM(psO[0:NT, k, h2, 0:HH], s_t[:, k, h2, :], qs[:, :, bass.ds(n * NT, NT)], start=True, stop=True)
                    mm.then_inc(om_done, 1)

                def results(k, n):
                    pe.wait_ge(es_ready, n + 3)
                    pe.wait_ge(om_ready, n + 3)
                    pe.wait_ge(r_added, n + 1)
                    for h in range(NH):
                        mm = MM(psR[:, k, 0:DM], om[:, k, h % 2 * (NH // 2) + h // 2, :], es[:, k, h * DM:(h + 1) * DM],
                                start=h == 0, stop=h == NH - 1)
                    mm.then_inc(r_done, 1)

                products(0, 0)
                with pe.Fori(0, NB // 2 - 1) as p:
                    for k in range(2):
                        products(1 - k, 2 * p + k + 1)
                        results(k, 2 * p + k)
                products(1, NB - 1)
                results(0, NB - 2)
                results(1, NB - 1)

            @block.scalar
            def _(act):
                A = nc.scalar.activation
                for n in range(0, NQS, 2):
                    act.wait_ge(qs_done, n + 1)
                    A(piece(n), bank(n), ACT.Copy).then_inc(qs_act, 1)
                act.sem_inc(es_ready, 2)
                with act.Fori(0, NB // 2) as p:
                    for k in range(2):
                        act.wait_ge(es_done, 2 * p + k + 1)
                        act.wait_ge(r_done, 2 * p + k + 1)
                        A(es[:, k, :], psE[:, k, :], ACT.Copy).then_inc(es_ready, 1)

            @block.vector
            def _(dve):
                V = nc.vector
                V.sem_inc(om_ready, 2)
                V.sem_inc(r_added, 2)
                dve.wait_ge(e_turned, 1)
                V.tensor_copy(e_t[:, :, :].rearrange("j h i -> j (h i)"), psR[0:DM, 0, :]).then_inc(e_ready, 1)
                for n in range(1, NQS, 2):
                    dve.wait_ge(qs_done, n + 1)
                    V.tensor_copy(piece(n), bank(n)).then_inc(qs_dve, 1)
                dve.wait_ge(mask_ready, 1)

                def masked(k, n):
                    dve.wait_ge(om_done, n + 1)
                    dve.wait_ge(r_done, n + 1)
                    for h2 in range(2):
                        ins = V.tensor_tensor(om[:, k, 4 * h2:4 * h2 + 4, :], psO[0:NT, k, h2, 0:HH].rearrange("u (h t) -> u h t", h=4),
                                              bc(causal[:, :].unsqueeze(1), NT, 4, NT), ALU.mult)
                    ins.then_inc(om_ready, 1)

                def add(k, n):
                    dve.wait_ge(r_done, n + 3)
                    V.tensor_tensor(H[:, bass.ds(n, 1), :], H[:, bass.ds(n, 1), :], psR[:, k:k + 1, 0:DM], ALU.add).then_inc(r_added, 1)

                masked(0, 0)
                with dve.Fori(0, NB // 2 - 1) as p:
                    for k in range(2):
                        masked(1 - k, 2 * p + k + 1)
                        add(k, 2 * p + k)
                masked(1, NB - 1)
                add(0, NB - 2)
                add(1, NB - 1)
                dve.wait_ge(r_added, NB + 2)


def top_two_experts(nc, H, XT, router_w1, router_b1, router_w2, router_b2, w1, b1, w2, b2, w3, b3):
    NE, RH, NP = 6, 32, 3
    G = 4
    N = G * NT
    NG = NB // G
    with ExitStack() as ctx:
        sb = lambda n, sh: ctx.enter_context(nc.sbuf_tensor("ff_" + n, sh, F32))
        pb = lambda n, sh: ctx.enter_context(nc.psum_tensor("ff_" + n, sh, F32))
        sem = lambda n: ctx.enter_context(nc.semaphore("ff_" + n))
        rw1, rb1, rw2, rb2 = sb("rw1", [DM, RH]), sb("rb1", [RH, 1]), sb("rw2", [RH, NE]), sb("rb2", [NT, NE])
        w1s = sb("w1s", [DM, NE, DM])
        w2s = sb("w2s", [128, NP, 128])
        w3s = sb("w3s", [128, NP, 128])
        b1s, b2s = sb("b1s", [128, NP]), sb("b2s", [128, NP])
        b3s = sb("b3s", [NT, NE * DM])
        prio = sb("prio", [NT, NE])
        rh = sb("rh", [RH, 2, N])
        pr = sb("pr", [NT, NB, NE])
        first = sb("first", [NT, NB, NE])
        second = sb("second", [NT, NB, NE])
        score = sb("score", [NT, NB, NE])
        mx = sb("mx", [NT, 4, NB])
        mix = sb("mix", [NT, NB, NE])
        h1 = sb("h1", [128, NP, N])
        h2 = sb("h2", [128, 2, NP, N])
        eo = sb("eo", [NT, 2, NE * DM])
        ew = sb("ew", [NT, 2, NE * DM])
        es = sb("es", [NT, 2, DM])
        psA = pb("psA", [128, 3, 512])
        psB = pb("psB", [128, 3, 512])
        psC = pb("psC", [NT, 2, 512])
        loaded, blocks_zero, prio_ready = sem("loaded"), sem("blocks_zero"), sem("prio_ready")
        diag_loaded = sem("diag_loaded")
        rh_done, rh_ready, lg_done, lg_ready = sem("rh_done"), sem("rh_ready"), sem("lg_done"), sem("lg_ready")
        centred, exp_ready, gap_ready, ratio_ready = sem("centred"), sem("exp_ready"), sem("gap_ready"), sem("ratio_ready")
        step = sem("step")
        h1_done, h1_ready, h2_done, h2_ready = sem("h1_done"), sem("h1_ready"), sem("h2_done"), sem("h2_ready")
        eo_done, eo_read, added, vstep = sem("eo_done"), sem("eo_read"), sem("added"), sem("vstep")
        staged = sem("staged")
        xs = sb("xs", [DM, N])
        lg = psC[:, 0, 0:NB * NE].rearrange("t (b e) -> t b e", e=NE)
        with nc.Block() as block:
            @block.sync
            def _(sp):
                with nc.allow_non_contiguous_dma(reason="small weights"):
                    sp.dma_start(rw1[:, :], router_w1).then_inc(loaded, 16)
                    sp.dma_start(rb1[:, :], router_b1.rearrange("(k a) -> k a", a=1)).then_inc(loaded, 16)
                    sp.dma_start(rw2[:, :], router_w2).then_inc(loaded, 16)
                    sp.dma_start(rb2[:, :], router_b2.rearrange("(a k) -> a k", a=1).broadcast_to([NT, NE])).then_inc(loaded, 16)
                    sp.dma_start(w1s[:, :, :], w1.rearrange("e d h -> d e h")).then_inc(loaded, 16)
                    sp.dma_start(b1s[:, :], b1.rearrange("(p e) h -> (e h) p", e=2)).then_inc(loaded, 16)
                    sp.dma_start(b2s[:, :], b2.rearrange("(p e) h -> (e h) p", e=2)).then_inc(loaded, 16)
                    sp.dma_start(b3s[:, :], b3.rearrange("(a e) d -> a (e d)", a=1).broadcast_to([NT, NE * DM])).then_inc(loaded, 16)
                    sp.wait_ge(blocks_zero, 2)
                    for dst, src in ((w2s, w2), (w3s, w3)):
                        for e in range(2):
                            sp.dma_start(dst[e * DM:(e + 1) * DM, :, e * DM:(e + 1) * DM],
                                         src.rearrange("(p e) h f -> e h p f", e=2)[e]).then_inc(diag_loaded, 16)

            @block.gpsimd
            def _(pool):
                nc.gpsimd.memset(w2s[:, :, :], 0.0).then_inc(blocks_zero, 1)
                nc.gpsimd.memset(w3s[:, :, :], 0.0).then_inc(blocks_zero, 1)
                for e in range(NE):
                    ins = nc.gpsimd.memset(prio[:, e:e + 1], float(NE - e))
                ins.then_inc(prio_ready, 1)
                nc.gpsimd.tensor_copy(xs[:, :], XT[:, 0:N]).then_inc(staged, 1)
                with pool.Fori(1, NG) as g:
                    pool.wait_ge(h1_done, NP * g)
                    nc.gpsimd.tensor_copy(xs[:, :], XT[:, bass.ds(g * N, N)]).then_inc(staged, 1)

            @block.tensor
            def _(pe):
                pe.wait_ge(loaded, 8 * 16)
                for g in range(NG):
                    if g >= 2:
                        pe.wait_ge(rh_ready, g - 1)
                    nc.tensor.matmul(psA[0:RH, g % 2, 0:N], rw1[:, :], XT[:, g * N:(g + 1) * N], start=True, stop=True).then_inc(rh_done, 1)
                    pe.wait_ge(rh_ready, g + 1)
                    for j in range(G):
                        b = g * G + j
                        mm = nc.tensor.matmul(psC[:, 0, b * NE:(b + 1) * NE], rh[:, g % 2, j * NT:(j + 1) * NT], rw2[:, :], start=True, stop=True)
                    mm.then_inc(lg_done, 1)
                pe.wait_ge(diag_loaded, 4 * 16)
                pe.wait_ge(lg_ready, 1)

                with pe.Fori(0, NG) as g:
                    pe.wait_ge(staged, g + 1)
                    for p in range(NP):
                        nc.tensor.matmul(psA[:, p, 0:N], w1s[:, 2 * p:2 * p + 2, :].rearrange("d e h -> d (e h)"), xs[:, :],
                                         start=True, stop=True).then_inc(h1_done, 1)
                    for p in range(NP):
                        pe.wait_ge(h1_ready, NP * g + p + 1)
                        nc.tensor.matmul(psB[:, p, 0:N], w2s[:, p, :], h1[:, p, :], start=True, stop=True).then_inc(h2_done, 1)
                    pe.wait_ge(h2_ready, NP * g + NP)
                    for j in range(G):
                        pe.wait_ge(eo_read, G * g + j + 1)
                        for p in range(NP):
                            mm = nc.tensor.matmul(psC[:, j % 2, p * 128:(p + 1) * 128], h2[:, 0, p, j * NT:(j + 1) * NT], w3s[:, p, :], start=True, stop=True)
                        mm.then_inc(eo_done, 1)

            @block.scalar
            def _(act):
                act.wait_ge(loaded, 8 * 16)
                for g in range(NG):
                    act.wait_ge(rh_done, g + 1)
                    if g >= 2:
                        act.wait_ge(lg_done, g - 1)
                    nc.scalar.activation(rh[:, g % 2, :], psA[0:RH, g % 2, 0:N], ACT.Relu, bias=rb1[:, 0:1]).then_inc(rh_ready, 1)
                act.wait_ge(centred, 1)
                nc.scalar.activation(pr[:, :, :], pr[:, :, :], ACT.Exp).then_inc(exp_ready, 1)
                act.wait_ge(gap_ready, 1)
                nc.scalar.activation(mx[:, 1, :], mx[:, 1, :], ACT.Exp).then_inc(ratio_ready, 1)
                with act.Fori(0, NG) as g:
                    for p in range(NP):
                        act.wait_ge(h1_done, NP * g + p + 1)
                        nc.scalar.activation(h1[:, p, :], psA[:, p, 0:N], ACT.Relu, bias=b1s[:, p:p + 1]).then_inc(h1_ready, 1)
                    for p in range(NP):
                        act.wait_ge(h2_done, NP * g + p + 1)
                        ins = nc.scalar.activation(h2[:, 0, p, :], psB[:, p, 0:N], ACT.Relu, bias=b2s[:, p:p + 1])
                        ins.then_inc(h2_ready, 1)

            @block.vector
            def _(dve):
                s = Steps(dve, step)
                V = nc.vector
                wide = lambda m: bc(m.unsqueeze(2), NT, NB, NE)
                across = lambda m: bc(m.unsqueeze(1), NT, NB, NE)
                dve.wait_ge(lg_done, NG)
                dve.wait_ge(loaded, 8 * 16)
                V.tensor_tensor(pr[:, :, :], lg, across(rb2[:, :]), ALU.add).then_inc(lg_ready, 1)
                dve.wait_ge(lg_ready, 1)
                s.link(V.reduce_max(mx[:, 0, :], pr[:, :, :], AX.X))
                V.tensor_tensor(pr[:, :, :], pr[:, :, :], wide(mx[:, 0, :]), ALU.subtract).then_inc(centred, 1)
                dve.wait_ge(exp_ready, 1)
                s.link(V.reduce_sum(mx[:, 0, :], pr[:, :, :], AX.X))
                s.link(V.reciprocal(mx[:, 1, :], mx[:, 0, :]))
                s.link(V.tensor_tensor(pr[:, :, :], pr[:, :, :], wide(mx[:, 1, :]), ALU.mult))
                dve.wait_ge(prio_ready, 1)

                def pick(chosen, best, probs):
                    s.link(V.reduce_max(best, probs, AX.X))
                    s.link(V.tensor_tensor(score[:, :, :], probs, wide(best), ALU.is_equal))
                    s.link(V.tensor_tensor(score[:, :, :], score[:, :, :], across(prio[:, :]), ALU.mult))
                    s.link(V.reduce_max(mx[:, 3, :], score[:, :, :], AX.X))
                    s.link(V.tensor_tensor(chosen, score[:, :, :], wide(mx[:, 3, :]), ALU.is_equal))

                pick(first[:, :, :], mx[:, 0, :], pr[:, :, :])
                s.link(V.scalar_tensor_tensor(pr[:, :, :], first[:, :, :], -2.0, pr[:, :, :], ALU.mult, ALU.add))
                pick(second[:, :, :], mx[:, 1, :], pr[:, :, :])
                V.tensor_tensor(mx[:, 1, :], mx[:, 1, :], mx[:, 0, :], ALU.subtract).then_inc(gap_ready, 1)
                dve.wait_ge(ratio_ready, 1)
                s.link(V.tensor_scalar(mx[:, 0, :], mx[:, 1, :], 1.0, None, ALU.add))
                s.link(V.reciprocal(mx[:, 2, :], mx[:, 0, :]))
                s.link(V.tensor_tensor(mx[:, 3, :], mx[:, 2, :], mx[:, 1, :], ALU.mult))
                s.link(V.tensor_tensor(first[:, :, :], first[:, :, :], wide(mx[:, 2, :]), ALU.mult))
                s.link(V.tensor_tensor(second[:, :, :], second[:, :, :], wide(mx[:, 3, :]), ALU.mult))
                s.link(V.tensor_tensor(mix[:, :, :], first[:, :, :], second[:, :, :], ALU.add))
                V.sem_inc(eo_read, 2)
                with dve.Fori(0, NG) as g:
                    t = Steps(dve, vstep, g * (3 * G))
                    for j in range(G):
                        b, k = g * G + j, j % 2
                        dve.wait_ge(eo_done, G * g + j + 1)
                        V.tensor_tensor(eo[:, k, :], psC[:, k, 0:NE * DM], b3s[:, :], ALU.add).then_inc(eo_read, 1)
                        dve.wait_ge(eo_read, G * g + j + 3)
                        t.link(V.tensor_tensor(ew[:, k, :].rearrange("t (e d) -> t e d", e=NE), eo[:, k, :].rearrange("t (e d) -> t e d", e=NE),
                                               bc(mix[:, bass.ds(b, 1), :].rearrange("t a e -> t (a e)").unsqueeze(2), NT, NE, DM), ALU.mult))
                        t.link(V.reduce_sum(es[:, k, :], ew[:, k, :].rearrange("t (e d) -> t d e", e=NE), AX.X))
                        t.link(V.tensor_tensor(H[:, bass.ds(b, 1), :], H[:, bass.ds(b, 1), :], es[:, k:k + 1, :], ALU.add))


def best_expert(nc, H, XT, ident, gate_w, gate_b, w1, b1, w2, b2):
    NE, F = 8, 256
    CAP = -(-5 * TOK // (4 * NE))
    KT = F // 128
    G = 4
    N = G * NT
    NG = NB // G
    with ExitStack() as ctx:
        sb = lambda n, sh: ctx.enter_context(nc.sbuf_tensor("sw_" + n, sh, F32))
        pb = lambda n, sh: ctx.enter_context(nc.psum_tensor("sw_" + n, sh, F32))
        sem = lambda n: ctx.enter_context(nc.semaphore("sw_" + n))
        gw, gb = sb("gw", [DM, NE]), sb("gb", [NT, NE])
        w1s = sb("w1s", [DM, NE, F])
        b1s = sb("b1s", [128, NE, KT])
        w2s = sb("w2s", [128, NE, KT, DM])
        b2s = sb("b2s", [NT, NE * DM])
        prio = sb("prio", [NT, NE])
        pr, score, chosen = sb("pr", [NT, NB, NE]), sb("score", [NT, NB, NE]), sb("chosen", [NT, NB, NE])
        mx = sb("mx", [NT, 4, NB])
        chT = sb("chT", [NE, TOK])
        ones = sb("ones", [NE, TOK])
        count = sb("count", [NE, TOK])
        gate = sb("gate", [NT, NB, NE])
        hid = sb("hid", [128, NE, KT, N])
        eo = sb("eo", [NT, 2, NE * DM])
        ew = sb("ew", [NT, 2, NE * DM])
        es = sb("es", [NT, 2, DM])
        fix = sb("fix", [NT, NB, DM])
        flag = ctx.enter_context(nc.sbuf_tensor("sw_flag", [NT, NB, DM], mybir.dt.uint32))
        const = sb("const", [NT, 3])
        staged = sem("staged")
        xs = sb("xs", [DM, N])
        psA = pb("psA", [128, 4, 512])
        psC = pb("psC", [NT, 2, 512])
        loaded, prio_ready, lg_done, lg_ready = sem("loaded"), sem("prio_ready"), sem("lg_done"), sem("lg_ready")
        centred, exp_ready, step = sem("centred"), sem("exp_ready"), sem("step")
        ch_ready, turned, taken, counted, back, gate_ready = sem("ch_ready"), sem("turned"), sem("taken"), sem("counted"), sem("back"), sem("gate_ready")
        hid_done, hid_a, hid_v = sem("hid_done"), sem("hid_a"), sem("hid_v")
        eo_done, eo_read, vstep = sem("eo_done"), sem("eo_read"), sem("vstep")
        lg = psC[:, 0, 0:NB * NE].rearrange("t (b e) -> t b e", e=NE)
        back_ps = psC[:, 1, 0:NB * NE].rearrange("t (b e) -> t b e", e=NE)
        with nc.Block() as block:
            @block.sync
            def _(sp):
                with nc.allow_non_contiguous_dma(reason="small weights"):
                    sp.dma_start(gw[:, :], gate_w).then_inc(loaded, 16)
                    sp.dma_start(gb[:, :], gate_b.rearrange("(a k) -> a k", a=1).broadcast_to([NT, NE])).then_inc(loaded, 16)
                    sp.dma_start(w1s[:, :, :], w1.rearrange("e d f -> d e f")).then_inc(loaded, 16)
                    sp.dma_start(b1s[:, :, :], b1.rearrange("e (k p) -> p e k", p=128)).then_inc(loaded, 16)
                    for k in range(KT):
                        sp.dma_start(w2s[:, :, k, :], w2[:, k * 128:(k + 1) * 128, :].rearrange("e p d -> p e d")).then_inc(loaded, 16)
                    sp.dma_start(b2s[:, :], b2.rearrange("(a e) d -> a (e d)", a=1).broadcast_to([NT, NE * DM])).then_inc(loaded, 16)
            LOADED = 7 * 16

            @block.gpsimd
            def _(pool):
                for e in range(NE):
                    nc.gpsimd.memset(prio[:, e:e + 1], float(NE - e))
                nc.gpsimd.memset(const[:, 0:1], 0.0)
                nc.gpsimd.memset(const[:, 1:2], 10000.0)
                nc.gpsimd.memset(const[:, 2:3], -10000.0)
                nc.gpsimd.memset(ones[:, :], 1.0).then_inc(prio_ready, 1)
                nc.gpsimd.tensor_copy(xs[:, :], XT[:, 0:N]).then_inc(staged, 1)
                with pool.Fori(1, NG) as g:
                    pool.wait_ge(hid_done, NE * KT * g)
                    nc.gpsimd.tensor_copy(xs[:, :], XT[:, bass.ds(g * N, N)]).then_inc(staged, 1)

            @block.tensor
            def _(pe):
                pe.wait_ge(loaded, LOADED)
                for b in range(NB):
                    mm = nc.tensor.matmul(lg[:, b, :], XT[:, b * NT:(b + 1) * NT], gw[:, :], start=True, stop=True)
                mm.then_inc(lg_done, 1)
                pe.wait_ge(ch_ready, 1)
                for g in range(NG):
                    if g >= 4:
                        pe.wait_ge(taken, g - 3)
                    for j in range(G):
                        mm = nc.tensor.transpose(psA[0:NE, g % 4, j * NT:(j + 1) * NT], chosen[:, g * G + j, :], ident[0:NT, 0:NT])
                    mm.then_inc(turned, 1)
                pe.wait_ge(counted, 1)
                for b in range(NB):
                    mm = nc.tensor.transpose(back_ps[:, b, :], chT[:, b * NT:(b + 1) * NT], ident[0:NE, 0:NE])
                mm.then_inc(back, 1)
                pe.wait_ge(gate_ready, 1)
                pe.sem_inc(eo_done, 1)

                with pe.Fori(0, NG) as g:
                    pe.wait_ge(staged, g + 1)
                    for e in range(NE):
                        for k in range(KT):
                            n = e * KT + k
                            if n >= 4:
                                pe.wait_ge(hid_a if n % 2 == 0 else hid_v, (NE * KT // 2) * g + (n - 4) // 2 + 1)
                            nc.tensor.matmul(psA[:, n % 4, 0:N], w1s[:, e, k * 128:(k + 1) * 128], xs[:, :],
                                             start=True, stop=True).then_inc(hid_done, 1)
                    pe.wait_ge(hid_a, (NE * KT // 2) * (g + 1))
                    pe.wait_ge(hid_v, (NE * KT // 2) * (g + 1))
                    for j in range(G):
                        pe.wait_ge(eo_read, G * g + j + 1)
                        for e in range(NE):
                            for k in range(KT):
                                mm = nc.tensor.matmul(psC[:, j % 2, e * DM:(e + 1) * DM], hid[:, e, k, j * NT:(j + 1) * NT], w2s[:, e, k, :],
                                                      start=k == 0, stop=k == KT - 1)
                        mm.then_inc(eo_done, 1)

            @block.scalar
            def _(act):
                act.wait_ge(loaded, LOADED)
                act.wait_ge(centred, 1)
                nc.scalar.activation(pr[:, :, :], pr[:, :, :], ACT.Exp).then_inc(exp_ready, 1)
                with act.Fori(0, NG) as g:
                    for n in range(0, NE * KT, 2):
                        if n == 0:
                            act.wait_ge(eo_done, G * g + 1)
                        act.wait_ge(hid_done, NE * KT * g + n + 1)
                        nc.scalar.activation(hid[:, n // KT, n % KT, :], psA[:, n % 4, 0:N], ACT.Relu, bias=b1s[:, n // KT, n % KT:n % KT + 1]).then_inc(hid_a, 1)

            @block.vector
            def _(dve):
                s = Steps(dve, step)
                V = nc.vector
                wide = lambda m: bc(m.unsqueeze(2), NT, NB, NE)
                across = lambda m: bc(m.unsqueeze(1), NT, NB, NE)
                dve.wait_ge(lg_done, 1)
                dve.wait_ge(loaded, LOADED)
                dve.wait_ge(prio_ready, 1)
                V.tensor_tensor(pr[:, :, :], lg, across(gb[:, :]), ALU.add).then_inc(lg_ready, 1)
                dve.wait_ge(lg_ready, 1)
                s.link(V.reduce_max(mx[:, 0, :], pr[:, :, :], AX.X))
                V.tensor_tensor(pr[:, :, :], pr[:, :, :], wide(mx[:, 0, :]), ALU.subtract).then_inc(centred, 1)
                dve.wait_ge(exp_ready, 1)
                s.link(V.reduce_sum(mx[:, 0, :], pr[:, :, :], AX.X))
                s.link(V.reciprocal(mx[:, 1, :], mx[:, 0, :]))
                s.link(V.tensor_tensor(pr[:, :, :], pr[:, :, :], wide(mx[:, 1, :]), ALU.mult))
                s.link(V.reduce_max(mx[:, 2, :], pr[:, :, :], AX.X))
                s.link(V.tensor_tensor(score[:, :, :], pr[:, :, :], wide(mx[:, 2, :]), ALU.is_equal))
                s.link(V.tensor_tensor(score[:, :, :], score[:, :, :], across(prio[:, :]), ALU.mult))
                s.link(V.reduce_max(mx[:, 3, :], score[:, :, :], AX.X))
                V.tensor_tensor(chosen[:, :, :], score[:, :, :], wide(mx[:, 3, :]), ALU.is_equal).then_inc(ch_ready, 1)
                for g in range(NG):
                    dve.wait_ge(turned, g + 1)
                    V.tensor_copy(chT[:, g * N:(g + 1) * N], psA[0:NE, g % 4, 0:N]).then_inc(taken, 1)
                dve.wait_ge(taken, NG)
                s.link(V.tensor_tensor_scan(count[:, :], ones[:, :], chT[:, :], 0.0, ALU.mult, ALU.add))
                s.link(V.tensor_scalar(count[:, :], count[:, :], float(CAP), None, ALU.is_le))
                V.tensor_tensor(chT[:, :], chT[:, :], count[:, :], ALU.mult).then_inc(counted, 1)
                dve.wait_ge(back, 1)
                V.tensor_tensor(gate[:, :, :], back_ps, wide(mx[:, 2, :]), ALU.mult).then_inc(gate_ready, 1)
                dve.wait_ge(gate_ready, 1)
                V.sem_inc(eo_read, 2)
                with dve.Fori(0, NG) as g:
                    t = Steps(dve, vstep, g * (2 * G))
                    for n in range(1, NE * KT, 2):
                        if n == 1:
                            dve.wait_ge(eo_done, G * g + 1)
                        dve.wait_ge(hid_done, NE * KT * g + n + 1)
                        V.tensor_scalar(hid[:, n // KT, n % KT, :], psA[:, n % 4, 0:N], b1s[:, n // KT, n % KT:n % KT + 1], 0.0, ALU.add, ALU.max).then_inc(hid_v, 1)
                    for j in range(G):
                        b, k = g * G + j, j % 2
                        dve.wait_ge(eo_done, G * g + j + 2)
                        V.tensor_tensor(eo[:, k, :], psC[:, k, :], b2s[:, :], ALU.add).then_inc(eo_read, 1)
                        dve.wait_ge(eo_read, G * g + j + 3)
                        t.link(V.tensor_tensor(ew[:, k, :].rearrange("t (e d) -> t e d", e=NE), eo[:, k, :].rearrange("t (e d) -> t e d", e=NE),
                                               bc(gate[:, bass.ds(b, 1), :].rearrange("t a e -> t (a e)").unsqueeze(2), NT, NE, DM), ALU.mult))
                        t.link(V.reduce_sum(fix[:, bass.ds(b, 1), :].rearrange("t a d -> t (a d)"), ew[:, k, :].rearrange("t (e d) -> t d e", e=NE), AX.X))
                BIG = 3.4028234663852886e38
                whole = lambda i: bc(const[:, i:i + 1].unsqueeze(2), NT, NB, DM)
                s.link(V.tensor_tensor(flag[:, :, :], fix[:, :, :], fix[:, :, :], ALU.not_equal))
                s.link(V.copy_predicated(fix[:, :, :], flag[:, :, :], whole(0)))
                s.link(V.tensor_scalar(flag[:, :, :], fix[:, :, :], BIG, None, ALU.is_gt))
                s.link(V.copy_predicated(fix[:, :, :], flag[:, :, :], whole(1)))
                s.link(V.tensor_scalar(flag[:, :, :], fix[:, :, :], -BIG, None, ALU.is_lt))
                s.link(V.copy_predicated(fix[:, :, :], flag[:, :, :], whole(2)))
                s.link(V.tensor_tensor(H[:, :, :], H[:, :, :], fix[:, :, :], ALU.add))


FH = 256
NC = 16
NCH = NT // NC
QB = 8
HB = NB // 2


def memory_tensors(nc, ctx):
    sb = lambda n, sh: ctx.enter_context(nc.sbuf_tensor("mem_" + n, sh, F32))
    dr = lambda n, sh: nc.dram_tensor("mem_" + n + "_dram", sh, F32).ap()
    return dict(
        a0=sb("a0", [DM, FH]),
        b0=sb("b0", [128, 2, 2, 128]),
        b0t=sb("b0t", [128, FH]),
        z_base=sb("z_base", [128, 2, NB, NT]),
        w_bs=sb("w_bs", [128, NCH - 1, 4, NT]), g_bs=sb("g_bs", [128, NCH - 1, 4, NT]),
        c_f=sb("c_f", [128, NB, NT]),
        v_y=sb("v_y", [128, HB, NT]),
        w_rows=dr("w_rows", [NT, NCH, NB, NC]),
        g_rows=dr("g_rows", [NT, NCH, NB, NC]),
        w_t=dr("w_t", [NT, TOK]),
        k_t=dr("k_t", [DM, TOK]), q_t=dr("q_t", [DM, TOK]), qc_t=dr("qc_t", [DM, TOK]),
        hist_h=dr("hist_h", [128, 2, NCH, NB, NC]), hist_dz=dr("hist_dz", [128, 2, NCH, NB, NC]),
        h=dr("h", [NT, NB, DM]),
        c_now=dr("c_now", [128, TOK]),
    )


def memory_setup(nc, M, H, XT, ident, inject, W_fused, W0, W1, P0, P1):
    NQ = 3 * DM
    G = 4
    N = G * NT
    NG = NB // G
    with ExitStack() as ctx:
        sb = lambda n, sh: ctx.enter_context(nc.sbuf_tensor("ms_" + n, sh, F32))
        pb = lambda n, sh: ctx.enter_context(nc.psum_tensor("ms_" + n, sh, F32))
        sem = lambda n: ctx.enter_context(nc.semaphore("ms_" + n))
        wf = sb("wf", [128, 2, DM])
        wft = sb("wft", [DM, 2, 128])
        gcol = sb("gcol", [DM, 3, 128])
        p0, w1, p1 = sb("p0", [DM, FH]), sb("w1", [128, 2, DM]), sb("p1", [128, 2, DM])
        fp = sb("fp", [NT, NB, NQ])
        sg = sb("sg", [NT, 2, 2, NQ])
        nrm = sb("nrm", [NT, 4, 2 * NB])
        keep, eta, theta, work = sb("keep", [128, NB, NT]), sb("eta", [128, NB, NT]), sb("theta", [128, NB, NT]), sb("work", [128, NB, NT])
        diag = sb("diag", [NT, NT])
        vv = sb("vv", [NT, HB, 128])
        kT, qT = sb("kT", [DM, TOK]), sb("qT", [DM, TOK])
        psG, psF, psT = pb("psG", [128, 2, 512]), pb("psF", [NT, 2, 512]), pb("psT", [128, 4, 512])
        flat = lambda t: t[:, :, :].rearrange("p b t -> p (b t)")
        loaded, turned, taken = sem("loaded"), sem("turned"), sem("taken")
        k_stored = sem("k_stored")
        step, zeroed = sem("step"), sem("zeroed")
        fp_ready = sem("fp_ready")
        gram_read, stored = sem("gram_read"), sem("stored")
        act_done, pe_done = sem("act_done"), sem("pe_done")
        GATES = 3 * 6
        ROOT = GATES + NB // 2 + 1
        made = sem("made")
        MADE = {n: i + 1 for i, n in enumerate(("b0", "wft", "sq", "kq", "w", "c", "wt", "kt", "rows", "qc", "g", "base"))}
        bs_turned, bs_ready = sem("bs_turned"), sem("bs_ready")
        by_chunk = lambda x: flat(x)[0:NT].rearrange("t (c b s) -> t b c s", c=NCH, s=NC)
        with nc.Block() as block:
            @block.sync
            def _(sp):
                sp.dma_start(M["h"], H[0:NT, :, :]).then_inc(stored, 16)
                sp.dma_start(diag[:, :], inject).then_inc(loaded, 16)
                sp.dma_start(wf[:, 0, :], W_fused[0:128, :]).then_inc(loaded, 16)
                sp.dma_start(wf[0:NQ + 3 - 128, 1, :], W_fused[128:NQ + 3, :]).then_inc(loaded, 16)
                sp.dma_start(M["a0"][:, :], W0).then_inc(loaded, 16)
                sp.dma_start(p0[:, :], P0).then_inc(loaded, 16)
                sp.dma_start(w1[:, :, :], W1.rearrange("(k p) d -> p k d", p=128)).then_inc(loaded, 16)
                sp.dma_start(p1[:, :, :], P1.rearrange("(k p) d -> p k d", p=128)).then_inc(loaded, 16)
                sp.wait_ge(made, MADE["wt"])
                sp.dma_start(M["w_t"], flat(work)[0:NT]).then_inc(stored, 16)
                sp.wait_ge(made, MADE["kt"])
                sp.dma_start(M["k_t"], kT[:, :]).then_inc(k_stored, 16)
                sp.dma_start(M["q_t"], qT[:, :]).then_inc(stored, 16)
                sp.wait_ge(made, MADE["rows"])
                sp.dma_start(M["w_rows"].rearrange("t c b s -> t (c b s)"), flat(eta)[0:NT]).then_inc(stored, 16)
                sp.wait_ge(made, MADE["c"])
                sp.dma_start(M["c_now"], flat(keep)).then_inc(stored, 16)
                sp.wait_ge(made, MADE["qc"])
                sp.dma_start(M["qc_t"], fp[0:DM, 0:16, :].rearrange("p a c -> p (a c)")).then_inc(stored, 16)
                sp.wait_ge(made, MADE["g"])
                sp.dma_start(M["g_rows"].rearrange("t c b s -> t (c b s)"), flat(theta)[0:NT]).then_inc(stored, 16)
                sp.wait_ge(stored, 16 * 7)
                sp.wait_ge(k_stored, 16)

            @block.gpsimd
            def _(pool):
                nc.gpsimd.memset(M["b0"][:, :, :, :], 0.0).then_inc(zeroed, 1)

            @block.tensor
            def _(pe):
                T, MM = nc.tensor.transpose, nc.tensor.matmul
                pe.wait_ge(loaded, 7 * 16)
                T(psT[0:DM, 0, 0:128], wf[:, 0, :], ident[:, :])
                T(psT[0:DM, 0, 128:128 + NQ + 3 - 128], wf[0:NQ + 3 - 128, 1, :], ident[0:NQ + 3 - 128, 0:NQ + 3 - 128]).then_inc(turned, 1)
                pe.wait_ge(made, MADE["b0"])
                for b2 in range(2):
                    for k in range(2):
                        mm = T(psT[:, 1, (2 * b2 + k) * 128:(2 * b2 + k + 1) * 128], M["b0"][:, k, b2, :], ident[:, :])
                mm.then_inc(turned, 1)
                pe.wait_ge(made, MADE["wft"])
                for j in range(3 * 6):
                    if j >= 2:
                        pe.wait_ge(act_done, j - 1)
                    MM(psG[:, j % 2, :], gcol[:, j // 6, :], XT[:, j % 6 * 512:(j % 6 + 1) * 512], start=True, stop=True).then_inc(pe_done, 1)
                for j in range(NB // 2):
                    if j >= 2:
                        pe.wait_ge(fp_ready, j - 1)
                    for i in range(2):
                        b = 2 * j + i
                        mm = MM(psF[:, j % 2, i * NQ:(i + 1) * NQ], XT[:, b * NT:(b + 1) * NT], wft[:, :, :].rearrange("d a c -> d (a c)")[:, 0:NQ], start=True, stop=True)
                    mm.then_inc(pe_done, 1)
                pe.wait_ge(made, MADE["kq"])
                n = 2
                for what in range(4):
                    if what == 3:
                        pe.wait_ge(made, MADE["w"])
                    for g in range(NG if what != 2 else NG // 2):
                        pe.wait_ge(taken, n - 5) if n >= 6 else None
                        for j in range(G):
                            b = g * G + j
                            if what < 2:
                                mm = T(psT[0:DM, n % 4, j * NT:(j + 1) * NT], fp[:, b, (1 - what) * DM:(2 - what) * DM], ident[0:NT, 0:NT])
                            elif what == 2:
                                mm = T(psT[:, n % 4, j * NT:(j + 1) * NT], vv[:, b, :], ident[0:NT, 0:NT])
                            else:
                                mm = T(psT[0:NT, n % 4, j * NT:(j + 1) * NT], theta[0:NT, b, :], ident[0:NT, 0:NT])
                        mm.then_inc(turned, 1)
                        n += 1
                pe.wait_ge(taken, n - 2)
                for g in range(NG):
                    if g >= 4:
                        pe.wait_ge(gram_read, g - 3)
                    for j in range(G):
                        b = g * G + j
                        mm = MM(psT[0:NT, g % 4, j * NT:(j + 1) * NT], kT[:, b * NT:(b + 1) * NT], kT[:, b * NT:(b + 1) * NT], start=True, stop=True)
                    mm.then_inc(pe_done, 1)
                pe.wait_ge(made, MADE["g"])
                for m in range(2 * (NCH - 1)):
                    if m >= 4:
                        pe.wait_ge(bs_ready, m - 3)
                    for q in range(4):
                        o = (m // 2 * NB + q * QB) * NC
                        mm = T(psT[:, m % 4, q * NT:(q + 1) * NT], flat((eta, theta)[m % 2])[0:NT, o:o + 128], ident[0:NT, 0:NT])
                    mm.then_inc(bs_turned, 1)
                pe.wait_ge(made, MADE["base"])
                for j in range(12):
                    if j >= 2:
                        pe.wait_ge(act_done, ROOT + j - 1)
                    MM(psG[:, j % 2, :], M["a0"][:, j // 6 * 128:(j // 6 + 1) * 128], kT[:, j % 6 * 512:(j % 6 + 1) * 512], start=True, stop=True).then_inc(pe_done, 1)

            @block.scalar
            def _(act):
                A = nc.scalar.activation
                for j in range(3 * 6):
                    act.wait_ge(pe_done, j + 1)
                    A(flat((keep, theta, eta)[j // 6])[:, j % 6 * 512:(j % 6 + 1) * 512], psG[:, j % 2, :], ACT.Sigmoid,
                      scale=(-1.0 if j < 6 else 1.0)).then_inc(act_done, 1)
                for j in range(NB // 2):
                    act.wait_ge(pe_done, GATES + j + 1)
                    if j >= 2:
                        act.wait_ge(fp_ready, j - 1)
                    A(sg[:, j % 2, :, :].rearrange("t a c -> t (a c)"), psF[:, j % 2, 0:2 * NQ], ACT.Sigmoid).then_inc(act_done, 1)
                act.wait_ge(made, MADE["sq"])
                A(nrm[:, 1, :], nrm[:, 0, :], ACT.Sqrt).then_inc(act_done, 1)
                for j in range(12):
                    act.wait_ge(pe_done, GATES + NB // 2 + NG + j + 1)
                    A(M["z_base"][:, j // 6, :, :].rearrange("p b t -> p (b t)")[:, j % 6 * 512:(j % 6 + 1) * 512], psG[:, j % 2, :], ACT.Copy).then_inc(act_done, 1)
                act.wait_ge(act_done, ROOT + 12)

            @block.vector
            def _(dve):
                V = nc.vector
                s = Steps(dve, step)
                dve.wait_ge(loaded, 7 * 16)
                s.link(V.tensor_tensor(M["a0"][:, :], M["a0"][:, :], p0[:, :], ALU.add))
                dve.wait_ge(zeroed, 1)
                for b2 in range(2):
                    ins = V.tensor_tensor(M["b0"][:, :, b2, b2 * DM:(b2 + 1) * DM], w1[:, :, :], p1[:, :, :], ALU.add)
                ins.then_inc(made, 1)
                dve.wait_ge(turned, 1)
                s.link(V.tensor_copy(wft[:, :, :].rearrange("d a c -> d (a c)")[:, 0:NQ + 3], psT[0:DM, 0, 0:NQ + 3]))
                V.tensor_copy(gcol[:, :, :], bc(wft[:, 1, NQ - 128:NQ - 128 + 3].unsqueeze(2), DM, 3, 128)).then_inc(made, 1)
                dve.wait_ge(turned, 2)
                for b2 in range(2):
                    h = slice(b2 * DM, (b2 + 1) * DM)
                    ins = V.tensor_copy(M["b0t"][h, :], psT[h, 1, b2 * FH:(b2 + 1) * FH])
                s.link(ins)
                for j in range(NB // 2):
                    dve.wait_ge(act_done, GATES + j + 1)
                    V.tensor_tensor(fp[:, 2 * j:2 * j + 2, :], psF[:, j % 2, 0:2 * NQ].rearrange("t (a c) -> t a c", a=2), sg[:, j % 2, :, :], ALU.mult).then_inc(fp_ready, 1)
                dve.wait_ge(fp_ready, NB // 2)
                qk = fp[:, :, 0:2 * DM].rearrange("t b (a d) -> t b a d", a=2)
                dve.wait_ge(act_done, GATES)
                for a in range(2):
                    sq = work[0:NT, :, 0:DM]
                    s.link(V.tensor_tensor(sq, qk[:, :, a, :], qk[:, :, a, :], ALU.mult))
                    ins = V.reduce_sum(nrm[:, 0, a * NB:(a + 1) * NB], sq, AX.X)
                    if a == 0:
                        s.link(ins)
                ins.then_inc(made, 1)
                dve.wait_ge(act_done, ROOT)
                s.link(V.tensor_scalar(nrm[:, 1, :], nrm[:, 1, :], 1e-12, None, ALU.max))
                s.link(V.reciprocal(nrm[:, 2, :], nrm[:, 1, :]))
                s.link(V.tensor_tensor(nrm[:, 3, :], nrm[:, 2, :], nrm[:, 0, :], ALU.mult))
                s.link(V.tensor_tensor(nrm[:, 2, :], nrm[:, 3, :], nrm[:, 1, :], ALU.add))
                s.link(V.tensor_scalar(nrm[:, 3, :], nrm[:, 2, :], 0.5, 1e-12, ALU.mult, ALU.max))
                s.link(V.reciprocal(nrm[:, 1, :], nrm[:, 3, :]))
                for a in range(2):
                    V.tensor_copy(vv[:, :, a * DM:(a + 1) * DM], fp[:, a * HB:(a + 1) * HB, 2 * DM:3 * DM])
                for a in range(2):
                    ins = V.tensor_tensor(qk[:, :, a, :], qk[:, :, a, :], bc(nrm[:, 1, a * NB:(a + 1) * NB].unsqueeze(2), NT, NB, DM), ALU.mult)
                ins.then_inc(made, 1)
                s.link(V.memset(work[:, :, :], 0.0))
                s.link(V.tensor_copy(work[:, :, 0:1], keep[:, :, 0:1]))
                s.link(V.memset(keep[:, :, 0:1], 0.0))
                s.link(V.memset(eta[:, :, 0:1], 0.0))
                s.link(V.tensor_tensor_scan(flat(work), flat(keep), flat(work), 0.0, ALU.mult, ALU.add))
                s.link(V.memset(M["c_f"][:, :, 0:1], 1.0))
                s.link(V.tensor_copy(M["c_f"][:, :, 1:NT], work[:, :, 0:NT - 1]))
                s.link(V.tensor_tensor(theta[0:NT, :, :], theta[0:NT, :, :], bc(diag[:, :].unsqueeze(1), NT, NB, NT), ALU.mult))
                s.link(V.tensor_tensor_scan(flat(eta)[0:NT], flat(eta)[0:NT], flat(theta)[0:NT], 0.0, ALU.mult, ALU.add))
                s.link(V.tensor_tensor_scan(flat(eta)[0:NT], flat(keep)[0:NT], flat(eta)[0:NT], 0.0, ALU.mult, ALU.add))
                s.link(V.memset(theta[0:NT, :, 0:1], 0.0))
                V.tensor_copy(theta[0:NT, :, 1:NT], eta[0:NT, :, 0:NT - 1]).then_inc(made, 1)
                V.tensor_copy(keep[:, :, :], work[:, :, :]).then_inc(made, 1)
                dve.wait_ge(made, MADE["c"])
                V.tensor_copy(work[0:NT, :, :], eta[0:NT, :, :]).then_inc(made, 1)
                dve.wait_ge(made, MADE["wt"])
                n = 2
                for what in range(4):
                    for g in range(NG if what != 2 else NG // 2):
                        dve.wait_ge(turned, n + 1)
                        src = psT[:, n % 4, 0:N]
                        if what < 2:
                            ins = V.tensor_copy((kT, qT)[what][:, g * N:(g + 1) * N], src[0:DM])
                        elif what == 2:
                            ins = V.tensor_copy(M["v_y"][:, g * G:(g + 1) * G, :].rearrange("p b t -> p (b t)"), src)
                        else:
                            ins = V.tensor_copy(by_chunk(eta)[:, g * G:(g + 1) * G], src[0:NT].rearrange("t (b c s) -> t b c s", b=G, s=NC))
                        ins.then_inc(taken, 1)
                        n += 1
                    if what == 1:
                        dve.wait_ge(taken, n - 2)
                        V.sem_inc(made, 1)
                dve.wait_ge(taken, n - 2)
                V.sem_inc(made, 1)
                qc = fp[0:DM, 0:16, :].rearrange("p a c -> p (a c)")
                V.tensor_tensor(qc, qT[:, :], flat(keep)[0:DM], ALU.mult).then_inc(made, 1)
                for g in range(NG):
                    dve.wait_ge(pe_done, GATES + NB // 2 + g + 1)
                    o = slice(g * G, (g + 1) * G)
                    V.tensor_tensor(by_chunk(theta)[:, o], psT[0:NT, g % 4, 0:N].rearrange("t (b c s) -> t b c s", b=G, s=NC), by_chunk(eta)[:, o], ALU.mult).then_inc(gram_read, 1)
                dve.wait_ge(gram_read, NG)
                V.sem_inc(made, 1)
                dve.wait_ge(k_stored, 16)
                V.tensor_tensor(kT[:, :], kT[:, :], flat(M["c_f"])[0:DM], ALU.mult).then_inc(made, 1)
                for m in range(2 * (NCH - 1)):
                    dve.wait_ge(bs_turned, m + 1)
                    V.tensor_copy((M["w_bs"], M["g_bs"])[m % 2][:, m // 2, :, :].rearrange("p q t -> p (q t)"), psT[:, m % 4, 0:4 * NT]).then_inc(bs_ready, 1)
                dve.wait_ge(bs_ready, 2 * (NCH - 1))


BF16 = mybir.dt.bfloat16
PAIRS = ((0, 0), (0, 1), (1, 0), (1, 1), (0, 2), (2, 0))


def memory_scan(nc, M, H_room, hist_y, ident, cols_in, rows_in, own_in):
    GW = QB * NC
    with ExitStack() as ctx:
        sb = lambda n, sh: ctx.enter_context(nc.sbuf_tensor("sc_" + n, sh, F32))
        sem = lambda n: ctx.enter_context(nc.semaphore("sc_" + n))
        bf = lambda n, sh: ctx.enter_context(nc.sbuf_tensor("sc_" + n, sh, BF16))
        h_t, dy_t = bf("h_t", [128, NCH - 1, 3, 4, FH]), bf("dy_t", [128, NCH - 1, 3, 2, 128])
        h_f, dy_f = bf("h_f", [128, NCH - 1, 3, 2, NB * NC]), bf("dy_f", [128, NCH - 1, 3, HB * NC])
        b0_f, b0_t = bf("b0_f", [128, 3, 2, 2, 128]), bf("b0_t", [128, 3, FH])
        h_now, dy_now = bf("h_now", [128, 2, 3, 4 * QB]), bf("dy_now", [128, 2, 3, 2 * QB])
        dz_t = sb("dz_t", [128, 4, FH])
        hist_h, hist_dz = sb("hist_h", [128, 2, 2, NB, NC]), sb("hist_dz", [128, 2, 2, NB, NC])
        g_mask = sb("g_mask", [128, NCH - 1, 4, QB, NC])
        wm = sb("wm", [128, 2, 2, NCH - 1, 2 * QB])
        own = sb("own", [128, QB])
        coef, coef_rest = sb("coef", [128, 2, NCH - 1, 2 * QB]), sb("coef_rest", [128, 2, NCH - 1, 2 * QB])
        coef_y, coef_h = bf("coef_y", [128, 2, 3, NCH - 1, 2 * QB]), bf("coef_h", [128, 2, 3, NCH - 1, 2 * QB])
        room = H_room[:, :, :].rearrange("p b d -> p (b d)")
        prod, z_prod = (room[:, n * 1024:(n + 1) * 1024].rearrange("p (g a x) -> p g a x", g=2, a=2) for n in range(2))
        dy_rest = sb("dy_rest", [128, 2 * GW])
        now_rest = sb("now_rest", [128, 2, 4 * QB])
        y_prod = sb("y_prod", [128, 2, GW])
        y_w = sb("y_w", [128, 2, GW])
        w_row = sb("w_row", [128, 2, HB * NC])
        g_row = sb("g_row", [128, 2, NB * NC])
        zsum, z_before, z, sg, slope, hs, hg, first_part, dh, dh2 = (sb(n, [128, 2, 4 * QB]) for n in ("zsum", "z_before", "z", "sg", "slope", "hs", "hg", "first_part", "dh", "dh2"))
        pred, off, ysum, rest = (sb(n, [128, 2, QB]) for n in ("pred", "off", "ysum", "rest"))
        dy_pad = sb("dy_pad", [128, 2, 2, QB])
        cols, rows_ = sb("cols", [128, 2, 128]), sb("rows", [128, 2, 128])
        ps = ctx.enter_context(nc.psum_tensor("sc_ps", [128, 8, 512], F32))
        score_h = lambda g: ps[:, g, 0:(NCH - 1) * 2 * QB].rearrange("p (c j) -> p c j", c=NCH - 1)
        score_y = lambda g: ps[:, g, 128:128 + (NCH - 1) * 2 * QB].rearrange("p (c j) -> p c j", c=NCH - 1)
        first_y = lambda g: ps[:, g, 256:256 + QB]
        first_h = lambda g: ps[:, g, 320:320 + 4 * QB]
        hh = lambda g: ps[:, 2 + g, 0:GW]
        yy = lambda g: ps[:, 2 + g, GW:3 * GW]
        past_y = lambda g: ps[:, 4 + g, 0:2 * QB]
        past_h = lambda g: ps[:, 4 + g, 64:64 + 4 * QB]
        quads = lambda x: x.rearrange("p (a c b) -> p a c b", a=2, c=2)
        h_at = lambda x, g, c, i: x[:, :, c % 2, :, bass.ds(i, 1)].rearrange("p a (c b) s -> p a c (b s)", c=2)[:, :, :, QB * g:QB * (g + 1)]
        y_at = lambda g, c, i: hist_y[:, c, QB * g:QB * (g + 1), bass.ds(i, 1)].rearrange("p b s -> p (b s)")
        cols_at = lambda x, g, t: x[:, QB * g:QB * (g + 1), bass.ds(t, 1)].rearrange("p b s -> p (b s)")
        chunk = lambda x, a, g, c: x[:, a, c % 2, :, :].rearrange("p (c b) s -> p c b s", c=2)[:, :, QB * g:QB * (g + 1), :]
        both = lambda x, g, c: x[:, :, c % 2, :, :].rearrange("p a (c b) s -> p a c (b s)", c=2)[:, :, :, GW * g:GW * (g + 1)]
        w_in, g_rows_in = [sem("w_in0"), sem("w_in1")], [sem("g_in0"), sem("g_in1")]
        parts_ready, split_ready, hi_ready, rest_ready, mid_ready, dumped = sem("parts_ready"), sem("split_ready"), sem("hi_ready"), sem("rest_ready"), sem("mid_ready"), [sem("dumped0"), sem("dumped1")]
        ones_in, zeroed, step = sem("ones_in"), sem("zeroed"), sem("step")
        z_ready, sg_ready, h_ready, slope_ready = sem("z_ready"), sem("sg_ready"), sem("h_ready"), sem("slope_ready")
        scores_done, coef_ready, prod_ready, hh_done, past_y_done = (sem(n) for n in ("scores_done", "coef_ready", "prod_ready", "hh_done", "past_y_done"))
        yw_ready, dy_ready, yprod_ready, yy_done, past_h_done = (sem(n) for n in ("yw_ready", "dy_ready", "yprod_ready", "yy_done", "past_h_done"))
        zprod_ready, dz_ready, pool_step, wm_ready = sem("zprod_ready"), sem("dz_ready"), sem("pool_step"), sem("wm_ready")
        turned, h_kept, dz_kept, base_done, base_added, g_masked = (sem(n) for n in ("turned", "h_kept", "dz_kept", "base_done", "base_added", "g_masked"))

        def split_work(c):
            s, flat = (c - 1) % 2, "p a x -> p (a x)"
            slot = hist_h[:, :, s, :, :].rearrange("p a b s -> p a (b s)")
            yield slot, lambda w: h_f[:, c - 1, w, :, :], room[:, 0:1024].rearrange("p (a x) -> p a x", a=2)
            yield (ps[:, 0:2, :].rearrange(flat), lambda w: h_t[:, c - 1, w, :, :].rearrange(flat), room[:, 1024:2048])
            yield (hist_y[:, c - 1, :, :].rearrange(flat), lambda w: dy_f[:, c - 1, w, :], y_prod[:, :, :].rearrange(flat))
            yield ps[:, 4, 0:2 * GW], lambda w: dy_t[:, c - 1, w, :, :].rearrange(flat), dy_rest[:, :]

        with nc.Block() as block:
            @block.sync
            def _(sp):
                sp.dma_start(cols[:, :, :], cols_in).then_inc(ones_in, 16)
                sp.dma_start(rows_[:, :, :], rows_in).then_inc(ones_in, 16)
                sp.dma_start(own[:, :], own_in).then_inc(ones_in, 16)
                for c in range(NCH):
                    def rows(k, t, turn):
                        if turn is not None:
                            sp.wait_ge(yw_ready, 2 * turn)
                            sp.wait_ge(z_ready, 2 * turn)
                        for b2 in range(2):
                            sp.dma_start(w_row[b2 * DM:(b2 + 1) * DM, k, :],
                                         M["w_rows"][bass.ds(t, 1), c, b2 * HB:(b2 + 1) * HB, :].rearrange("t b s -> t (b s)").broadcast_to([DM, HB * NC])).then_inc(w_in[k], 16)
                        sp.dma_start(g_row[:, k, :], M["g_rows"][bass.ds(t, 1), c, :, :].rearrange("t b s -> t (b s)").broadcast_to([128, NB * NC])).then_inc(g_rows_in[k], 16)

                    if c == 0:
                        for k in range(2):
                            rows(k, k, None)
                        with sp.Fori(1, NC // 2) as i:
                            for k in range(2):
                                rows(k, 2 * i + k, 2 * i + k - 1)
                    else:
                        with sp.Fori(0, NC // 2) as i:
                            for k in range(2):
                                rows(k, c * NC + 2 * i + k, c * NC + 2 * i + k - 1)
                for n in range(2):
                    sp.wait_ge(dumped[n], 16 * NCH)

            @block.gpsimd
            def _(pool):
                P = nc.gpsimd
                for t in (hist_h, hist_dz):
                    P.memset(t[:, :, :, :, :], 0.0).then_inc(zeroed, 1)
                P.memset(hist_y[:, :, :, :], 0.0).then_inc(zeroed, 1)
                P.memset(dy_pad[:, :, :, :], 0.0).then_inc(zeroed, 1)
                P.memset(dy_now[:, :, :, :], 0.0).then_inc(zeroed, 1)
                pool.wait_ge(zeroed, 5)
                pool.wait_ge(ones_in, 48)
                for c in range(NCH):
                    pool.wait_ge(g_rows_in[0], (c * NC // 2) * 16 + 16)
                    if c >= 2:
                        pool.wait_ge(zeroed, 5 + c - 1)

                    def one_step(i, k, last):
                        t = c * NC + 2 * i + k
                        if c >= 1:
                            pool.wait_ge(dz_ready, 2 * t - 2)
                            for g in range(2):
                                ins = P.tensor_tensor(wm[:, k, g, 0:c, :].rearrange("p c (q b) -> p c q b", q=2),
                                                      bc(M["w_bs"][:, 0:c, :, bass.ds(t, 1)].rearrange("p c (q h) t -> p c q (h t)", q=2)[:, :, :, g:g + 1], 128, c, 2, QB),
                                                      bc(own[:, :].unsqueeze(1).unsqueeze(1), 128, c, 2, QB), ALU.mult)
                                ins.then_inc(wm_ready, 1)
                        pool.wait_ge(w_in[k], (c * NC + 2 * i) * 16 + 32)
                        for g in range(2):
                            pool.wait_ge(yprod_ready, 2 * t + g + 1)
                            P.tensor_tensor(y_w[:, g, :], w_row[:, k, g * GW:(g + 1) * GW],
                                            hist_y[:, c, g * QB:(g + 1) * QB, :].rearrange("p b s -> p (b s)"), ALU.mult).then_inc(yw_ready, 1)
                        for g in range(2):
                            pool.wait_ge(h_ready, 2 * t + g + 1)
                            for a in range(2):
                                ins = P.tensor_tensor(prod[:, g, a, :].rearrange("p (c b s) -> p c b s", c=2, s=NC), chunk(hist_h, a, g, c),
                                                      bc(hist_h[:, a, c % 2, :, bass.ds(2 * i + k, 1)].rearrange("p (c b) s -> p c b s", c=2)[:, :, QB * g:QB * (g + 1), :], 128, 2, QB, NC), ALU.mult)
                            ins.then_inc(prod_ready, 1)
                            h = h_at(hist_h, g, c, 2 * i + k)
                            P.tensor_tensor(quads(hg[:, g, :]), h, quads(sg[:, g, :]), ALU.mult)
                            P.tensor_tensor(quads(hs[:, g, :]), h, quads(sg[:, g, :]), ALU.add).then_inc(pool_step, 1)
                            pool.wait_ge(pool_step, 2 * t + g + 1)
                            P.tensor_tensor(slope[:, g, :], hs[:, g, :], hg[:, g, :], ALU.subtract).then_inc(slope_ready, 1)
                        if not last:
                            pool.wait_ge(g_rows_in[1 - k], (c * NC // 2 + i + k) * 16 + 16)
                            for g in range(2):
                                P.tensor_tensor(z_prod[:, g, :, :].rearrange("p a (c x) -> p a c x", c=2), both(hist_dz, g, c),
                                                bc(g_row[:, 1 - k, :].rearrange("p (c x) -> p c x", c=2)[:, :, GW * g:GW * (g + 1)].unsqueeze(1), 128, 2, 2, GW), ALU.mult).then_inc(zprod_ready, 1)

                    with pool.Fori(0, NC // 2 - 1) as i:
                        for k in range(2):
                            one_step(i, k, False)
                    for k in range(2):
                        one_step(NC // 2 - 1, k, k == 1)
                    if 1 <= c < NCH - 1:
                        pool.wait_ge(dumped[(c - 1) % 2], 32 * ((c - 1) // 2 + 1))
                        pool.wait_ge(turned, 5 * c)
                        P.memset(hist_dz[:, :, (c + 1) % 2, :, :], 0.0).then_inc(zeroed, 1)

            @block.scalar
            def _(act):
                A = nc.scalar.activation

                def dump(c):
                    for n, x in (("h", hist_h), ("dz", hist_dz)):
                        nc.scalar.dma_start(M["hist_" + n][:, :, c, :, :], x[:, :, c % 2, :, :]).then_inc(dumped[c % 2], 16)

                act.wait_ge(ones_in, 48)
                for c in range(NCH):
                    if c >= 1:
                        n = 4 * (c - 1)
                        act.wait_ge(dz_ready, 2 * c * NC)
                        dump(c - 1)
                        for j, (src, parts, rest) in enumerate(split_work(c)):
                            if j in (1, 3):
                                act.wait_ge(turned, 5 * (c - 1) + (2 if j == 1 else 5))
                            A(parts(0), src, ACT.Copy).then_inc(hi_ready, 1)
                        for j, (src, parts, rest) in enumerate(split_work(c)):
                            act.wait_ge(rest_ready, n + j + 1)
                            A(parts(1), rest, ACT.Copy).then_inc(mid_ready, 1)
                        act.wait_ge(base_done, c * (2 * NCH - 1 - c) // 2)
                    with act.Fori(0, NC // 2) as i:
                        for k in range(2):
                            for g in range(2):
                                act.wait_ge(z_ready, 2 * (c * NC + 2 * i + k) + g + 1)
                                A(sg[:, g, :], z[:, g, :], ACT.Sigmoid).then_inc(sg_ready, 1)
                        if c < NCH - 1:
                            A(g_mask[:, c:NCH - 1, :, bass.ds(i, 1), :].rearrange("p c q b t -> p c q (b t)"),
                              M["g_bs"][:, c, :, (c + 1) * NC:NT].rearrange("p q (c t) -> p c q t", t=NC), ACT.Copy,
                              scale=own[:, bass.ds(i, 1)]).then_inc(g_masked, 1)
                act.wait_ge(dz_ready, 2 * NT)
                dump(NCH - 1)

            @block.tensor
            def _(pe):
                MM, T = nc.tensor.matmul, nc.tensor.transpose
                pe.wait_ge(ones_in, 48)
                pe.wait_ge(split_ready, 1)
                for c in range(NCH):
                    if c >= 1:
                        pe.wait_ge(dz_ready, 2 * c * NC)
                        for n, x in ((0, hist_h), (2, hist_dz)):
                            for q in range(4):
                                for a in range(2):
                                    mm = T(ps[:, n + q // 2, (q % 2 * 2 + a) * 128:(q % 2 * 2 + a + 1) * 128],
                                           x[:, a, (c - 1) % 2, q * QB:(q + 1) * QB, :].rearrange("p b s -> p (b s)"), ident[:, :])
                                if q % 2 == 1:
                                    mm.then_inc(turned, 1)
                        for g in range(2):
                            mm = T(ps[:, 4, g * 128:(g + 1) * 128], hist_y[:, c - 1, g * QB:(g + 1) * QB, :].rearrange("p b s -> p (b s)"), ident[:, :])
                        mm.then_inc(turned, 1)
                        pe.wait_ge(dz_kept, 2 * c)
                        pe.wait_ge(g_masked, c * NC // 2)
                        for cc in range(c, NCH):
                            n = (c - 1) * (2 * NCH - c) // 2 + cc - c
                            if n:
                                pe.wait_ge(base_added, 2 * n)
                            for a in range(2):
                                for q in range(4):
                                    mm = MM(ps[:, 6 + a, q * GW:(q + 1) * GW], dz_t[:, q, a * 128:(a + 1) * 128],
                                            g_mask[:, cc - 1, q, :, :].rearrange("p b t -> p (b t)"), start=True, stop=True)
                            mm.then_inc(base_done, 1)
                        pe.wait_ge(split_ready, c + 1)
                    with pe.Fori(0, NC) as i:
                        t = c * NC + i

                        def forward_scores(g):
                            now = lambda a, b2, m: h_now[:, g, m, (2 * a + b2) * QB:(2 * a + b2 + 1) * QB]
                            pe.wait_ge(parts_ready, 4 * t + g + 1)
                            for cc in range(c):
                                for b2 in range(2):
                                    for n, (a, (w, m)) in enumerate((a, p) for a in range(2) for p in PAIRS):
                                        MM(score_h(g)[:, cc, b2 * QB:(b2 + 1) * QB], h_f[:, cc, w, a, (2 * b2 + g) * GW:(2 * b2 + g + 1) * GW], now(a, b2, m),
                                           start=n == 0, stop=n == 11)
                            for n, (a, b2, (w, m)) in enumerate((a, b2, p) for a in range(2) for b2 in range(2) for p in PAIRS):
                                mm = MM(first_y(g), b0_f[:, w, a, b2, :], now(a, b2, m), start=n == 0, stop=n == 23)
                            mm.then_inc(scores_done, 1)
                            pe.wait_ge(prod_ready, 2 * t + g + 1)
                            for a in range(2):
                                for b2 in range(2):
                                    mm = MM(hh(g), cols[:, b2, :], prod[:, g, a, b2 * GW:(b2 + 1) * GW], start=a + b2 == 0, stop=a + b2 == 2)
                            mm.then_inc(hh_done, 1)

                        def forward_past(g):
                            if c >= 1:
                                pe.wait_ge(coef_ready, 4 * (t - NC) + g + 1)
                                for n, (cc, (w, m)) in enumerate((cc, p) for cc in range(c) for p in PAIRS):
                                    mm = MM(past_y(g), dy_t[:, cc, w, g, :], coef_y[:, g, m, cc, :], start=n == 0, stop=n == 6 * c - 1)
                                mm.then_inc(past_y_done, 1)

                        def backward_scores(g):
                            pe.wait_ge(parts_ready, 4 * t + 2 + g + 1)
                            for cc in range(c):
                                for n, (w, m) in enumerate(PAIRS):
                                    MM(score_y(g)[:, cc, :], dy_f[:, cc, w, g * GW:(g + 1) * GW], dy_now[:, g, m, :], start=n == 0, stop=n == 5)
                            for a in range(2):
                                for n, (w, m) in enumerate(PAIRS):
                                    mm = MM(first_h(g)[:, a * 2 * QB:(a + 1) * 2 * QB], b0_t[:, w, a * 128:(a + 1) * 128], dy_now[:, g, m, :], start=n == 0, stop=n == 5)
                            mm.then_inc(scores_done, 1)
                            pe.wait_ge(yprod_ready, 2 * t + g + 3)
                            for b2 in range(2):
                                mm = MM(yy(g)[:, b2 * GW:(b2 + 1) * GW], rows_[:, b2, :], y_prod[:, g, :], start=True, stop=True)
                            mm.then_inc(yy_done, 1)

                        def backward_past(g):
                            if c >= 1:
                                pe.wait_ge(coef_ready, 4 * (t - NC) + 2 + g + 1)
                                for a in range(2):
                                    for b2 in range(2):
                                        o = (2 * a + b2) * QB
                                        for n, (cc, (w, m)) in enumerate((cc, p) for cc in range(c) for p in PAIRS):
                                            mm = MM(past_h(g)[:, o:o + QB], h_t[:, cc, w, 2 * b2 + g, a * 128:(a + 1) * 128], coef_h[:, g, m, cc, b2 * QB:(b2 + 1) * QB],
                                                    start=n == 0, stop=n == 6 * c - 1)
                                mm.then_inc(past_h_done, 1)

                        forward_scores(0)
                        forward_past(0)
                        forward_scores(1)
                        backward_scores(0)
                        forward_past(1)
                        backward_past(0)
                        backward_scores(1)
                        backward_past(1)

            @block.vector
            def _(dve):
                V = nc.vector
                V.sem_inc(yprod_ready, 2)
                s = Steps(dve, step)
                for parts, x, left in ((lambda w: b0_f[:, w, :, :, :].rearrange("p a c m -> p (a c m)"), M["b0"][:, :, :, :].rearrange("p a c m -> p (a c m)"), room[:, 0:512]),
                                       (lambda w: b0_t[:, w, :], M["b0t"][:, :], room[:, 1024:1024 + FH])):
                    s.link(V.tensor_copy(parts(0), x))
                    V.tensor_tensor(parts(1), x, parts(0), ALU.subtract)
                    s.link(V.tensor_tensor(left, x, parts(0), ALU.subtract))
                    s.link(V.tensor_tensor(parts(2), left, parts(1), ALU.subtract))
                V.sem_inc(split_ready, 1)
                K0 = s.n
                dve.wait_ge(zeroed, 5)
                KS, KP, K1, KL = 38, 2, 10, 8

                for c in range(NCH):
                    base_at = lambda g, t: M["z_base"][:, :, :, bass.ds(t, 1)].rearrange("p a (c b) s -> p a c (b s)", c=2)[:, :, :, QB * g:QB * (g + 1)]

                    def hidden_before(s, g, t):
                        dve.wait_ge(zprod_ready, 2 * (t - c - 1) + g + 1)
                        s.link(V.reduce_sum(zsum[:, g, :], z_prod[:, g, :, :].rearrange("p a (b s) -> p (a b) s", s=NC), AX.X))
                        s.mark(V.tensor_tensor(quads(z_before[:, g, :]), quads(zsum[:, g, :]), base_at(g, t), ALU.add))

                    def hidden(s, g, t, i, k, turn):
                        dve.wait_ge(g_rows_in[k], turn * 16 + 16)
                        weight = g_row[:, k, :].rearrange("p (b s) -> p b s", s=NC)[:, :, bass.ds(i, 1)].rearrange("p (c b) s -> p c (b s)", c=2)[:, :, QB * g:QB * (g + 1)]
                        s.link(V.tensor_tensor(quads(zsum[:, g, :]), h_at(hist_dz, g, c, i), bc(weight.unsqueeze(1), 128, 2, 2, QB), ALU.mult))
                        V.tensor_tensor(z[:, g, :], z_before[:, g, :], zsum[:, g, :], ALU.add).then_inc(z_ready, 1)

                    def weigh(s, parts, score, g, k, beside=()):
                        beside = [*beside, *[lambda: None] * 3]
                        hi, mid, lo = (parts[:, g, w, 0:c, :] for w in range(3))
                        full, rest = coef[:, g, 0:c, :], coef_rest[:, g, 0:c, :]
                        V.tensor_tensor(hi, score(g)[:, 0:c, :], wm[:, k, g, 0:c, :], ALU.mult)
                        s.mark(V.tensor_tensor(full, score(g)[:, 0:c, :], wm[:, k, g, 0:c, :], ALU.mult))
                        beside[0]()
                        dve.wait_ge(step, s.base + s.n)
                        V.tensor_tensor(mid, full, hi, ALU.subtract)
                        s.mark(V.tensor_tensor(rest, full, hi, ALU.subtract))
                        beside[1]()
                        dve.wait_ge(step, s.base + s.n)
                        V.tensor_tensor(lo, rest, mid, ALU.subtract).then_inc(coef_ready, 1)
                        beside[2]()

                    def silu(s, g, t, i):
                        dve.wait_ge(sg_ready, 2 * t + g + 1)
                        V.tensor_tensor(h_at(hist_h, g, c, i), quads(z[:, g, :]), quads(sg[:, g, :]), ALU.mult).then_inc(h_ready, 1)
                        hi, mid, lo = (h_now[:, g, w, :] for w in range(3))
                        V.tensor_tensor(hi, z[:, g, :], sg[:, g, :], ALU.mult).then_inc(step, 1)
                        s.n += 1
                        dve.wait_ge(step, s.base + s.n)
                        dve.wait_ge(h_ready, 2 * t + g + 1)
                        V.tensor_tensor(quads(mid), h_at(hist_h, g, c, i), quads(hi), ALU.subtract)
                        s.link(V.tensor_tensor(quads(now_rest[:, g, :]), h_at(hist_h, g, c, i), quads(hi), ALU.subtract))
                        V.tensor_tensor(lo, now_rest[:, g, :], mid, ALU.subtract).then_inc(parts_ready, 1)

                    def output(s, g, t, k):
                        dve.wait_ge(scores_done, 4 * t + g + 1)

                        def scaled():
                            for b2 in range(2):
                                h, o = slice(b2 * DM, (b2 + 1) * DM), b2 * HB + g * QB
                                ins = V.scalar_tensor_tensor(pred[h, g, :], first_y(g)[h], 2.0 / DM, M["c_f"][h, o:o + QB, bass.ds(t, 1)].rearrange("p b s -> p (b s)"), ALU.mult, ALU.mult)
                            s.mark(ins)

                        def minus_v():
                            s.mark(V.scalar_tensor_tensor(off[:, g, :], cols_at(M["v_y"], g, t), -2.0 / DM, pred[:, g, :], ALU.mult, ALU.add))

                        def this_chunk():
                            dve.wait_ge(hh_done, 2 * t + g + 1)
                            dve.wait_ge(yw_ready, 2 * t + g + 1)
                            s.mark(V.tensor_tensor(y_prod[:, g, :], hh(g), y_w[:, g, :], ALU.mult))

                        if c >= 1:
                            dve.wait_ge(wm_ready, 2 * (t - NC) + g + 1)
                            weigh(s, coef_y, score_h, g, k, (scaled, minus_v, this_chunk))
                        else:
                            scaled()
                            dve.wait_ge(step, s.base + s.n)
                            minus_v()
                            this_chunk()
                        dve.wait_ge(step, s.base + s.n)
                        s.link(V.reduce_sum(ysum[:, g, :], y_prod[:, g, :].rearrange("p (b s) -> p b s", s=NC), AX.X))

                    def output_end(s, g, t, i):
                        if c >= 1:
                            dve.wait_ge(past_y_done, 2 * (t - NC) + g + 1)
                            for b2 in range(2):
                                h = slice(b2 * DM, (b2 + 1) * DM)
                                ins = V.scalar_tensor_tensor(rest[h, g, :], past_y(g)[h, b2 * QB:(b2 + 1) * QB], 2.0 / DM, off[h, g, :], ALU.mult, ALU.add)
                        else:
                            ins = V.tensor_copy(rest[:, g, :], off[:, g, :])
                        s.link(ins)
                        for b2 in range(2):
                            h = slice(b2 * DM, (b2 + 1) * DM)
                            V.scalar_tensor_tensor(dy_pad[h, g, b2, :], ysum[h, g, :], 2.0 / DM, rest[h, g, :], ALU.mult, ALU.add)
                            V.scalar_tensor_tensor(dy_now[h, g, 0, b2 * QB:(b2 + 1) * QB], ysum[h, g, :], 2.0 / DM, rest[h, g, :], ALU.mult, ALU.add)
                        V.scalar_tensor_tensor(y_at(g, c, i), ysum[:, g, :], 2.0 / DM, rest[:, g, :], ALU.mult, ALU.add).then_inc(dy_ready, 1)
                        dve.wait_ge(dy_ready, 2 * t + g + 1)
                        full = dy_pad[:, g, :, :].rearrange("p c b -> p (c b)")
                        V.tensor_tensor(dy_now[:, g, 1, :], full, dy_now[:, g, 0, :], ALU.subtract)
                        s.mark(V.tensor_tensor(now_rest[:, g, 0:2 * QB], full, dy_now[:, g, 0, :], ALU.subtract))
                        V.tensor_tensor(y_prod[:, g, :].rearrange("p (b s) -> p b s", s=NC), y_w[:, g, :].rearrange("p (b s) -> p b s", s=NC),
                                        bc(hist_y[:, c, QB * g:QB * (g + 1), bass.ds(i, 1)], 128, QB, NC), ALU.mult).then_inc(yprod_ready, 1)
                        dve.wait_ge(step, s.base + s.n)
                        V.tensor_tensor(dy_now[:, g, 2, :], now_rest[:, g, 0:2 * QB], dy_now[:, g, 1, :], ALU.subtract).then_inc(parts_ready, 1)

                    def gradient_scores(s, g, t, k, beside=()):
                        dve.wait_ge(scores_done, 4 * t + 2 + g + 1)
                        beside = [*beside, *[lambda: None] * 2]

                        def first():
                            cf = M["c_f"][:, :, bass.ds(t, 1)].rearrange("p (c b) s -> p c (b s)", c=2)[:, :, QB * g:QB * (g + 1)]
                            V.tensor_tensor(quads(first_part[:, g, :]), quads(first_h(g)), bc(cf.unsqueeze(1), 128, 2, 2, QB), ALU.mult)
                            beside[0]()

                        if c >= 1:
                            weigh(s, coef_h, score_y, g, k, (first, beside[1]))
                        else:
                            first()
                            beside[1]()

                    def gradient_chunk(s, g, t):
                        dve.wait_ge(yy_done, 2 * t + g + 1)
                        s.link(V.tensor_tensor(prod[:, g, :, :].rearrange("p a (c x) -> p a c x", c=2), both(hist_h, g, c),
                                               bc(yy(g).rearrange("p (c x) -> p c x", c=2).unsqueeze(1), 128, 2, 2, GW), ALU.mult))
                        s.link(V.reduce_sum(dh[:, g, :], prod[:, g, :, :].rearrange("p a (b s) -> p (a b) s", s=NC), AX.X))

                    def add_first(s, g, t):
                        s.mark(V.tensor_tensor(dh2[:, g, :], dh[:, g, :], first_part[:, g, :], ALU.add))

                    def add_past(s, g, t):
                        if c >= 1:
                            dve.wait_ge(past_h_done, 2 * (t - NC) + g + 1)
                            s.mark(V.tensor_tensor(dh[:, g, :], dh2[:, g, :], past_h(g), ALU.add))

                    def gradient_end(s, g, t, i):
                        dve.wait_ge(slope_ready, 2 * t + g + 1)
                        dve.wait_ge(step, s.base + s.n)
                        d = dh if c >= 1 else dh2
                        V.tensor_tensor(h_at(hist_dz, g, c, i), quads(d[:, g, :]), quads(slope[:, g, :]), ALU.mult).then_inc(dz_ready, 1)

                    if c >= 1:
                        for n in range(2):
                            dve.wait_ge(turned, 5 * (c - 1) + 3 + n)
                            V.tensor_copy(dz_t[:, 2 * n:2 * n + 2, :].rearrange("p g f -> p (g f)"), ps[:, 2 + n, :]).then_inc(dz_kept, 1)
                        n = 4 * (c - 1)
                        for j, (src, parts, left) in enumerate(split_work(c)):
                            dve.wait_ge(hi_ready, n + j + 1)
                            V.tensor_tensor(left, src, parts(0), ALU.subtract).then_inc(rest_ready, 1)
                        for j, (src, parts, left) in enumerate(split_work(c)):
                            dve.wait_ge(mid_ready, n + j + 1)
                            dve.wait_ge(rest_ready, n + j + 1)
                            ins = V.tensor_tensor(parts(2), left, parts(1), ALU.subtract)
                        ins.then_inc(split_ready, 1)
                        dve.wait_ge(split_ready, c + 1)
                        for cc in range(c, NCH):
                            n = (c - 1) * (2 * NCH - c) // 2 + cc - c
                            dve.wait_ge(base_done, n + 1)
                            for a in range(2):
                                part = M["z_base"][:, a, :, cc * NC:(cc + 1) * NC]
                                V.tensor_tensor(part, part, ps[:, 6 + a, :].rearrange("p (b s) -> p b s", s=NC), ALU.add).then_inc(base_added, 1)
                        dve.wait_ge(base_added, 2 * n + 2)
                    if c >= 2:
                        dve.wait_ge(dumped[c % 2], 32 * (c // 2))
                        dve.wait_ge(zeroed, 5 + c - 1)
                    ks = KS if c >= 1 else KS - K1
                    start = K0 + (0 if c == 0 else NC * (KS - K1) - KL + KP + (c - 1) * (NC * KS - KL + KP))
                    s = Steps(dve, step, start)
                    for g in range(2):
                        V.tensor_copy(quads(z[:, g, :]), base_at(g, c * NC)).then_inc(z_ready, 1)
                    silu(s, 0, c * NC, 0)
                    assert s.n == KP, s.n

                    def one_step(turn, k, i, last):
                        t = c * NC + i
                        s = Steps(dve, step, start + KP + i * ks)
                        silu(s, 1, t, i)
                        output(s, 0, t, k)
                        output_end(s, 0, t, i)
                        if not last:
                            hidden_before(s, 0, t + 1)
                        output(s, 1, t, k)
                        gradient_scores(s, 0, t, k)
                        if not last:
                            hidden_before(s, 1, t + 1)
                        output_end(s, 1, t, i)
                        gradient_chunk(s, 0, t)
                        gradient_scores(s, 1, t, k, (lambda: add_first(s, 0, t), lambda: add_past(s, 0, t)))
                        gradient_end(s, 0, t, i)
                        if not last:
                            dve.wait_ge(dz_ready, 2 * t + 1)
                            hidden(s, 0, t + 1, i, 1 - k, turn + k)
                            silu(s, 0, t + 1, i + 1)
                        gradient_chunk(s, 1, t)
                        add_first(s, 1, t)
                        dve.wait_ge(step, s.base + s.n)
                        add_past(s, 1, t)
                        gradient_end(s, 1, t, i)
                        if not last:
                            dve.wait_ge(dz_ready, 2 * t + 2)
                            hidden(s, 1, t + 1, i, 1 - k, turn + k)
                        assert s.n == ks - (KL if last else 0), s.n

                    with dve.Fori(0, NC // 2 - 1) as j:
                        for k in range(2):
                            one_step(c * NC // 2 + j, k, 2 * j + k, False)
                    for k in range(2):
                        one_step(c * NC // 2 + NC // 2 - 1, k, NC - 2 + k, k == 1)
                    dve.wait_ge(dz_ready, 2 * (c + 1) * NC)


def memory_outputs(nc, M, H, hist_y, ident):
    NS = 4
    NR = HB // 2
    with ExitStack() as ctx:
        sb = lambda n, sh: ctx.enter_context(nc.sbuf_tensor("mo_" + n, sh, F32))
        sem = lambda n: ctx.enter_context(nc.semaphore("mo_" + n))
        hist_h, hist_dz = sb("hist_h", [128, 2, NCH, NB, NC]), sb("hist_dz", [128, 2, NCH, NB, NC])
        hist_in = sem("hist_in")
        kq = sb("kq", [DM, NS, 3, NT])
        w = sb("w", [NT, NS, NT])
        cn = sb("cn", [128, NS, NT])
        dz, hs = sb("dz", [128, NS, 2, NT]), sb("hs", [128, NS, 2, NT])
        dzt = sb("dzt", [NT, NS, FH])
        dy = sb("dy", [128, HB, NT])
        dyt = sb("dyt", [NT, HB, 128])
        s1, s2 = sb("s1", [NT, NS, NT]), sb("s2", [NT, NS, NT])
        sg, hq, hqc = (sb(n, [128, NS, 2, NT]) for n in ("sg", "hq", "hqc"))
        psA = ctx.enter_context(nc.psum_tensor("mo_psA", [128, NS, 512], F32))
        psB = ctx.enter_context(nc.psum_tensor("mo_psB", [128, NS, 512], F32))
        loaded = [sem(f"loaded{k}") for k in range(NS)]
        dy_turned, dyt_ready, staged, dz_turned, dzt_ready = sem("dy_turned"), sem("dyt_ready"), sem("staged"), sem("dz_turned"), sem("dzt_ready")
        s1_done, s1_ready, z_done, sg_ready, hq_ready = sem("s1_done"), sem("s1_ready"), sem("z_done"), sem("sg_ready"), sem("hq_ready")
        hqc_ready, s2_done, s2_ready, out_done, added = sem("hqc_ready"), sem("s2_done"), sem("s2_ready"), sem("out_done"), sem("added")
        dy_rowed = sem("dy_rowed")
        batch = lambda i, k: 2 * i + k // 2 + HB * (k % 2)
        zq = lambda k: psA[:, k, 256:256 + 2 * NT].rearrange("p (a t) -> p a t", a=2)
        with nc.Block() as block:
            @block.sync
            def _(sp):
                sp.dma_start(hist_dz[:, :, :, :, :], M["hist_dz"]).then_inc(hist_in, 16)
                sp.dma_start(hist_h[:, :, :, :, :], M["hist_h"]).then_inc(hist_in, 16)
                sp.dma_start(H[0:NT, :, :], M["h"]).then_inc(hist_in, 16)
                def load(i, k):
                    cols = bass.ds(batch(i, k) * NT, NT)
                    for j, n in enumerate(("k_t", "q_t", "qc_t")):
                        sp.dma_start(kq[:, k, j, :], M[n][:, cols]).then_inc(loaded[k], 16)
                    sp.dma_start(w[:, k, :], M["w_t"][:, cols]).then_inc(loaded[k], 16)
                    sp.dma_start(cn[:, k, :], M["c_now"][:, cols]).then_inc(loaded[k], 16)

                for k in range(NS):
                    load(0, k)
                with sp.Fori(1, NR) as i:
                    for k in range(NS):
                        sp.wait_ge(out_done, NS * i - NS + k + 1)
                        load(i, k)

            @block.gpsimd
            def _(pool):
                P = nc.gpsimd

                P.tensor_copy(dy[:, :, :].rearrange("p b (c s) -> p c b s", s=NC), hist_y[:, :, :, :]).then_inc(dy_rowed, 1)

                def stage(i, k):
                    b = batch(i, k)
                    P.tensor_copy(dz[:, k, :, :].rearrange("p a (c s) -> p a c s", s=NC), hist_dz[:, :, :, bass.ds(b, 1), :].rearrange("p a c b s -> p a c (b s)"))
                    P.tensor_copy(hs[:, k, :, :].rearrange("p a (c s) -> p a c s", s=NC), hist_h[:, :, :, bass.ds(b, 1), :].rearrange("p a c b s -> p a c (b s)")).then_inc(staged, 1)

                def scale(i, k):
                    pool.wait_ge(hq_ready, NS * i + k + 1)
                    P.tensor_tensor(hqc[:, k, :, :], hq[:, k, :, :], bc(cn[:, k:k + 1, :], 128, 2, NT), ALU.mult).then_inc(hqc_ready, 1)

                pool.wait_ge(hist_in, 48)
                for k in range(NS):
                    stage(0, k)
                with pool.Fori(0, NR - 1) as i:
                    for k in range(NS):
                        scale(i, k)
                    for k in range(NS):
                        pool.wait_ge(s2_done, NS * i + k + 1)
                        stage(i + 1, k)
                for k in range(NS):
                    scale(NR - 1, k)

            @block.tensor
            def _(pe):
                T, MM = nc.tensor.transpose, nc.tensor.matmul
                pe.wait_ge(dy_rowed, 1)
                for b in range(HB):
                    mm = T(psA[0:NT, b // 4, b % 4 * 128:(b % 4 + 1) * 128], dy[:, b, :], ident[:, :])
                    if b % 4 == 3:
                        mm.then_inc(dy_turned, 1)
                pe.wait_ge(dyt_ready, 4)
                with pe.Fori(0, NR) as i:
                    for k in range(NS):
                        pe.wait_ge(staged, NS * i + k + 1)
                        for a in range(2):
                            mm = T(psA[0:NT, k, a * 128:(a + 1) * 128], dz[:, k, a, :], ident[:, :])
                        mm.then_inc(dz_turned, 1)
                        pe.wait_ge(added, NS * i + k + 1)
                        pe.wait_ge(loaded[k], 80 * i + 80)
                        MM(psB[0:NT, k, 0:NT], kq[:, k, 0, :], kq[:, k, 1, :], start=True, stop=True).then_inc(s1_done, 1)
                    for k in range(NS):
                        pe.wait_ge(dzt_ready, NS * i + k + 1)
                        pe.wait_ge(s1_ready, NS * i + k + 1)
                        for a in range(2):
                            o = slice(a * 128, (a + 1) * 128)
                            MM(psA[:, k, 256 + a * NT:256 + (a + 1) * NT], dzt[:, k, o], s1[:, k, :], start=True, stop=False)
                            mm = MM(psA[:, k, 256 + a * NT:256 + (a + 1) * NT], M["a0"][:, o], kq[:, k, 2, :], start=False, stop=True)
                        mm.then_inc(z_done, 1)
                    for k in range(NS):
                        pe.wait_ge(hq_ready, NS * i + k + 1)
                        for a in range(2):
                            mm = MM(psB[0:NT, k, 128:128 + NT], hs[:, k, a, :], hq[:, k, a, :], start=a == 0, stop=a == 1)
                        mm.then_inc(s2_done, 1)
                    for k in range(NS):
                        pe.wait_ge(hqc_ready, NS * i + k + 1)
                        pe.wait_ge(s2_ready, NS * i + k + 1)
                        for a in range(2):
                            MM(psB[0:NT, k, 256:256 + DM], hqc[:, k, a, :], M["b0"][:, a, 0, 0:DM], start=a == 0, stop=False)
                        MM(psB[0:NT, k, 256:256 + DM], s2[:, k, :], dyt[:, bass.ds(2 * i + k // 2, 1), k % 2 * DM:(k % 2 + 1) * DM].rearrange("p b d -> p (b d)"),
                           start=False, stop=True).then_inc(out_done, 1)

            @block.scalar
            def _(act):
                with act.Fori(0, NR) as i:
                    for k in range(NS):
                        act.wait_ge(dz_turned, NS * i + k + 1)
                        nc.scalar.activation(dzt[:, k, :], psA[0:NT, k, 0:FH], ACT.Copy).then_inc(dzt_ready, 1)
                    for k in range(NS):
                        act.wait_ge(z_done, NS * i + k + 1)
                        nc.scalar.activation(sg[:, k, :, :], zq(k), ACT.Sigmoid).then_inc(sg_ready, 1)

            @block.vector
            def _(dve):
                V = nc.vector
                V.sem_inc(added, NS)
                dve.wait_ge(hist_in, 48)
                for j in range(4):
                    dve.wait_ge(dy_turned, j + 1)
                    V.tensor_copy(dyt[:, 4 * j:4 * j + 4, :].rearrange("p b c -> p (b c)"), psA[0:NT, j, :]).then_inc(dyt_ready, 1)
                with dve.Fori(0, NR) as i:
                    for k in range(NS):
                        dve.wait_ge(s1_done, NS * i + k + 1)
                        V.tensor_tensor(s1[:, k, :], psB[0:NT, k, 0:NT], w[:, k, :], ALU.mult).then_inc(s1_ready, 1)
                    for k in range(NS):
                        dve.wait_ge(sg_ready, NS * i + k + 1)
                        V.tensor_tensor(hq[:, k, :, :], zq(k), sg[:, k, :, :], ALU.mult).then_inc(hq_ready, 1)
                    for k in range(NS):
                        dve.wait_ge(s2_done, NS * i + k + 1)
                        V.tensor_tensor(s2[:, k, :], psB[0:NT, k, 128:128 + NT], w[:, k, :], ALU.mult).then_inc(s2_ready, 1)
                    for k in range(NS):
                        dve.wait_ge(out_done, NS * i + k + 1)
                        row = H[:, bass.ds(batch(i, k), 1), :].rearrange("t b d -> t (b d)")
                        V.tensor_tensor(row, row, psB[0:NT, k, 256:256 + DM], ALU.add).then_inc(added, 1)
                dve.wait_ge(added, NB + NS)


def early_fusion(nc, out, A):
    with ExitStack() as ctx:
        sb = lambda n, sh: ctx.enter_context(nc.sbuf_tensor(n, sh, F32))
        ident = sb("ident", [128, 128])
        moved = ctx.enter_context(nc.semaphore("moved"))
        image = nc.dram_tensor("image_rows", [NB, S, S], F32).ap()
        with nc.Block() as block:
            @block.sync
            def _(sp):
                sp.dma_start(ident[:, :], A["c_ident"]).then_inc(moved, 16)
                sp.wait_ge(moved, 16)

        t = lambda n: A["L0_tok_" + n]
        image_network(nc, A["x"], image, ident, {n: A["c_" + n] for n in ("d1", "d2", "e1", "e2")},
                      t("fc0_w"), t("fc0_b"), [t(f"sw{i}") for i in range(NL)], [t(f"cw{i}") for i in range(NL)],
                      [t(f"cb{i}") for i in range(NL)], t("fc1_w"), t("fc1_b"), t("fc2_w"), t("fc2_b"))

        H_room = sb("H", [128, NB, DM])
        H = H_room[0:NT]
        ln = layernorm_semaphores(nc, ctx)
        with nc.Block() as block:
            @block.sync
            def _(sp):
                sp.dma_start(H[0:S, :, :], image.rearrange("b t d -> t b d")).then_inc(moved, 16)
                sp.dma_start(H[S:NT, :, :], A["txt"].rearrange("b t d -> t b d")).then_inc(moved, 16)
                sp.wait_ge(moved, 48)

        def normed(tag, stage):
            XT = stage.enter_context(nc.sbuf_tensor("XT_" + tag, [DM, TOK], F32))
            with ExitStack() as own:
                XN, squares = (own.enter_context(nc.sbuf_tensor(n + tag, [NT, NB, DM], F32)) for n in ("XN_", "squares_"))
                layernorm_transposed(nc, ln, "abcd".index(tag), H, XN, squares, XT, ident)
            return XT

        with ExitStack() as stage:
            XT = normed("a", stage)
            linear_attention(nc, H, XT, ident, A["c_rows"], A["L0_attn_Q"], A["L0_attn_E"])
        with ExitStack() as stage:
            XT = normed("b", stage)
            f = lambda n: A["L0_ffn_" + n]
            top_two_experts(nc, H, XT, f("router_w1"), f("router_b1"), f("router_w2"), f("router_b2"), f("expert_w1"), f("expert_b1"),
                            f("expert_w2"), f("expert_b2"), f("expert_w3"), f("expert_b3"))
        with ExitStack() as mem:
            M = memory_tensors(nc, mem)
            m = lambda n: A["L1_attn_" + n]
            with ExitStack() as stage:
                XT = normed("c", stage)
                memory_setup(nc, M, H, XT, ident, A["c_inject"], m("W_fused"), m("W0"), m("W1"), m("P0"), m("P1"))
            msb = lambda n, sh: mem.enter_context(nc.sbuf_tensor(n, sh, F32))
            hist_y = msb("hist_y", [128, NCH, HB, NC])
            memory_scan(nc, M, H_room, hist_y, ident, A["c_cols"], A["c_rows"], A["c_own"])
            memory_outputs(nc, M, H, hist_y, ident)
        with ExitStack() as stage:
            XT = normed("d", stage)
            w = lambda n: A["L1_ffn_" + n]
            best_expert(nc, H, XT, ident, w("gate_w"), w("gate_b"), w("w1"), w("b1"), w("w2"), w("b2"))
        with nc.Block() as block:
            @block.sync
            def _(sp):
                sp.dma_start(out.rearrange("b t d -> t b d"), H[:, :, :]).then_inc(moved, 16)
                sp.wait_ge(moved, 64)


def shape_constants():
    half = np.zeros((128, 2, 128), np.float32)
    half[:, 0, 0:64] = 1.0
    half[:, 1, 64:128] = 1.0
    return dict(spectral_constants(), ident=np.eye(128, dtype=np.float32), inject=(-2 * MAX_LR * np.eye(NT)).astype(np.float32),
                cols=half, rows=np.ascontiguousarray(half.transpose(2, 1, 0)), own=np.repeat(np.eye(QB, dtype=np.float32), NC, axis=0))


_INS = ['x', 'txt', 'L0_tok_fc0_w', 'L0_tok_fc0_b', 'L0_tok_sw0', 'L0_tok_cw0', 'L0_tok_cb0', 'L0_tok_sw1', 'L0_tok_cw1', 'L0_tok_cb1',
        'L0_tok_sw2', 'L0_tok_cw2', 'L0_tok_cb2', 'L0_tok_sw3', 'L0_tok_cw3', 'L0_tok_cb3', 'L0_tok_fc1_w', 'L0_tok_fc1_b', 'L0_tok_fc2_w',
        'L0_tok_fc2_b', 'L0_attn_Q', 'L0_attn_E', 'L0_ffn_router_w1', 'L0_ffn_router_b1', 'L0_ffn_router_w2', 'L0_ffn_router_b2',
        'L0_ffn_expert_w1', 'L0_ffn_expert_b1', 'L0_ffn_expert_w2', 'L0_ffn_expert_b2', 'L0_ffn_expert_w3', 'L0_ffn_expert_b3',
        'L1_attn_W_fused', 'L1_attn_W0', 'L1_attn_W1', 'L1_attn_P0', 'L1_attn_P1', 'L1_ffn_gate_w', 'L1_ffn_gate_b', 'L1_ffn_w1',
        'L1_ffn_b1', 'L1_ffn_w2', 'L1_ffn_b2']


def kernel(**inputs):
    import concourse.bacc as bacc
    from concourse.bass_utils import run_bass_kernel_spmd

    nc = bacc.Bacc("TRN2", target_bir_lowering=False, num_devices=1)
    arrays, A = {}, {}
    for name, a in [*((n, inputs[n]) for n in _INS), *(("c_" + n, a) for n, a in shape_constants().items())]:
        a = np.ascontiguousarray(a)
        arrays[f"in_{name}_dram"] = a
        A[name] = nc.dram_tensor(f"in_{name}_dram", a.shape, mybir.dt.from_np(a.dtype), kind="ExternalInput").ap()
    out = nc.dram_tensor("out_0_dram", (NB, NT, DM), F32, kind="ExternalOutput").ap()
    early_fusion(nc, out, A)
    r = run_bass_kernel_spmd(nc, [arrays], core_ids=[0])
    return r.results[0]["out_0_dram"]
```

```python
from contextlib import ExitStack

import numpy as np
import concourse.bass as bass
from concourse import mybir

F32 = mybir.dt.float32
ALU = mybir.AluOpType
ACT = mybir.ActivationFunctionType
AX = mybir.AxisListType

NB = 32
NT = 96
DM = 64
TOK = NB * NT
EPS = 1e-5
MAX_LR = 0.1


def bc(ap, *shape):
    return ap.broadcast_to(list(shape))


class Steps:

    def __init__(self, eng, sem, base=0):
        self.eng, self.sem, self.base, self.n = eng, sem, base, 0

    def mark(self, ins):
        ins.then_inc(self.sem, 1)
        self.n += 1
        return self.n

    def link(self, ins):
        self.mark(ins)
        self.eng.wait_ge(self.sem, self.base + self.n)


C = 32
S = 64
MO = 20
KG, KJ = 5, 4
NL = 4
NGRP = 4


def spectral_constants():
    n = np.arange(S)
    kx = np.array([KG * j + g for g in range(KG) for j in range(KJ)])
    ky = np.arange(MO)
    scale = 1.0 / np.sqrt(S)
    cx, sx = (f(2 * np.pi * np.outer(n, kx) / S) * scale for f in (np.cos, np.sin))
    cy, sy = (f(2 * np.pi * np.outer(n, ky) / S) * scale for f in (np.cos, np.sin))
    d1 = np.zeros((2, S, 2, 2, MO))
    d2 = np.zeros((2, 2, S, MO, 2, 2))
    e1 = np.zeros((2, MO, 2, 2, S))
    e2 = np.zeros((128, 2, S))
    twice = np.where(ky == 0, 1.0, 2.0)[:, None]
    ck, sk = (f(2 * np.pi * np.outer(ky, n) / S) * scale for f in (np.cos, np.sin))
    for b in range(2):
        d1[b, :, b, 0], d1[b, :, b, 1] = cx, -sx
        d2[0, b, :, :, b, 0], d2[0, b, :, :, b, 1] = cy, -sy
        d2[1, b, :, :, b, 0], d2[1, b, :, :, b, 1] = sy, cy
        e1[b, :, 0, b, :], e1[b, :, 1, b, :] = twice * ck, -twice * sk
        e2[b * 40:b * 40 + 20, b], e2[b * 40 + 20:b * 40 + 40, b] = ck, -sk
    e2[96] = 1.0
    f = lambda a, *s: np.ascontiguousarray(a.reshape(s).astype(np.float32))
    return dict(d1=f(d1, 128, 80), d2=f(d2.reshape(2, 128, 80).transpose(1, 0, 2), 128, 160), e1=f(e1, 80, 128), e2=f(e2, 128, 128))


def image_network(nc, x, h_out, ident, consts, fc0_w, fc0_b, sw, cw, cb, fc1_w, fc1_b, fc2_w, fc2_b):
    RING = 6
    PH = 8
    with ExitStack() as ctx:
        sb = lambda n, sh: ctx.enter_context(nc.sbuf_tensor("im_" + n, sh, F32))
        sem = lambda n: ctx.enter_context(nc.semaphore("im_" + n))
        a = sb("a", [128, NGRP, 2 * S * C])
        spec = sb("spec", [128, KG * MO, 32])
        mixed = sb("mixed", [128, KG, NGRP, 2, 2, 80])
        half_t = sb("half_t", [128, 2, 2560])
        u = sb("u", [97, 2 * S * C])
        wbd = sb("wbd", [128, 128, KG * MO])
        chan = sb("chan", [128, 2, 512])
        xi = sb("xi", [128, 2, 2, 192])
        xt = sb("xt", [97, 4, 128])
        fc0 = sb("fc0", [97, 1024])
        d1, d2, e1, e2 = sb("d1", [128, 80]), sb("d2", [128, 2, 80]), sb("e1", [80, 128]), sb("e2", [128, 128])
        cwn, cwt = sb("cwn", [128, 128]), sb("cwt", [128, NL, 128])
        fc1 = sb("fc1", [128, 2, 128])
        fc1b, fc2, fc2b = sb("fc1b", [128, 1]), sb("fc2", [128, 2]), sb("fc2b", [128, 1])
        ho = sb("ho", [128, 2, S])
        gl = half_t[:, :, 0:512]
        ring = ctx.enter_context(nc.psum_tensor("im_ring", [128, RING, 512], F32))
        acc = ctx.enter_context(nc.psum_tensor("im_acc", [128, 2, 512], F32))
        zeroed, loaded, cw_in, cw_turned, cw_ready = sem("zeroed"), sem("loaded"), sem("cw_in"), sem("cw_turned"), sem("cw_ready")
        with nc.Block() as block:
            @block.gpsimd
            def _(pool):
                nc.gpsimd.memset(wbd[:, :, :], 0.0).then_inc(zeroed, 1)

            @block.vector
            def _(dve):
                for t in (u[64:97, :], xt[:, :, :], fc0[:, :], cwn[:, :], fc1[:, :, :], fc2[:, :]):
                    nc.vector.memset(t, 0.0).then_inc(zeroed, 1)
                dve.wait_ge(zeroed, 7)
                nc.vector.memset(xt[96:97, :, :], 1.0).then_inc(zeroed, 1)
                for l in range(NL):
                    dve.wait_ge(cw_turned, l + 1)
                    nc.vector.tensor_copy(cwt[:, l, :], acc[:, l % 2, 0:128]).then_inc(cw_ready, 1)
                dve.wait_ge(cw_ready, NL)
                dve.wait_ge(zeroed, 8)

            @block.tensor
            def _(pe):
                for l in range(NL):
                    pe.wait_ge(cw_in, 64 * (l + 1))
                    if l >= 2:
                        pe.wait_ge(cw_ready, l - 1)
                    nc.tensor.transpose(acc[:, l % 2, 0:128], cwn[:, :], ident[:, :]).then_inc(cw_turned, 1)

            @block.sync
            def _(sp):
                sp.wait_ge(zeroed, 7)
                for l in range(NL):
                    if l:
                        sp.wait_ge(cw_turned, l)
                    for k in range(4):
                        sp.dma_start(cwn[k * C:(k + 1) * C, k * C:(k + 1) * C], cw[l]).then_inc(cw_in, 16)

            @block.scalar
            def _(act):
                n = 0
                act.wait_ge(zeroed, 7)
                with nc.allow_non_contiguous_dma(reason="small weights"):
                    for dst, src in ((d1[:, :], consts["d1"]), (d2[:, :, :].rearrange("p a c -> p (a c)"), consts["d2"]), (e1[:, :], consts["e1"]), (e2[:, :], consts["e2"]),
                                     (fc0[96:97, :].rearrange("p (w c) -> p w c", c=C), fc0_b.rearrange("(a b c) -> a b c", a=1, b=1).broadcast_to([1, 32, C])),
                                     (fc2b[:, :], fc2_b.rearrange("(a b) -> a b", a=1).broadcast_to([128, 1]))):
                        act.dma_start(dst, src).then_inc(loaded, 16)
                        n += 1
                    for k in range(4):
                        act.dma_start(fc1[k * C:(k + 1) * C, k // 2, k % 2 * 64:(k % 2 + 1) * 64], fc1_w).then_inc(loaded, 16)
                    for k in range(2):
                        act.dma_start(fc1b[k * 64:(k + 1) * 64, :], fc1_b.rearrange("(p a) -> p a", a=1)).then_inc(loaded, 16)
                        act.dma_start(fc2[k * 64:(k + 1) * 64, k:k + 1], fc2_w).then_inc(loaded, 16)
                    for k in range(32):
                        act.dma_start(fc0[3 * k:3 * k + 3, k * C:(k + 1) * C], fc0_w).then_inc(loaded, 16)
                    n += 4 + 4 + 32
                act.wait_ge(loaded, 16 * n)

        filled, drained = sem("filled"), sem("drained")
        acc_full, acc_read = sem("acc_full"), sem("acc_read")
        w_in, bias_in, xi_in = sem("w_in"), sem("bias_in"), [sem("xi_in0"), sem("xi_in1")]
        ho_ready, ho_stored = sem("ho_ready"), sem("ho_stored")
        FC0_FILLS, LAYER_FILLS, FC_FILLS = 4 * 9, 4 * 8 + 10 + 4 * 21, 4 * 10
        HALF_FILLS = FC0_FILLS + NL * LAYER_FILLS + FC_FILLS
        LAYER_ACC, HALF_ACC = 4 * PH, NL * 4 * PH + 4 * PH * 2
        assert LAYER_FILLS % RING == 0
        MIXED_AT = 4 * 8 + 10
        img = x.rearrange("(n b c) h w k -> n b h c (w k)", b=2, c=2)
        out_img = h_out.rearrange("(n b c) h w -> n b h c w", b=2, c=2)

        class Fills:
            def __init__(self, start, base=0):
                self.n, self.bank, self.base = start, start % RING, base
            def next(self):
                n, bank = self.n, self.bank
                self.n, self.bank = n + 1, (bank + 1) % RING
                return self.base + n, bank

        with nc.Block() as block:
            @block.sync
            def _(sp):
                for half in range(2):
                    base = half * HALF_FILLS
                    for l in range(NL):
                        r = NL * half + l
                        if r:
                            sp.wait_ge(filled, base + FC0_FILLS + (l - 1) * LAYER_FILLS + MIXED_AT if l else base - FC_FILLS - LAYER_FILLS + MIXED_AT)
                        for j in range(KJ):
                            o = slice(j * C, (j + 1) * C)
                            sp.dma_start(wbd[o, o, :], sw[l][:, :, KG * j:KG * (j + 1), :].rearrange("i o x y -> i o (x y)")).then_inc(w_in, 16)
                        if r:
                            sp.wait_ge(acc_full, half * HALF_ACC + l * LAYER_ACC if l else half * HALF_ACC - 4 * PH * 2)
                        sp.dma_start(u[96:97, :].rearrange("p (w c) -> p w c", c=C),
                                     cb[l].rearrange("(a b c) -> a b c", a=1, b=1).broadcast_to([1, 2 * S, C])).then_inc(bias_in, 16)

            @block.gpsimd
            def _(pool):
                def load_image(n):
                    if n >= 2:
                        pool.wait_ge(filled, (n - 2) // NGRP * HALF_FILLS + (n - 2) % NGRP * 9 + 1)
                    for b2 in range(2):
                        pool.dma_start(xi[b2 * S:(b2 + 1) * S, n % 2, :, :], img[n, b2]).then_inc(xi_in[n % 2], 16)

                def store_result(n):
                    pool.wait_ge(ho_ready, n + 1)
                    for b2 in range(2):
                        pool.dma_start(out_img[n, b2], ho[b2 * S:(b2 + 1) * S, :, :]).then_inc(ho_stored, 16)

                for n in range(NGRP + 2):
                    load_image(n)
                for n in range(NGRP):
                    store_result(n)
                for n in range(NGRP + 2, 2 * NGRP):
                    load_image(n)
                for n in range(NGRP, 2 * NGRP):
                    store_result(n)
                pool.wait_ge(ho_stored, 32 * 2 * NGRP)

            def second_layer(pe, MM, item, start):
                n, p, v = item
                if p + v == 0:
                    pe.wait_ge(drained, start + 4 + 1)
                pe.wait_ge(acc_read, n + 3)
                for m in range(4):
                    col = p * 16 + m * 4 + v * 2
                    mm = MM(ring[:, (start + 4) % RING, col:col + 2], gl[:, v, m * 128:(m + 1) * 128], fc2[:, :], start=True, stop=True)
                return mm

            @block.tensor
            def _(pe):
                T, MM = nc.tensor.transpose, nc.tensor.matmul

                def fill(f):
                    n, bank = f.next()
                    pe.wait_ge(drained, n + 1)
                    return ring[:, bank, :]

                def have(n):
                    pe.wait_ge(drained, n + RING)

                def input_layer(f, half):
                    for g in range(NGRP):
                        n = half * NGRP + g
                        pe.wait_ge(xi_in[n % 2], 32 * (n // 2 + 1))
                        ps = fill(f)
                        for k in range(4):
                            mm = T(ps[0:96, k * 128:(k + 1) * 128], xi[:, n % 2, k // 2, k % 2 * 96:(k % 2 + 1) * 96], ident[:, :])
                        mm.then_inc(filled, 1)
                        have(f.n)
                        for p in range(PH):
                            ps = fill(f)
                            MM(ps, xt[:, p // 2, :], fc0[:, p % 2 * 512:(p % 2 + 1) * 512], start=True, stop=True).then_inc(filled, 1)

                def rows_transform(f, g):
                    for q in range(0, C, 6):
                        ps = fill(f)
                        for i, c in enumerate(range(q, min(q + 6, C))):
                            mm = MM(ps[:, i * 80:(i + 1) * 80], a[:, g, c:2 * S * C:C], d1[:, :], start=True, stop=True)
                        mm.then_inc(filled, 1)

                def columns_transform(f, g):
                    for b2 in range(2):
                        ps = fill(f)
                        for k in range(KG):
                            for r in range(2):
                                o = (b2 * 2 + r) * 640 + k * 128
                                mm = MM(ps[:, k * 80:(k + 1) * 80], half_t[:, g % 2, o:o + 128], d2[:, r, :], start=r == 0, stop=r == 1)
                        mm.then_inc(filled, 1)

                def mixing(f, r):
                    pe.wait_ge(w_in, 64 * r + 64)
                    for k in range(KG):
                        for y in range(0, MO, 10):
                            ps = fill(f)[:, 0:320].rearrange("p (b y r) -> p b y r", b=16, r=2)
                            for i in range(10):
                                m = k * MO + y + i
                                mm = MM(ps[:, :, i, :], wbd[:, :, m], spec[:, m, :].rearrange("p (b r) -> p b r", r=2), start=True, stop=True)
                            mm.then_inc(filled, 1)

                def turn_mixed(f, g):
                    for k in range(KG):
                        ps = fill(f)
                        for q in range(4):
                            mm = T(ps[0:80, q * 128:(q + 1) * 128], mixed[:, k, g, q // 2, q % 2, :], ident[:, :])
                        mm.then_inc(filled, 1)

                def columns_inverse(f, g):
                    for q in range(0, C, 4):
                        ps = fill(f)
                        for i in range(4):
                            mm = MM(ps[0:80, i * 128:(i + 1) * 128], half_t[0:80, g % 2, q + i:2560:C], e1[:, :], start=True, stop=True)
                        mm.then_inc(filled, 1)

                def turn_activations(f, g, p):
                    ps = fill(f)
                    for m in range(4):
                        o = p * 512 + m * 128
                        mm = T(ps[:, m * 128:(m + 1) * 128], a[:, g, o:o + 128], ident[:, :])
                    mm.then_inc(filled, 1)
                    return f.n

                for half in range(2):
                    at, acc_at = half * HALF_FILLS, half * HALF_ACC
                    if half == 0:
                        pe.sem_inc(drained, RING)
                        pe.sem_inc(acc_read, 2)
                    input_layer(Fills(at), half)
                    at += FC0_FILLS
                    with pe.Fori(0, NL) as l:
                        f = Fills(at, l * LAYER_FILLS)
                        first, acc_base = f.n, acc_at + l * LAYER_ACC
                        pe.wait_ge(acc_read, acc_base + 2)
                        have(f.base + f.n)
                        marks = {}
                        for g in range(NGRP):
                            rows_transform(f, g)
                            marks[g] = f.n
                            if g:
                                have(f.base + marks[g - 1])
                                columns_transform(f, g - 1)
                        have(f.base + marks[NGRP - 1])
                        columns_transform(f, NGRP - 1)
                        have(f.base + f.n)
                        mixing(f, NL * half + l)
                        have(f.base + f.n)
                        turn_mixed(f, 0)
                        for g in range(NGRP):
                            have(f.base + f.n)
                            columns_inverse(f, g)
                            if g + 1 < NGRP:
                                turn_mixed(f, g + 1)
                            chan_at = turn_activations(f, g, 0)
                            for p in range(PH):
                                n = acc_base + g * PH + p
                                nxt = turn_activations(f, g, p + 1) if p + 1 < PH else None
                                have(f.base + chan_at)
                                if g + p == 0:
                                    pe.wait_ge(bias_in, 16 * (NL * half + l) + 16)
                                pe.wait_ge(acc_read, n + 1)
                                MM(acc[:, p % 2, :], e2[0:97, :], u[:, p * 512:(p + 1) * 512], start=True, stop=True, skip_group_check=True)
                                for m in range(4):
                                    mm = MM(acc[:, p % 2, m * 128:(m + 1) * 128], chan[:, p % 2, m * 128:(m + 1) * 128],
                                            cwt[:, bass.ds(l, 1), :].rearrange("p a c -> p (a c)"), start=False, stop=True, skip_group_check=True)
                                mm.then_inc(acc_full, 1)
                                chan_at = nxt
                        assert f.n == first + LAYER_FILLS
                    at += NL * LAYER_FILLS
                    acc_at += NL * LAYER_ACC
                    pe.wait_ge(acc_read, acc_at + 2)
                    f = Fills(at)
                    for g in range(NGRP):
                        for q in range(2):
                            start = f.n
                            turn_activations(f, g, 4 * q)
                            pend = []
                            for p in range(4):
                                if p < 3:
                                    turn_activations(f, g, 4 * q + p + 1)
                                have(start + p + 1)
                                for v in range(2):
                                    n = acc_at + ((g * 2 + q) * 4 + p) * 2 + v
                                    pe.wait_ge(acc_read, n + 1)
                                    MM(acc[:, v, :], fc1[:, v, :], chan[:, p % 2, :], start=True, stop=True).then_inc(acc_full, 1)
                                    pend.append((n, p, v))
                                    if len(pend) == 2:
                                        second_layer(pe, MM, pend.pop(0), start)
                            second_layer(pe, MM, pend.pop(0), start).then_inc(filled, 1)
                            f.next()

            @block.vector
            def _(dve):
                V = nc.vector

                def drain(f):
                    n, bank = f.next()
                    dve.wait_ge(filled, n + 1)
                    return ring[:, bank, :]

                for half in range(2):
                    at = half * HALF_FILLS
                    f = Fills(at)
                    for g in range(NGRP):
                        V.tensor_copy(xt[0:96, :, :].rearrange("p a c -> p (a c)"), drain(f)[0:96, :]).then_inc(drained, 1)
                        for p in range(PH):
                            V.tensor_copy(a[:, g, p * 512:(p + 1) * 512], drain(f)).then_inc(drained, 1)
                    at += FC0_FILLS
                    with dve.Fori(0, NL) as l:
                        f = Fills(at, l * LAYER_FILLS)

                        def rows(g):
                            for q in range(0, C, 6):
                                w = min(6, C - q)
                                src = drain(f)[:, 0:w * 80].rearrange("p (c n) -> p c n", n=80)
                                V.tensor_copy(half_t[:, g % 2, :].rearrange("p (n c) -> p c n", c=C)[:, q:q + w, :], src).then_inc(drained, 1)

                        def columns(g):
                            for b2 in range(2):
                                o = (g * 2 + b2) * 4
                                V.tensor_copy(spec[:, :, o:o + 4], drain(f)[:, 0:400].rearrange("p (m n) -> p m n", n=4)).then_inc(drained, 1)

                        for g in range(NGRP):
                            rows(g)
                            if g:
                                columns(g - 1)
                        columns(NGRP - 1)
                        for k in range(KG):
                            for y in range(0, MO, 10):
                                src = drain(f)[:, 0:320].rearrange("p (n b m) -> p n b m", n=8, b=2)
                                dst = mixed[:, k, :, :, :, :].rearrange("p g b r (c y) -> p (g b) r c y", c=2)
                                V.tensor_copy(dst[:, :, 0, :, 2 * y:2 * y + 20], src)
                                V.tensor_copy(dst[:, :, 1, :, 2 * y:2 * y + 20:2], src[:, :, :, 1:20:2])
                                V.tensor_scalar(dst[:, :, 1, :, 2 * y + 1:2 * y + 20:2], src[:, :, :, 0:20:2], -1.0, None, ALU.mult).then_inc(drained, 1)

                        def turned(g):
                            for k in range(KG):
                                src = drain(f)[0:80, :].rearrange("p (n o) -> p n o", o=C)
                                V.tensor_copy(half_t[0:80, g % 2, :].rearrange("p (n k o) -> p n k o", k=KG, o=C)[:, :, k, :], src).then_inc(drained, 1)

                        turned(0)
                        for g in range(NGRP):
                            for q in range(0, C, 4):
                                src = drain(f)[0:80, :].rearrange("p (o w) -> p o w", o=4)
                                V.tensor_copy(u[0:80, :].rearrange("p (w o) -> p o w", o=C)[:, q:q + 4, :], src).then_inc(drained, 1)
                            if g + 1 < NGRP:
                                turned(g + 1)
                            for p in range(PH):
                                V.tensor_copy(chan[:, p % 2, :], drain(f)).then_inc(drained, 1)
                    at += NL * LAYER_FILLS
                    f = Fills(at)
                    for g in range(NGRP):
                        for q in range(2):
                            for p in range(4):
                                V.tensor_copy(chan[:, p % 2, :], drain(f)).then_inc(drained, 1)
                            n = half * NGRP + g
                            if q == 0 and n >= 1:
                                dve.wait_ge(ho_stored, 32 * n)
                            V.tensor_scalar(ho[:, q, :], drain(f)[:, 0:S], fc2b[:, 0:1], None, ALU.add).then_inc(drained, 1)
                        dve.wait_ge(drained, f.n + RING)
                        V.sem_inc(ho_ready, 1)

            @block.scalar
            def _(act):
                for half in range(2):
                    with act.Fori(0, NL) as l:
                        for g in range(NGRP):
                            for p in range(PH):
                                act.wait_ge(acc_full, half * HALF_ACC + l * LAYER_ACC + g * PH + p + 1)
                                nc.scalar.activation(a[:, g, p * 512:(p + 1) * 512], acc[:, p % 2, :], ACT.Gelu).then_inc(acc_read, 1)
                    for n in range(4 * PH * 2):
                        act.wait_ge(acc_full, half * HALF_ACC + NL * LAYER_ACC + n + 1)
                        nc.scalar.activation(gl[:, n % 2, :], acc[:, n % 2, :], ACT.Gelu, bias=fc1b[:, 0:1]).then_inc(acc_read, 1)


def layernorm_semaphores(nc, ctx):
    return {n: ctx.enter_context(nc.semaphore("ln_" + n))
            for n in ("step", "var_ready", "root_ready", "normed", "turned", "copied_a", "copied_v")}


def layernorm_transposed(nc, sems, turn, H, XN, sq, XT, ident):
    G = 4
    with ExitStack() as ctx:
        st = ctx.enter_context(nc.sbuf_tensor(f"ln_st{turn}", [NT, 8, NB], F32))
        ps = ctx.enter_context(nc.psum_tensor(f"ln_ps{turn}", [DM, 4, 512], F32))
        step, var_ready, root_ready, normed = sems["step"], sems["var_ready"], sems["root_ready"], sems["normed"]
        turned, copied_a, copied_v = sems["turned"], sems["copied_a"], sems["copied_v"]
        LINKS, FILLS, HALF = 10, NB // G, NB // G // 2
        sums, mean, var, root, inv, other = (st[:, i, :] for i in range(6))
        wide = lambda s: bc(s.unsqueeze(2), NT, NB, DM)
        with nc.Block() as block:
            @block.vector
            def _(dve):
                s = Steps(dve, step, turn * LINKS)
                s.link(nc.vector.reduce_sum(sums, H[:, :, :], AX.X))
                s.link(nc.vector.tensor_scalar(mean, sums, 1.0 / DM, None, ALU.mult))
                s.link(nc.vector.tensor_tensor(XN[:, :, :], H[:, :, :], wide(mean), ALU.subtract))
                s.link(nc.vector.tensor_tensor(sq[:, :, :], XN[:, :, :], XN[:, :, :], ALU.mult))
                s.link(nc.vector.reduce_sum(sums, sq[:, :, :], AX.X))
                nc.vector.tensor_scalar(var, sums, 1.0 / DM, EPS, ALU.mult, ALU.add).then_inc(var_ready, 1)
                dve.wait_ge(var_ready, turn + 1)
                dve.wait_ge(root_ready, turn + 1)
                s.link(nc.vector.reciprocal(inv, root))
                s.link(nc.vector.tensor_tensor(other, var, inv, ALU.mult))
                s.link(nc.vector.tensor_tensor(sums, other, root, ALU.add))
                s.link(nc.vector.tensor_scalar(other, sums, 0.5, None, ALU.mult))
                s.link(nc.vector.reciprocal(inv, other))
                nc.vector.tensor_tensor(XN[:, :, :], XN[:, :, :], wide(inv), ALU.mult).then_inc(normed, 1)
                for g in range(1, NB // G, 2):
                    dve.wait_ge(turned, turn * FILLS + g + 1)
                    nc.vector.tensor_copy(XT[:, g * G * NT:(g + 1) * G * NT], ps[:, g % 4, 0:G * NT]).then_inc(copied_v, 1)
                dve.wait_ge(copied_v, (turn + 1) * HALF)
                assert s.n == LINKS

            @block.scalar
            def _(act):
                act.wait_ge(var_ready, turn + 1)
                nc.scalar.activation(root, var, ACT.Sqrt).then_inc(root_ready, 1)
                for g in range(0, NB // G, 2):
                    act.wait_ge(turned, turn * FILLS + g + 1)
                    nc.scalar.activation(XT[:, g * G * NT:(g + 1) * G * NT], ps[:, g % 4, 0:G * NT], ACT.Copy).then_inc(copied_a, 1)
                act.wait_ge(copied_a, (turn + 1) * HALF)

            @block.tensor
            def _(pe):
                pe.wait_ge(normed, turn + 1)
                for g in range(NB // G):
                    if g >= 4:
                        pe.wait_ge(copied_a if g % 2 == 0 else copied_v, turn * HALF + (g - 4) // 2 + 1)
                    for j in range(G):
                        mm = nc.tensor.transpose(ps[:, g % 4, j * NT:(j + 1) * NT], XN[:, g * G + j, :], ident[0:NT, 0:NT])
                    mm.then_inc(turned, 1)


def linear_attention(nc, H, XT, ident, rows_in, Q, E):
    NH = 8
    with ExitStack() as ctx:
        sb = lambda n, sh: ctx.enter_context(nc.sbuf_tensor(n, sh, F32))
        pb = lambda n, sh: ctx.enter_context(nc.psum_tensor(n, sh, F32))
        sem = lambda n: ctx.enter_context(nc.semaphore(n))
        q_w = sb("at_q_w", [DM, NH, DM])
        e_w = sb("at_e_w", [DM, NH, DM])
        e_t = sb("at_e_t", [DM, NH, DM])
        causal = sb("at_causal", [NT, NT])
        s_t = sb("at_s_t", [128, 2, 2, NT])
        xt_2 = sb("at_xt_2", [128, TOK])
        half = sb("at_half", [128, 2])
        es = sb("at_es", [NT, 2, NH * DM])
        qs = sb("at_qs", [128, NH // 2, TOK])
        om = sb("at_om", [NT, 2, NH, NT])
        psE = pb("at_psE", [NT, 2, 512])
        psO = pb("at_psO", [128, 2, 2, 512])
        psR = pb("at_psR", [NT, 2, 512])
        HH = NH // 2 * NT
        PIECES = TOK // 512
        NQS = NH // 2 * PIECES
        loaded, ones, mask_ready = sem("at_loaded"), sem("at_ones"), sem("at_mask_ready")
        e_turned, e_ready = sem("at_e_turned"), sem("at_e_ready")
        staged, es_done, es_ready = sem("at_staged"), sem("at_es_done"), sem("at_es_ready")
        qs_done, qs_act, qs_dve = sem("at_qs_done"), sem("at_qs_act"), sem("at_qs_dve")
        om_done, om_ready, r_done, r_added = sem("at_om_done"), sem("at_om_ready"), sem("at_r_done"), sem("at_r_added")
        bank = lambda n: psO[:, n % 4 // 2, n % 2, :]
        piece = lambda n: qs[:, n // PIECES, n % PIECES * 512:(n % PIECES + 1) * 512]
        with nc.Block() as block:
            @block.sync
            def _(sp):
                sp.dma_start(q_w[:, :, :], Q.rearrange("h i j -> i h j")).then_inc(loaded, 16)
                sp.dma_start(e_w[:, :, :], E.rearrange("h i j -> i h j")).then_inc(loaded, 16)
                for k in range(2):
                    sp.dma_start(xt_2[k * DM:(k + 1) * DM, :], XT[:, :]).then_inc(loaded, 16)
                with nc.allow_non_contiguous_dma(reason="a column"):
                    sp.dma_start(half[:, :], rows_in[:, :, 0:1].rearrange("k a m -> k (a m)")).then_inc(loaded, 16)

            @block.gpsimd
            def _(pool):
                P = nc.gpsimd

                def stage(k, n):
                    P.tensor_tensor(s_t[:, k, :, :], bc(xt_2[:, bass.ds(n * NT, NT)].unsqueeze(1), 128, 2, NT),
                                    bc(half[:, :].unsqueeze(2), 128, 2, NT), ALU.mult).then_inc(staged, 1)

                P.memset(causal[:, :], 1.0).then_inc(ones, 1)
                pool.wait_ge(ones, 1)
                P.affine_select(out=causal[:, :], in_=causal[:, :], compare_op=ALU.is_ge, fill=0.0,
                                base=0, pattern=[[1, NT]], channel_multiplier=-1).then_inc(mask_ready, 1)
                pool.wait_ge(mask_ready, 1)
                pool.wait_ge(loaded, 80)
                for k in range(2):
                    stage(k, k)
                with pool.Fori(0, NB // 2 - 1) as p:
                    for k in range(2):
                        pool.wait_ge(om_done, 2 * p + k + 1)
                        stage(k, 2 * p + 2 + k)

            @block.tensor
            def _(pe):
                MM = nc.tensor.matmul
                pe.sem_inc(r_done, 2)
                pe.wait_ge(loaded, 80)
                for h in range(NH):
                    mm = nc.tensor.transpose(psR[0:DM, 0, h * DM:(h + 1) * DM], e_w[:, h, :], ident[0:DM, 0:DM])
                mm.then_inc(e_turned, 1)
                for n in range(NQS):
                    if n >= 4:
                        pe.wait_ge((qs_act, qs_dve)[n % 2], (n - 4) // 2 + 1)
                    MM(bank(n), q_w[:, n // PIECES * 2:n // PIECES * 2 + 2, :].rearrange("i h j -> i (h j)"), XT[:, n % PIECES * 512:(n % PIECES + 1) * 512],
                       start=True, stop=True).then_inc(qs_done, 1)
                pe.wait_ge(e_ready, 1)
                pe.wait_ge(qs_act, NQS // 2)
                pe.wait_ge(qs_dve, NQS // 2)

                def products(k, n):
                    pe.wait_ge(staged, n + 1)
                    pe.wait_ge(es_ready, n + 1)
                    pe.wait_ge(om_ready, n + 1)
                    MM(psE[:, k, :], s_t[0:DM, k, 0, :], e_t[:, :, :].rearrange("j h i -> j (h i)"), start=True, stop=True).then_inc(es_done, 1)
                    for h2 in range(2):
                        mm = MM(psO[0:NT, k, h2, 0:HH], s_t[:, k, h2, :], qs[:, :, bass.ds(n * NT, NT)], start=True, stop=True)
                    mm.then_inc(om_done, 1)

                def results(k, n):
                    pe.wait_ge(es_ready, n + 3)
                    pe.wait_ge(om_ready, n + 3)
                    pe.wait_ge(r_added, n + 1)
                    for h in range(NH):
                        mm = MM(psR[:, k, 0:DM], om[:, k, h % 2 * (NH // 2) + h // 2, :], es[:, k, h * DM:(h + 1) * DM],
                                start=h == 0, stop=h == NH - 1)
                    mm.then_inc(r_done, 1)

                products(0, 0)
                with pe.Fori(0, NB // 2 - 1) as p:
                    for k in range(2):
                        products(1 - k, 2 * p + k + 1)
                        results(k, 2 * p + k)
                products(1, NB - 1)
                results(0, NB - 2)
                results(1, NB - 1)

            @block.scalar
            def _(act):
                A = nc.scalar.activation
                for n in range(0, NQS, 2):
                    act.wait_ge(qs_done, n + 1)
                    A(piece(n), bank(n), ACT.Copy).then_inc(qs_act, 1)
                act.sem_inc(es_ready, 2)
                with act.Fori(0, NB // 2) as p:
                    for k in range(2):
                        act.wait_ge(es_done, 2 * p + k + 1)
                        act.wait_ge(r_done, 2 * p + k + 1)
                        A(es[:, k, :], psE[:, k, :], ACT.Copy).then_inc(es_ready, 1)

            @block.vector
            def _(dve):
                V = nc.vector
                V.sem_inc(om_ready, 2)
                V.sem_inc(r_added, 2)
                dve.wait_ge(e_turned, 1)
                V.tensor_copy(e_t[:, :, :].rearrange("j h i -> j (h i)"), psR[0:DM, 0, :]).then_inc(e_ready, 1)
                for n in range(1, NQS, 2):
                    dve.wait_ge(qs_done, n + 1)
                    V.tensor_copy(piece(n), bank(n)).then_inc(qs_dve, 1)
                dve.wait_ge(mask_ready, 1)

                def masked(k, n):
                    dve.wait_ge(om_done, n + 1)
                    dve.wait_ge(r_done, n + 1)
                    for h2 in range(2):
                        ins = V.tensor_tensor(om[:, k, 4 * h2:4 * h2 + 4, :], psO[0:NT, k, h2, 0:HH].rearrange("u (h t) -> u h t", h=4),
                                              bc(causal[:, :].unsqueeze(1), NT, 4, NT), ALU.mult)
                    ins.then_inc(om_ready, 1)

                def add(k, n):
                    dve.wait_ge(r_done, n + 3)
                    V.tensor_tensor(H[:, bass.ds(n, 1), :], H[:, bass.ds(n, 1), :], psR[:, k:k + 1, 0:DM], ALU.add).then_inc(r_added, 1)

                masked(0, 0)
                with dve.Fori(0, NB // 2 - 1) as p:
                    for k in range(2):
                        masked(1 - k, 2 * p + k + 1)
                        add(k, 2 * p + k)
                masked(1, NB - 1)
                add(0, NB - 2)
                add(1, NB - 1)
                dve.wait_ge(r_added, NB + 2)


def top_two_experts(nc, H, XT, router_w1, router_b1, router_w2, router_b2, w1, b1, w2, b2, w3, b3):
    NE, RH, NP = 6, 32, 3
    G = 4
    N = G * NT
    NG = NB // G
    with ExitStack() as ctx:
        sb = lambda n, sh: ctx.enter_context(nc.sbuf_tensor("ff_" + n, sh, F32))
        pb = lambda n, sh: ctx.enter_context(nc.psum_tensor("ff_" + n, sh, F32))
        sem = lambda n: ctx.enter_context(nc.semaphore("ff_" + n))
        rw1, rb1, rw2, rb2 = sb("rw1", [DM, RH]), sb("rb1", [RH, 1]), sb("rw2", [RH, NE]), sb("rb2", [NT, NE])
        w1s = sb("w1s", [DM, NE, DM])
        w2s = sb("w2s", [128, NP, 128])
        w3s = sb("w3s", [128, NP, 128])
        b1s, b2s = sb("b1s", [128, NP]), sb("b2s", [128, NP])
        b3s = sb("b3s", [NT, NE * DM])
        prio = sb("prio", [NT, NE])
        rh = sb("rh", [RH, 2, N])
        pr = sb("pr", [NT, NB, NE])
        first = sb("first", [NT, NB, NE])
        second = sb("second", [NT, NB, NE])
        score = sb("score", [NT, NB, NE])
        mx = sb("mx", [NT, 4, NB])
        mix = sb("mix", [NT, NB, NE])
        h1 = sb("h1", [128, NP, N])
        h2 = sb("h2", [128, 2, NP, N])
        eo = sb("eo", [NT, 2, NE * DM])
        ew = sb("ew", [NT, 2, NE * DM])
        es = sb("es", [NT, 2, DM])
        psA = pb("psA", [128, 3, 512])
        psB = pb("psB", [128, 3, 512])
        psC = pb("psC", [NT, 2, 512])
        loaded, blocks_zero, prio_ready = sem("loaded"), sem("blocks_zero"), sem("prio_ready")
        diag_loaded = sem("diag_loaded")
        rh_done, rh_ready, lg_done, lg_ready = sem("rh_done"), sem("rh_ready"), sem("lg_done"), sem("lg_ready")
        centred, exp_ready, gap_ready, ratio_ready = sem("centred"), sem("exp_ready"), sem("gap_ready"), sem("ratio_ready")
        step = sem("step")
        h1_done, h1_ready, h2_done, h2_ready = sem("h1_done"), sem("h1_ready"), sem("h2_done"), sem("h2_ready")
        eo_done, eo_read, added, vstep = sem("eo_done"), sem("eo_read"), sem("added"), sem("vstep")
        staged = sem("staged")
        xs = sb("xs", [DM, N])
        lg = psC[:, 0, 0:NB * NE].rearrange("t (b e) -> t b e", e=NE)
        with nc.Block() as block:
            @block.sync
            def _(sp):
                with nc.allow_non_contiguous_dma(reason="small weights"):
                    sp.dma_start(rw1[:, :], router_w1).then_inc(loaded, 16)
                    sp.dma_start(rb1[:, :], router_b1.rearrange("(k a) -> k a", a=1)).then_inc(loaded, 16)
                    sp.dma_start(rw2[:, :], router_w2).then_inc(loaded, 16)
                    sp.dma_start(rb2[:, :], router_b2.rearrange("(a k) -> a k", a=1).broadcast_to([NT, NE])).then_inc(loaded, 16)
                    sp.dma_start(w1s[:, :, :], w1.rearrange("e d h -> d e h")).then_inc(loaded, 16)
                    sp.dma_start(b1s[:, :], b1.rearrange("(p e) h -> (e h) p", e=2)).then_inc(loaded, 16)
                    sp.dma_start(b2s[:, :], b2.rearrange("(p e) h -> (e h) p", e=2)).then_inc(loaded, 16)
                    sp.dma_start(b3s[:, :], b3.rearrange("(a e) d -> a (e d)", a=1).broadcast_to([NT, NE * DM])).then_inc(loaded, 16)
                    sp.wait_ge(blocks_zero, 2)
                    for dst, src in ((w2s, w2), (w3s, w3)):
                        for e in range(2):
                            sp.dma_start(dst[e * DM:(e + 1) * DM, :, e * DM:(e + 1) * DM],
                                         src.rearrange("(p e) h f -> e h p f", e=2)[e]).then_inc(diag_loaded, 16)

            @block.gpsimd
            def _(pool):
                nc.gpsimd.memset(w2s[:, :, :], 0.0).then_inc(blocks_zero, 1)
                nc.gpsimd.memset(w3s[:, :, :], 0.0).then_inc(blocks_zero, 1)
                for e in range(NE):
                    ins = nc.gpsimd.memset(prio[:, e:e + 1], float(NE - e))
                ins.then_inc(prio_ready, 1)
                nc.gpsimd.tensor_copy(xs[:, :], XT[:, 0:N]).then_inc(staged, 1)
                with pool.Fori(1, NG) as g:
                    pool.wait_ge(h1_done, NP * g)
                    nc.gpsimd.tensor_copy(xs[:, :], XT[:, bass.ds(g * N, N)]).then_inc(staged, 1)

            @block.tensor
            def _(pe):
                pe.wait_ge(loaded, 8 * 16)

                def router(g):
                    if g >= 2:
                        pe.wait_ge(rh_ready, g - 1)
                    nc.tensor.matmul(psA[0:RH, g % 2, 0:N], rw1[:, :], XT[:, g * N:(g + 1) * N], start=True, stop=True).then_inc(rh_done, 1)

                router(0)
                for g in range(NG):
                    if g + 1 < NG:
                        router(g + 1)
                    pe.wait_ge(rh_ready, g + 1)
                    for j in range(G):
                        b = g * G + j
                        mm = nc.tensor.matmul(psC[:, 0, b * NE:(b + 1) * NE], rh[:, g % 2, j * NT:(j + 1) * NT], rw2[:, :], start=True, stop=True)
                    mm.then_inc(lg_done, 1)
                pe.wait_ge(diag_loaded, 4 * 16)
                pe.wait_ge(lg_ready, 1)

                with pe.Fori(0, NG) as g:
                    pe.wait_ge(staged, g + 1)
                    for p in range(NP):
                        nc.tensor.matmul(psA[:, p, 0:N], w1s[:, 2 * p:2 * p + 2, :].rearrange("d e h -> d (e h)"), xs[:, :],
                                         start=True, stop=True).then_inc(h1_done, 1)
                    for p in range(NP):
                        pe.wait_ge(h1_ready, NP * g + p + 1)
                        nc.tensor.matmul(psB[:, p, 0:N], w2s[:, p, :], h1[:, p, :], start=True, stop=True).then_inc(h2_done, 1)
                    pe.wait_ge(h2_ready, NP * g + NP)
                    for j in range(G):
                        pe.wait_ge(eo_read, G * g + j + 1)
                        for p in range(NP):
                            mm = nc.tensor.matmul(psC[:, j % 2, p * 128:(p + 1) * 128], h2[:, 0, p, j * NT:(j + 1) * NT], w3s[:, p, :], start=True, stop=True)
                        mm.then_inc(eo_done, 1)

            @block.scalar
            def _(act):
                act.wait_ge(loaded, 8 * 16)
                for g in range(NG):
                    act.wait_ge(rh_done, g + 1)
                    if g >= 2:
                        act.wait_ge(lg_done, g - 1)
                    nc.scalar.activation(rh[:, g % 2, :], psA[0:RH, g % 2, 0:N], ACT.Relu, bias=rb1[:, 0:1]).then_inc(rh_ready, 1)
                act.wait_ge(centred, 1)
                nc.scalar.activation(pr[:, :, :], pr[:, :, :], ACT.Exp).then_inc(exp_ready, 1)
                act.wait_ge(gap_ready, 1)
                nc.scalar.activation(mx[:, 1, :], mx[:, 1, :], ACT.Exp).then_inc(ratio_ready, 1)
                with act.Fori(0, NG) as g:
                    for p in range(NP):
                        act.wait_ge(h1_done, NP * g + p + 1)
                        nc.scalar.activation(h1[:, p, :], psA[:, p, 0:N], ACT.Relu, bias=b1s[:, p:p + 1]).then_inc(h1_ready, 1)
                    for p in range(NP):
                        act.wait_ge(h2_done, NP * g + p + 1)
                        ins = nc.scalar.activation(h2[:, 0, p, :], psB[:, p, 0:N], ACT.Relu, bias=b2s[:, p:p + 1])
                        ins.then_inc(h2_ready, 1)

            @block.vector
            def _(dve):
                s = Steps(dve, step)
                V = nc.vector
                wide = lambda m: bc(m.unsqueeze(2), NT, NB, NE)
                across = lambda m: bc(m.unsqueeze(1), NT, NB, NE)
                dve.wait_ge(lg_done, NG)
                dve.wait_ge(loaded, 8 * 16)
                V.tensor_tensor(pr[:, :, :], lg, across(rb2[:, :]), ALU.add).then_inc(lg_ready, 1)
                dve.wait_ge(lg_ready, 1)
                s.link(V.reduce_max(mx[:, 0, :], pr[:, :, :], AX.X))
                V.tensor_tensor(pr[:, :, :], pr[:, :, :], wide(mx[:, 0, :]), ALU.subtract).then_inc(centred, 1)
                dve.wait_ge(exp_ready, 1)
                s.link(V.reduce_sum(mx[:, 0, :], pr[:, :, :], AX.X))
                s.link(V.reciprocal(mx[:, 1, :], mx[:, 0, :]))
                s.link(V.tensor_tensor(pr[:, :, :], pr[:, :, :], wide(mx[:, 1, :]), ALU.mult))
                dve.wait_ge(prio_ready, 1)

                def pick(chosen, best, probs):
                    s.link(V.reduce_max(best, probs, AX.X))
                    s.link(V.tensor_tensor(score[:, :, :], probs, wide(best), ALU.is_equal))
                    s.link(V.tensor_tensor(score[:, :, :], score[:, :, :], across(prio[:, :]), ALU.mult))
                    s.link(V.reduce_max(mx[:, 3, :], score[:, :, :], AX.X))
                    s.link(V.tensor_tensor(chosen, score[:, :, :], wide(mx[:, 3, :]), ALU.is_equal))

                pick(first[:, :, :], mx[:, 0, :], pr[:, :, :])
                s.link(V.scalar_tensor_tensor(pr[:, :, :], first[:, :, :], -2.0, pr[:, :, :], ALU.mult, ALU.add))
                pick(second[:, :, :], mx[:, 1, :], pr[:, :, :])
                V.tensor_tensor(mx[:, 1, :], mx[:, 1, :], mx[:, 0, :], ALU.subtract).then_inc(gap_ready, 1)
                dve.wait_ge(ratio_ready, 1)
                s.link(V.tensor_scalar(mx[:, 0, :], mx[:, 1, :], 1.0, None, ALU.add))
                s.link(V.reciprocal(mx[:, 2, :], mx[:, 0, :]))
                s.link(V.tensor_tensor(mx[:, 3, :], mx[:, 2, :], mx[:, 1, :], ALU.mult))
                s.link(V.tensor_tensor(first[:, :, :], first[:, :, :], wide(mx[:, 2, :]), ALU.mult))
                s.link(V.tensor_tensor(second[:, :, :], second[:, :, :], wide(mx[:, 3, :]), ALU.mult))
                s.link(V.tensor_tensor(mix[:, :, :], first[:, :, :], second[:, :, :], ALU.add))
                V.sem_inc(eo_read, 2)
                with dve.Fori(0, NG) as g:
                    t = Steps(dve, vstep, g * (3 * G))
                    for j in range(G):
                        b, k = g * G + j, j % 2
                        dve.wait_ge(eo_done, G * g + j + 1)
                        V.tensor_tensor(eo[:, k, :], psC[:, k, 0:NE * DM], b3s[:, :], ALU.add).then_inc(eo_read, 1)
                        dve.wait_ge(eo_read, G * g + j + 3)
                        t.link(V.tensor_tensor(ew[:, k, :].rearrange("t (e d) -> t e d", e=NE), eo[:, k, :].rearrange("t (e d) -> t e d", e=NE),
                                               bc(mix[:, bass.ds(b, 1), :].rearrange("t a e -> t (a e)").unsqueeze(2), NT, NE, DM), ALU.mult))
                        t.link(V.reduce_sum(es[:, k, :], ew[:, k, :].rearrange("t (e d) -> t d e", e=NE), AX.X))
                        t.link(V.tensor_tensor(H[:, bass.ds(b, 1), :], H[:, bass.ds(b, 1), :], es[:, k:k + 1, :], ALU.add))


def best_expert(nc, H, XT, ident, gate_w, gate_b, w1, b1, w2, b2):
    NE, F = 8, 256
    CAP = -(-5 * TOK // (4 * NE))
    KT = F // 128
    G = 4
    N = G * NT
    NG = NB // G
    with ExitStack() as ctx:
        sb = lambda n, sh: ctx.enter_context(nc.sbuf_tensor("sw_" + n, sh, F32))
        pb = lambda n, sh: ctx.enter_context(nc.psum_tensor("sw_" + n, sh, F32))
        sem = lambda n: ctx.enter_context(nc.semaphore("sw_" + n))
        gw, gb = sb("gw", [DM, NE]), sb("gb", [NT, NE])
        w1s = sb("w1s", [DM + 1, NE, F])
        w2s = sb("w2s", [128, NE, KT, DM])
        b2s = sb("b2s", [NE, DM])
        prio = sb("prio", [NT, NE])
        pr, score, chosen = sb("pr", [NT, NB, NE]), sb("score", [NT, NB, NE]), sb("chosen", [NT, NB, NE])
        mx = sb("mx", [NT, 4, NB])
        chT = sb("chT", [NE, TOK])
        ones = sb("ones", [NE, TOK])
        count = sb("count", [NE, TOK])
        gate = sb("gate", [NT, NB, NE])
        gT = sb("gT", [NE, TOK])
        hid = sb("hid", [128, NE, KT, N])
        oT = sb("oT", [128, N])
        fix = sb("fix", [NT, NB, DM])
        flag = ctx.enter_context(nc.sbuf_tensor("sw_flag", [NT, NB, DM], mybir.dt.uint32))
        const = sb("const", [NT, 3])
        g_all, xs = sb("g_all", [DM, 2, NE, N]), sb("xs", [DM + 1, 2, NE, N])
        g_rows = sb("g_rows", [NE, 2, N])
        staged, g_in = sem("staged"), [sem("g_in0"), sem("g_in1")]
        psA = pb("psA", [128, 4, 512])
        psO = pb("psO", [DM, 512])
        psC = pb("psC", [NT, 2, 512])
        loaded, prio_ready, lg_done, lg_ready = sem("loaded"), sem("prio_ready"), sem("lg_done"), sem("lg_ready")
        centred, exp_ready, step = sem("centred"), sem("exp_ready"), sem("step")
        ch_ready, turned, taken, counted, g_stored = sem("ch_ready"), sem("turned"), sem("taken"), sem("counted"), sem("g_stored")
        hid_done, hid_a, hid_v = sem("hid_done"), sem("hid_a"), sem("hid_v")
        w2_done, out_done, o_taken, o_turned, fixed = sem("w2_done"), sem("out_done"), sem("o_taken"), sem("o_turned"), sem("fixed")
        g_dram = nc.dram_tensor("sw_gates", [NE, TOK], F32).ap()
        lg = psC[:, 0, 0:NB * NE].rearrange("t (b e) -> t b e", e=NE)
        with nc.Block() as block:
            @block.sync
            def _(sp):
                with nc.allow_non_contiguous_dma(reason="small weights"):
                    sp.dma_start(gw[:, :], gate_w).then_inc(loaded, 16)
                    sp.dma_start(gb[:, :], gate_b.rearrange("(a k) -> a k", a=1).broadcast_to([NT, NE])).then_inc(loaded, 16)
                    sp.dma_start(w1s[0:DM, :, :], w1.rearrange("e d f -> d e f")).then_inc(loaded, 16)
                    sp.dma_start(w1s[DM:DM + 1, :, :], b1.rearrange("(a e) f -> a e f", a=1)).then_inc(loaded, 16)
                    for k in range(KT):
                        sp.dma_start(w2s[:, :, k, :], w2[:, k * 128:(k + 1) * 128, :].rearrange("e p d -> p e d")).then_inc(loaded, 16)
                    sp.dma_start(b2s[:, :], b2).then_inc(loaded, 16)
                sp.wait_ge(counted, 1)
                sp.dma_start(g_dram, gT[:, :]).then_inc(g_stored, 16)
                sp.wait_ge(g_stored, 16)

                def gates(k, g):
                    tile = g_dram[:, bass.ds(g * N, N)].rearrange("(a e) n -> a e n", a=1)
                    sp.dma_start(g_all[:, k, :, :], tile.broadcast_to([DM, NE, N])).then_inc(g_in[k], 16)
                    sp.dma_start(xs[DM:DM + 1, k, :, :], tile).then_inc(g_in[k], 16)
                    sp.dma_start(g_rows[:, k, :], g_dram[:, bass.ds(g * N, N)]).then_inc(g_in[k], 16)

                for k in range(2):
                    gates(k, k)
                with sp.Fori(1, NG // 2) as i:
                    for k in range(2):
                        sp.wait_ge(out_done, 2 * i + k - 1)
                        gates(k, 2 * i + k)
            LOADED = 7 * 16

            @block.gpsimd
            def _(pool):
                for e in range(NE):
                    nc.gpsimd.memset(prio[:, e:e + 1], float(NE - e))
                nc.gpsimd.memset(const[:, 0:1], 0.0)
                nc.gpsimd.memset(const[:, 1:2], 10000.0)
                nc.gpsimd.memset(const[:, 2:3], -10000.0)
                nc.gpsimd.memset(oT[:, :], 0.0)
                nc.gpsimd.memset(ones[:, :], 1.0).then_inc(prio_ready, 1)

                def scale(k, g, turn):
                    pool.wait_ge(g_in[k], 48 * turn + 48)
                    nc.gpsimd.tensor_tensor(xs[0:DM, k, :, :], bc(XT[:, bass.ds(g * N, N)].unsqueeze(1), DM, NE, N), g_all[:, k, :, :], ALU.mult).then_inc(staged, 1)

                pool.wait_ge(prio_ready, 1)
                for k in range(2):
                    scale(k, k, 0)
                with pool.Fori(1, NG // 2) as i:
                    for k in range(2):
                        pool.wait_ge(hid_done, NE * KT * (2 * i + k - 1))
                        scale(k, 2 * i + k, i)

            @block.tensor
            def _(pe):
                pe.wait_ge(loaded, LOADED)
                for b in range(NB):
                    mm = nc.tensor.matmul(lg[:, b, :], XT[:, b * NT:(b + 1) * NT], gw[:, :], start=True, stop=True)
                mm.then_inc(lg_done, 1)
                pe.wait_ge(ch_ready, 1)
                for g in range(2 * NG):
                    if g >= 4:
                        pe.wait_ge(taken, g - 3)
                    for j in range(G):
                        mm = nc.tensor.transpose(psA[0:NE, g % 4, j * NT:(j + 1) * NT], (chosen, gate)[g // NG][:, g % NG * G + j, :], ident[0:NT, 0:NT])
                    mm.then_inc(turned, 1)
                pe.wait_ge(counted, 1)
                pe.sem_inc(o_turned, 1)
                pe.sem_inc(w2_done, NE * KT)
                MM = nc.tensor.matmul
                with pe.Fori(0, NG // 2) as i:
                    for s in range(2):
                        g = 2 * i + s
                        pe.wait_ge(staged, g + 1)
                        pe.wait_ge(g_in[s], 48 * i + 48)

                        def second(n):
                            pe.wait_ge(hid_a if n % 2 == 0 else hid_v, (NE * KT // 2) * g + n // 2 + 1)
                            if n == 0:
                                pe.wait_ge(o_taken, g + 1)
                            MM(psO[:, 0:N], w2s[:, n // KT, n % KT, :], hid[:, n // KT, n % KT, :], start=n == 0, stop=False).then_inc(w2_done, 1)

                        for n in range(NE * KT):
                            if n >= 4:
                                pe.wait_ge(hid_a if n % 2 == 0 else hid_v, (NE * KT // 2) * g + (n - 4) // 2 + 1)
                            MM(psA[:, n % 4, 0:N], w1s[:, n // KT, n % KT * 128:(n % KT + 1) * 128], xs[:, s, n // KT, :],
                               start=True, stop=True).then_inc(hid_done, 1)
                            if n >= 3:
                                second(n - 3)
                        for n in range(NE * KT - 3, NE * KT):
                            second(n)
                        MM(psO[:, 0:N], b2s[:, :], g_rows[:, s, :], start=False, stop=True).then_inc(out_done, 1)
                        pe.wait_ge(o_taken, g + 2)
                        pe.wait_ge(fixed, g + 1)
                        for j in range(G):
                            mm = nc.tensor.transpose(psC[:, 1, j * 128:(j + 1) * 128], oT[:, j * NT:(j + 1) * NT], ident[:, :])
                        mm.then_inc(o_turned, 1)

            @block.scalar
            def _(act):
                act.wait_ge(loaded, LOADED)
                act.wait_ge(centred, 1)
                nc.scalar.activation(pr[:, :, :], pr[:, :, :], ACT.Exp).then_inc(exp_ready, 1)
                act.sem_inc(o_taken, 1)
                with act.Fori(0, NG) as g:
                    for n in range(0, NE * KT, 2):
                        act.wait_ge(hid_done, NE * KT * g + n + 1)
                        act.wait_ge(w2_done, NE * KT * g + n + 1)
                        nc.scalar.activation(hid[:, n // KT, n % KT, :], psA[:, n % 4, 0:N], ACT.Relu).then_inc(hid_a, 1)
                    act.wait_ge(out_done, g + 1)
                    act.wait_ge(o_turned, g + 1)
                    nc.scalar.activation(oT[0:DM, :], psO[:, 0:N], ACT.Copy).then_inc(o_taken, 1)

            @block.vector
            def _(dve):
                s = Steps(dve, step)
                V = nc.vector
                wide = lambda m: bc(m.unsqueeze(2), NT, NB, NE)
                across = lambda m: bc(m.unsqueeze(1), NT, NB, NE)
                dve.wait_ge(lg_done, 1)
                dve.wait_ge(loaded, LOADED)
                dve.wait_ge(prio_ready, 1)
                V.tensor_tensor(pr[:, :, :], lg, across(gb[:, :]), ALU.add).then_inc(lg_ready, 1)
                dve.wait_ge(lg_ready, 1)
                s.link(V.reduce_max(mx[:, 0, :], pr[:, :, :], AX.X))
                V.tensor_tensor(pr[:, :, :], pr[:, :, :], wide(mx[:, 0, :]), ALU.subtract).then_inc(centred, 1)
                dve.wait_ge(exp_ready, 1)
                s.link(V.reduce_sum(mx[:, 0, :], pr[:, :, :], AX.X))
                s.link(V.reciprocal(mx[:, 1, :], mx[:, 0, :]))
                s.link(V.tensor_tensor(pr[:, :, :], pr[:, :, :], wide(mx[:, 1, :]), ALU.mult))
                s.link(V.reduce_max(mx[:, 2, :], pr[:, :, :], AX.X))
                s.link(V.tensor_tensor(score[:, :, :], pr[:, :, :], wide(mx[:, 2, :]), ALU.is_equal))
                s.link(V.tensor_tensor(score[:, :, :], score[:, :, :], across(prio[:, :]), ALU.mult))
                s.link(V.reduce_max(mx[:, 3, :], score[:, :, :], AX.X))
                s.link(V.tensor_tensor(chosen[:, :, :], score[:, :, :], wide(mx[:, 3, :]), ALU.is_equal))
                V.tensor_tensor(gate[:, :, :], chosen[:, :, :], wide(mx[:, 2, :]), ALU.mult).then_inc(ch_ready, 1)
                for g in range(2 * NG):
                    dve.wait_ge(turned, g + 1)
                    V.tensor_copy((chT, gT)[g // NG][:, g % NG * N:(g % NG + 1) * N], psA[0:NE, g % 4, 0:N]).then_inc(taken, 1)
                dve.wait_ge(taken, 2 * NG)
                s.link(V.tensor_tensor_scan(count[:, :], ones[:, :], chT[:, :], 0.0, ALU.mult, ALU.add))
                s.link(V.tensor_scalar(count[:, :], count[:, :], float(CAP), None, ALU.is_le))
                V.tensor_tensor(gT[:, :], gT[:, :], count[:, :], ALU.mult).then_inc(counted, 1)
                V.sem_inc(fixed, 1)
                with dve.Fori(0, NG) as g:
                    for n in range(1, NE * KT, 2):
                        dve.wait_ge(hid_done, NE * KT * g + n + 1)
                        dve.wait_ge(w2_done, NE * KT * g + n + 1)
                        V.tensor_scalar(hid[:, n // KT, n % KT, :], psA[:, n % 4, 0:N], 0.0, None, ALU.max).then_inc(hid_v, 1)
                    dve.wait_ge(o_turned, g + 2)
                    V.tensor_copy(fix[:, bass.ds(g * G, G), :], psC[:, 1, :].rearrange("t (b d) -> t b d", b=G)[:, :, 0:DM]).then_inc(fixed, 1)
                dve.wait_ge(fixed, NG + 1)
                BIG = 3.4028234663852886e38
                whole = lambda i: bc(const[:, i:i + 1].unsqueeze(2), NT, NB, DM)
                s.link(V.tensor_tensor(flag[:, :, :], fix[:, :, :], fix[:, :, :], ALU.not_equal))
                s.link(V.copy_predicated(fix[:, :, :], flag[:, :, :], whole(0)))
                s.link(V.tensor_scalar(flag[:, :, :], fix[:, :, :], BIG, None, ALU.is_gt))
                s.link(V.copy_predicated(fix[:, :, :], flag[:, :, :], whole(1)))
                s.link(V.tensor_scalar(flag[:, :, :], fix[:, :, :], -BIG, None, ALU.is_lt))
                s.link(V.copy_predicated(fix[:, :, :], flag[:, :, :], whole(2)))
                s.link(V.tensor_tensor(H[:, :, :], H[:, :, :], fix[:, :, :], ALU.add))


FH = 256
NC = 16
NCH = NT // NC
QB = 8
HB = NB // 2


def memory_tensors(nc, ctx):
    sb = lambda n, sh: ctx.enter_context(nc.sbuf_tensor("mem_" + n, sh, F32))
    dr = lambda n, sh: nc.dram_tensor("mem_" + n + "_dram", sh, F32).ap()
    return dict(
        a0=sb("a0", [DM, FH]),
        b0=sb("b0", [128, 2, 2, 128]),
        b0t=sb("b0t", [128, FH]),
        z_base=sb("z_base", [128, 2, NB, NT]),
        w_bs=sb("w_bs", [128, NCH - 1, 4, NT]), g_bs=sb("g_bs", [128, NCH - 1, 4, NT]),
        c_f=sb("c_f", [128, NB, NT]),
        v_y=sb("v_y", [128, HB, NT]),
        w_rows=dr("w_rows", [NT, NCH, NB, NC]),
        g_rows=dr("g_rows", [NT, NCH, NB, NC]),
        w_t=dr("w_t", [NT, TOK]),
        k_t=dr("k_t", [DM, TOK]), q_t=dr("q_t", [DM, TOK]), qc_t=dr("qc_t", [DM, TOK]),
        hist_h=dr("hist_h", [128, 2, NCH, NB, NC]), hist_dz=dr("hist_dz", [128, 2, NCH, NB, NC]),
        h=dr("h", [NT, NB, DM]),
        c_now=dr("c_now", [128, TOK]),
    )


def memory_setup(nc, M, H, XT, ident, inject, W_fused, W0, W1, P0, P1):
    NQ = 3 * DM
    G = 4
    N = G * NT
    NG = NB // G
    with ExitStack() as ctx:
        sb = lambda n, sh: ctx.enter_context(nc.sbuf_tensor("ms_" + n, sh, F32))
        pb = lambda n, sh: ctx.enter_context(nc.psum_tensor("ms_" + n, sh, F32))
        sem = lambda n: ctx.enter_context(nc.semaphore("ms_" + n))
        wf = sb("wf", [128, 2, DM])
        wft = sb("wft", [DM, 2, 128])
        gcol = sb("gcol", [DM, 3, 128])
        p0, w1, p1 = sb("p0", [DM, FH]), sb("w1", [128, 2, DM]), sb("p1", [128, 2, DM])
        fp = sb("fp", [NT, NB, NQ])
        sg = sb("sg", [NT, 2, 2, NQ])
        nrm = sb("nrm", [NT, 4, 2 * NB])
        keep, eta, theta, work = sb("keep", [128, NB, NT]), sb("eta", [128, NB, NT]), sb("theta", [128, NB, NT]), sb("work", [128, NB, NT])
        diag = sb("diag", [NT, NT])
        vv = sb("vv", [NT, HB, 128])
        kT, qT = sb("kT", [DM, TOK]), sb("qT", [DM, TOK])
        psG, psF, psT = pb("psG", [128, 2, 512]), pb("psF", [NT, 2, 512]), pb("psT", [128, 4, 512])
        flat = lambda t: t[:, :, :].rearrange("p b t -> p (b t)")
        loaded, turned, taken = sem("loaded"), sem("turned"), sem("taken")
        k_stored = sem("k_stored")
        step, zeroed = sem("step"), sem("zeroed")
        fp_ready = sem("fp_ready")
        gram_read, stored = sem("gram_read"), sem("stored")
        act_done, pe_done = sem("act_done"), sem("pe_done")
        GATES = 3 * 6
        ROOT = GATES + NB // 2 + 1
        made = sem("made")
        MADE = {n: i + 1 for i, n in enumerate(("b0", "wft", "sq", "kq", "w", "c", "wt", "kt", "rows", "qc", "g", "base"))}
        bs_turned, bs_ready = sem("bs_turned"), sem("bs_ready")
        by_chunk = lambda x: flat(x)[0:NT].rearrange("t (c b s) -> t b c s", c=NCH, s=NC)
        with nc.Block() as block:
            @block.sync
            def _(sp):
                sp.dma_start(M["h"], H[0:NT, :, :]).then_inc(stored, 16)
                sp.dma_start(diag[:, :], inject).then_inc(loaded, 16)
                sp.dma_start(wf[:, 0, :], W_fused[0:128, :]).then_inc(loaded, 16)
                sp.dma_start(wf[0:NQ + 3 - 128, 1, :], W_fused[128:NQ + 3, :]).then_inc(loaded, 16)
                sp.dma_start(M["a0"][:, :], W0).then_inc(loaded, 16)
                sp.dma_start(p0[:, :], P0).then_inc(loaded, 16)
                sp.dma_start(w1[:, :, :], W1.rearrange("(k p) d -> p k d", p=128)).then_inc(loaded, 16)
                sp.dma_start(p1[:, :, :], P1.rearrange("(k p) d -> p k d", p=128)).then_inc(loaded, 16)
                sp.wait_ge(made, MADE["wt"])
                sp.dma_start(M["w_t"], flat(work)[0:NT]).then_inc(stored, 16)
                sp.wait_ge(made, MADE["kt"])
                sp.dma_start(M["k_t"], kT[:, :]).then_inc(k_stored, 16)
                sp.dma_start(M["q_t"], qT[:, :]).then_inc(stored, 16)
                sp.wait_ge(made, MADE["rows"])
                sp.dma_start(M["w_rows"].rearrange("t c b s -> t (c b s)"), flat(eta)[0:NT]).then_inc(stored, 16)
                sp.wait_ge(made, MADE["c"])
                sp.dma_start(M["c_now"], flat(keep)).then_inc(stored, 16)
                sp.wait_ge(made, MADE["qc"])
                sp.dma_start(M["qc_t"], fp[0:DM, 0:16, :].rearrange("p a c -> p (a c)")).then_inc(stored, 16)
                sp.wait_ge(made, MADE["g"])
                sp.dma_start(M["g_rows"].rearrange("t c b s -> t (c b s)"), flat(theta)[0:NT]).then_inc(stored, 16)
                sp.wait_ge(stored, 16 * 7)
                sp.wait_ge(k_stored, 16)

            @block.gpsimd
            def _(pool):
                nc.gpsimd.memset(M["b0"][:, :, :, :], 0.0).then_inc(zeroed, 1)

            @block.tensor
            def _(pe):
                T, MM = nc.tensor.transpose, nc.tensor.matmul
                pe.wait_ge(loaded, 7 * 16)
                T(psT[0:DM, 0, 0:128], wf[:, 0, :], ident[:, :])
                T(psT[0:DM, 0, 128:128 + NQ + 3 - 128], wf[0:NQ + 3 - 128, 1, :], ident[0:NQ + 3 - 128, 0:NQ + 3 - 128]).then_inc(turned, 1)
                pe.wait_ge(made, MADE["b0"])
                for b2 in range(2):
                    for k in range(2):
                        mm = T(psT[:, 1, (2 * b2 + k) * 128:(2 * b2 + k + 1) * 128], M["b0"][:, k, b2, :], ident[:, :])
                mm.then_inc(turned, 1)
                pe.wait_ge(made, MADE["wft"])
                for j in range(3 * 6):
                    if j >= 2:
                        pe.wait_ge(act_done, j - 1)
                    MM(psG[:, j % 2, :], gcol[:, j // 6, :], XT[:, j % 6 * 512:(j % 6 + 1) * 512], start=True, stop=True).then_inc(pe_done, 1)
                for j in range(NB // 2):
                    if j >= 2:
                        pe.wait_ge(fp_ready, j - 1)
                    for i in range(2):
                        b = 2 * j + i
                        mm = MM(psF[:, j % 2, i * NQ:(i + 1) * NQ], XT[:, b * NT:(b + 1) * NT], wft[:, :, :].rearrange("d a c -> d (a c)")[:, 0:NQ], start=True, stop=True)
                    mm.then_inc(pe_done, 1)
                pe.wait_ge(made, MADE["kq"])
                n = 2
                for what in range(4):
                    if what == 3:
                        pe.wait_ge(made, MADE["w"])
                    for g in range(NG if what != 2 else NG // 2):
                        pe.wait_ge(taken, n - 5) if n >= 6 else None
                        for j in range(G):
                            b = g * G + j
                            if what < 2:
                                mm = T(psT[0:DM, n % 4, j * NT:(j + 1) * NT], fp[:, b, (1 - what) * DM:(2 - what) * DM], ident[0:NT, 0:NT])
                            elif what == 2:
                                mm = T(psT[:, n % 4, j * NT:(j + 1) * NT], vv[:, b, :], ident[0:NT, 0:NT])
                            else:
                                mm = T(psT[0:NT, n % 4, j * NT:(j + 1) * NT], theta[0:NT, b, :], ident[0:NT, 0:NT])
                        mm.then_inc(turned, 1)
                        n += 1
                pe.wait_ge(taken, n - 2)
                for g in range(NG):
                    if g >= 4:
                        pe.wait_ge(gram_read, g - 3)
                    for j in range(G):
                        b = g * G + j
                        mm = MM(psT[0:NT, g % 4, j * NT:(j + 1) * NT], kT[:, b * NT:(b + 1) * NT], kT[:, b * NT:(b + 1) * NT], start=True, stop=True)
                    mm.then_inc(pe_done, 1)
                pe.wait_ge(made, MADE["g"])
                for m in range(2 * (NCH - 1)):
                    if m >= 4:
                        pe.wait_ge(bs_ready, m - 3)
                    for q in range(4):
                        o = (m // 2 * NB + q * QB) * NC
                        mm = T(psT[:, m % 4, q * NT:(q + 1) * NT], flat((eta, theta)[m % 2])[0:NT, o:o + 128], ident[0:NT, 0:NT])
                    mm.then_inc(bs_turned, 1)
                pe.wait_ge(made, MADE["base"])
                for j in range(12):
                    if j >= 2:
                        pe.wait_ge(act_done, ROOT + j - 1)
                    MM(psG[:, j % 2, :], M["a0"][:, j // 6 * 128:(j // 6 + 1) * 128], kT[:, j % 6 * 512:(j % 6 + 1) * 512], start=True, stop=True).then_inc(pe_done, 1)

            @block.scalar
            def _(act):
                A = nc.scalar.activation
                for j in range(3 * 6):
                    act.wait_ge(pe_done, j + 1)
                    A(flat((keep, theta, eta)[j // 6])[:, j % 6 * 512:(j % 6 + 1) * 512], psG[:, j % 2, :], ACT.Sigmoid,
                      scale=(-1.0 if j < 6 else 1.0)).then_inc(act_done, 1)
                for j in range(NB // 2):
                    act.wait_ge(pe_done, GATES + j + 1)
                    if j >= 2:
                        act.wait_ge(fp_ready, j - 1)
                    A(sg[:, j % 2, :, :].rearrange("t a c -> t (a c)"), psF[:, j % 2, 0:2 * NQ], ACT.Sigmoid).then_inc(act_done, 1)
                act.wait_ge(made, MADE["sq"])
                A(nrm[:, 1, :], nrm[:, 0, :], ACT.Sqrt).then_inc(act_done, 1)
                for j in range(12):
                    act.wait_ge(pe_done, GATES + NB // 2 + NG + j + 1)
                    A(M["z_base"][:, j // 6, :, :].rearrange("p b t -> p (b t)")[:, j % 6 * 512:(j % 6 + 1) * 512], psG[:, j % 2, :], ACT.Copy).then_inc(act_done, 1)
                act.wait_ge(act_done, ROOT + 12)

            @block.vector
            def _(dve):
                V = nc.vector
                s = Steps(dve, step)
                dve.wait_ge(loaded, 7 * 16)
                s.link(V.tensor_tensor(M["a0"][:, :], M["a0"][:, :], p0[:, :], ALU.add))
                dve.wait_ge(zeroed, 1)
                for b2 in range(2):
                    ins = V.tensor_tensor(M["b0"][:, :, b2, b2 * DM:(b2 + 1) * DM], w1[:, :, :], p1[:, :, :], ALU.add)
                ins.then_inc(made, 1)
                dve.wait_ge(turned, 1)
                s.link(V.tensor_copy(wft[:, :, :].rearrange("d a c -> d (a c)")[:, 0:NQ + 3], psT[0:DM, 0, 0:NQ + 3]))
                V.tensor_copy(gcol[:, :, :], bc(wft[:, 1, NQ - 128:NQ - 128 + 3].unsqueeze(2), DM, 3, 128)).then_inc(made, 1)
                dve.wait_ge(turned, 2)
                for b2 in range(2):
                    h = slice(b2 * DM, (b2 + 1) * DM)
                    ins = V.tensor_copy(M["b0t"][h, :], psT[h, 1, b2 * FH:(b2 + 1) * FH])
                s.link(ins)
                for j in range(NB // 2):
                    dve.wait_ge(act_done, GATES + j + 1)
                    V.tensor_tensor(fp[:, 2 * j:2 * j + 2, :], psF[:, j % 2, 0:2 * NQ].rearrange("t (a c) -> t a c", a=2), sg[:, j % 2, :, :], ALU.mult).then_inc(fp_ready, 1)
                dve.wait_ge(fp_ready, NB // 2)
                qk = fp[:, :, 0:2 * DM].rearrange("t b (a d) -> t b a d", a=2)
                dve.wait_ge(act_done, GATES)
                for a in range(2):
                    sq = work[0:NT, :, 0:DM]
                    s.link(V.tensor_tensor(sq, qk[:, :, a, :], qk[:, :, a, :], ALU.mult))
                    ins = V.reduce_sum(nrm[:, 0, a * NB:(a + 1) * NB], sq, AX.X)
                    if a == 0:
                        s.link(ins)
                ins.then_inc(made, 1)
                dve.wait_ge(act_done, ROOT)
                s.link(V.tensor_scalar(nrm[:, 1, :], nrm[:, 1, :], 1e-12, None, ALU.max))
                s.link(V.reciprocal(nrm[:, 2, :], nrm[:, 1, :]))
                s.link(V.tensor_tensor(nrm[:, 3, :], nrm[:, 2, :], nrm[:, 0, :], ALU.mult))
                s.link(V.tensor_tensor(nrm[:, 2, :], nrm[:, 3, :], nrm[:, 1, :], ALU.add))
                s.link(V.tensor_scalar(nrm[:, 3, :], nrm[:, 2, :], 0.5, 1e-12, ALU.mult, ALU.max))
                s.link(V.reciprocal(nrm[:, 1, :], nrm[:, 3, :]))
                for a in range(2):
                    V.tensor_copy(vv[:, :, a * DM:(a + 1) * DM], fp[:, a * HB:(a + 1) * HB, 2 * DM:3 * DM])
                for a in range(2):
                    ins = V.tensor_tensor(qk[:, :, a, :], qk[:, :, a, :], bc(nrm[:, 1, a * NB:(a + 1) * NB].unsqueeze(2), NT, NB, DM), ALU.mult)
                ins.then_inc(made, 1)
                s.link(V.memset(work[:, :, :], 0.0))
                s.link(V.tensor_copy(work[:, :, 0:1], keep[:, :, 0:1]))
                s.link(V.memset(keep[:, :, 0:1], 0.0))
                s.link(V.memset(eta[:, :, 0:1], 0.0))
                s.link(V.tensor_tensor_scan(flat(work), flat(keep), flat(work), 0.0, ALU.mult, ALU.add))
                s.link(V.memset(M["c_f"][:, :, 0:1], 1.0))
                s.link(V.tensor_copy(M["c_f"][:, :, 1:NT], work[:, :, 0:NT - 1]))
                s.link(V.tensor_tensor(theta[0:NT, :, :], theta[0:NT, :, :], bc(diag[:, :].unsqueeze(1), NT, NB, NT), ALU.mult))
                s.link(V.tensor_tensor_scan(flat(eta)[0:NT], flat(eta)[0:NT], flat(theta)[0:NT], 0.0, ALU.mult, ALU.add))
                s.link(V.tensor_tensor_scan(flat(eta)[0:NT], flat(keep)[0:NT], flat(eta)[0:NT], 0.0, ALU.mult, ALU.add))
                s.link(V.memset(theta[0:NT, :, 0:1], 0.0))
                V.tensor_copy(theta[0:NT, :, 1:NT], eta[0:NT, :, 0:NT - 1]).then_inc(made, 1)
                V.tensor_copy(keep[:, :, :], work[:, :, :]).then_inc(made, 1)
                dve.wait_ge(made, MADE["c"])
                V.tensor_copy(work[0:NT, :, :], eta[0:NT, :, :]).then_inc(made, 1)
                dve.wait_ge(made, MADE["wt"])
                n = 2
                for what in range(4):
                    for g in range(NG if what != 2 else NG // 2):
                        dve.wait_ge(turned, n + 1)
                        src = psT[:, n % 4, 0:N]
                        if what < 2:
                            ins = V.tensor_copy((kT, qT)[what][:, g * N:(g + 1) * N], src[0:DM])
                        elif what == 2:
                            ins = V.tensor_copy(M["v_y"][:, g * G:(g + 1) * G, :].rearrange("p b t -> p (b t)"), src)
                        else:
                            ins = V.tensor_copy(by_chunk(eta)[:, g * G:(g + 1) * G], src[0:NT].rearrange("t (b c s) -> t b c s", b=G, s=NC))
                        ins.then_inc(taken, 1)
                        n += 1
                    if what == 1:
                        dve.wait_ge(taken, n - 2)
                        V.sem_inc(made, 1)
                dve.wait_ge(taken, n - 2)
                V.sem_inc(made, 1)
                qc = fp[0:DM, 0:16, :].rearrange("p a c -> p (a c)")
                V.tensor_tensor(qc, qT[:, :], flat(keep)[0:DM], ALU.mult).then_inc(made, 1)
                for g in range(NG):
                    dve.wait_ge(pe_done, GATES + NB // 2 + g + 1)
                    o = slice(g * G, (g + 1) * G)
                    V.tensor_tensor(by_chunk(theta)[:, o], psT[0:NT, g % 4, 0:N].rearrange("t (b c s) -> t b c s", b=G, s=NC), by_chunk(eta)[:, o], ALU.mult).then_inc(gram_read, 1)
                dve.wait_ge(gram_read, NG)
                V.sem_inc(made, 1)
                dve.wait_ge(k_stored, 16)
                V.tensor_tensor(kT[:, :], kT[:, :], flat(M["c_f"])[0:DM], ALU.mult).then_inc(made, 1)
                for m in range(2 * (NCH - 1)):
                    dve.wait_ge(bs_turned, m + 1)
                    V.tensor_copy((M["w_bs"], M["g_bs"])[m % 2][:, m // 2, :, :].rearrange("p q t -> p (q t)"), psT[:, m % 4, 0:4 * NT]).then_inc(bs_ready, 1)
                dve.wait_ge(bs_ready, 2 * (NCH - 1))


BF16 = mybir.dt.bfloat16
PAIRS = ((0, 0), (0, 1), (1, 0), (1, 1), (0, 2), (2, 0))


def memory_scan(nc, M, H_room, hist_y, ident, cols_in, rows_in, own_in):
    GW = QB * NC
    APART = 4
    with ExitStack() as ctx:
        sb = lambda n, sh: ctx.enter_context(nc.sbuf_tensor("sc_" + n, sh, F32))
        sem = lambda n: ctx.enter_context(nc.semaphore("sc_" + n))
        bf = lambda n, sh: ctx.enter_context(nc.sbuf_tensor("sc_" + n, sh, BF16))
        h_t, dy_t = bf("h_t", [128, NCH - 1, 3, 4, FH]), bf("dy_t", [128, NCH - 1, 3, 2, 128])
        h_f, dy_f = bf("h_f", [128, NCH - 1, 3, 2, NB * NC]), bf("dy_f", [128, NCH - 1, 3, HB * NC])
        b0_f, b0_t = bf("b0_f", [128, 3, 2, 2, 128]), bf("b0_t", [128, 3, FH])
        h_now, dy_now = bf("h_now", [128, 2, 3, 4 * QB]), bf("dy_now", [128, 2, 3, 2 * QB])
        dz_t = sb("dz_t", [128, 4, FH])
        hist_h, hist_dz = sb("hist_h", [128, 2, 2, NB, NC]), sb("hist_dz", [128, 2, 2, NB, NC])
        g_mask = sb("g_mask", [128, NCH - 1, 4, QB, NC])
        wm = sb("wm", [128, 2, 2, NCH - 1, 2 * QB])
        own = sb("own", [128, QB])
        coef, coef_rest = sb("coef", [128, 2, NCH - 1, 2 * QB]), sb("coef_rest", [128, 2, NCH - 1, 2 * QB])
        coef_y, coef_h = bf("coef_y", [128, 2, 3, NCH - 1, 2 * QB]), bf("coef_h", [128, 2, 3, NCH - 1, 2 * QB])
        room = H_room[:, :, :].rearrange("p b d -> p (b d)")
        prod, z_prod = (room[:, n * 1024:(n + 1) * 1024].rearrange("p (g a x) -> p g a x", g=2, a=2) for n in range(2))
        dy_rest = sb("dy_rest", [128, 2 * GW])
        now_rest = sb("now_rest", [128, 2, 4 * QB])
        y_prod = sb("y_prod", [128, 2, GW])
        y_w = sb("y_w", [128, 2, GW])
        w_row = sb("w_row", [128, 2, HB * NC])
        g_row = sb("g_row", [128, 2, NB * NC])
        past_sum, zsum, z_before, z, sg, slope, hs, hg, first_part, dh, dh2 = (sb(n, [128, 2, 4 * QB]) for n in ("past_sum", "zsum", "z_before", "z", "sg", "slope", "hs", "hg", "first_part", "dh", "dh2"))
        pred, off, ysum, rest = (sb(n, [128, 2, QB]) for n in ("pred", "off", "ysum", "rest"))
        dy_pad = sb("dy_pad", [128, 2, 2, QB])
        cols, rows_ = sb("cols", [128, 2, 128]), sb("rows", [128, 2, 128])
        ps = ctx.enter_context(nc.psum_tensor("sc_ps", [128, 8, 512], F32))
        score_h = lambda g: ps[:, g, 0:(NCH - 1) * 2 * QB].rearrange("p (c j) -> p c j", c=NCH - 1)
        score_y = lambda g: ps[:, g, 128:128 + (NCH - 1) * 2 * QB].rearrange("p (c j) -> p c j", c=NCH - 1)
        first_y = lambda g: ps[:, g, 256:256 + QB]
        first_h = lambda g: ps[:, g, 320:320 + 4 * QB]
        hh = lambda g: ps[:, 2 + g, 0:GW]
        yy = lambda g: ps[:, 2 + g, GW:3 * GW]
        past_y = lambda g: ps[:, 4 + g, 0:2 * QB]
        past_h = lambda g: ps[:, 4 + g, 64:64 + 4 * QB]
        past_h3 = lambda g: ps[:, 4 + g, 64:64 + 12 * QB].rearrange("p (x m b) -> p x m b", x=4, m=3)
        base_bank = lambda n: 6 if n % 2 == 0 else 2
        quads = lambda x: x.rearrange("p (a c b) -> p a c b", a=2, c=2)
        h_at = lambda x, g, c, i: x[:, :, c % 2, :, bass.ds(i, 1)].rearrange("p a (c b) s -> p a c (b s)", c=2)[:, :, :, QB * g:QB * (g + 1)]
        y_at = lambda g, c, i: hist_y[:, c, QB * g:QB * (g + 1), bass.ds(i, 1)].rearrange("p b s -> p (b s)")
        cols_at = lambda x, g, t: x[:, QB * g:QB * (g + 1), bass.ds(t, 1)].rearrange("p b s -> p (b s)")
        chunk = lambda x, a, g, c: x[:, a, c % 2, :, :].rearrange("p (c b) s -> p c b s", c=2)[:, :, QB * g:QB * (g + 1), :]
        both = lambda x, g, c: x[:, :, c % 2, :, :].rearrange("p a (c b) s -> p a c (b s)", c=2)[:, :, :, GW * g:GW * (g + 1)]
        w_in, g_rows_in = [sem("w_in0"), sem("w_in1")], [sem("g_in0"), sem("g_in1")]
        parts_ready, split_ready, hi_ready, rest_ready, mid_ready, dumped = sem("parts_ready"), sem("split_ready"), sem("hi_ready"), sem("rest_ready"), sem("mid_ready"), [sem("dumped0"), sem("dumped1")]
        ones_in, zeroed, step = sem("ones_in"), sem("zeroed"), sem("step")
        z_ready, sg_ready, h_ready, slope_ready = sem("z_ready"), sem("sg_ready"), sem("h_ready"), sem("slope_ready")
        scores_done, coef_ready, prod_ready, hh_done, past_y_done = (sem(n) for n in ("scores_done", "coef_ready", "prod_ready", "hh_done", "past_y_done"))
        yw_ready, dy_ready, yprod_ready, yy_done, past_h_done = (sem(n) for n in ("yw_ready", "dy_ready", "yprod_ready", "yy_done", "past_h_done"))
        summed, zprod_ready, dz_ready, pool_step, wm_ready = sem("summed"), sem("zprod_ready"), sem("dz_ready"), sem("pool_step"), sem("wm_ready")
        turned, h_kept, dz_kept, base_done, base_added, g_masked = (sem(n) for n in ("turned", "h_kept", "dz_kept", "base_done", "base_added", "g_masked"))

        def split_work(c):
            s, flat = (c - 1) % 2, "p a x -> p (a x)"
            slot = hist_h[:, :, s, :, :].rearrange("p a b s -> p a (b s)")
            yield slot, lambda w: h_f[:, c - 1, w, :, :], room[:, 0:1024].rearrange("p (a x) -> p a x", a=2)
            yield (hist_y[:, c - 1, :, :].rearrange(flat), lambda w: dy_f[:, c - 1, w, :], y_prod[:, :, :].rearrange(flat))
            yield (ps[:, 0:2, :].rearrange(flat), lambda w: h_t[:, c - 1, w, :, :].rearrange(flat), room[:, 1024:2048])
            yield ps[:, 4, 0:2 * GW], lambda w: dy_t[:, c - 1, w, :, :].rearrange(flat), dy_rest[:, :]

        with nc.Block() as block:
            @block.sync
            def _(sp):
                sp.dma_start(cols[:, :, :], cols_in).then_inc(ones_in, 16)
                sp.dma_start(rows_[:, :, :], rows_in).then_inc(ones_in, 16)
                sp.dma_start(own[:, :], own_in).then_inc(ones_in, 16)
                for c in range(NCH):
                    def rows(k, t, turn):
                        if turn is not None:
                            sp.wait_ge(yw_ready, 2 * turn)
                            sp.wait_ge(z_ready, 2 * turn)
                        for b2 in range(2):
                            sp.dma_start(w_row[b2 * DM:(b2 + 1) * DM, k, :],
                                         M["w_rows"][bass.ds(t, 1), c, b2 * HB:(b2 + 1) * HB, :].rearrange("t b s -> t (b s)").broadcast_to([DM, HB * NC])).then_inc(w_in[k], 16)
                        sp.dma_start(g_row[:, k, :], M["g_rows"][bass.ds(t, 1), c, :, :].rearrange("t b s -> t (b s)").broadcast_to([128, NB * NC])).then_inc(g_rows_in[k], 16)

                    if c == 0:
                        for k in range(2):
                            rows(k, k, None)
                        with sp.Fori(1, NC // 2) as i:
                            for k in range(2):
                                rows(k, 2 * i + k, 2 * i + k - 1)
                    else:
                        with sp.Fori(0, NC // 2) as i:
                            for k in range(2):
                                rows(k, c * NC + 2 * i + k, c * NC + 2 * i + k - 1)
                for n in range(2):
                    sp.wait_ge(dumped[n], 16 * NCH)

            @block.gpsimd
            def _(pool):
                P = nc.gpsimd
                for t in (hist_h, hist_dz):
                    P.memset(t[:, :, :, :, :], 0.0).then_inc(zeroed, 1)
                P.memset(hist_y[:, :, :, :], 0.0).then_inc(zeroed, 1)
                P.memset(dy_pad[:, :, :, :], 0.0).then_inc(zeroed, 1)
                P.memset(dy_now[:, :, :, :], 0.0).then_inc(zeroed, 1)
                pool.wait_ge(zeroed, 5)
                pool.wait_ge(ones_in, 48)
                for c in range(NCH):
                    pool.wait_ge(g_rows_in[0], (c * NC // 2) * 16 + 16)
                    if c >= 2:
                        pool.wait_ge(zeroed, 5 + c - 1)

                    def one_step(i, k, last):
                        t = c * NC + 2 * i + k
                        if c >= 1:
                            pool.wait_ge(dz_ready, 2 * t - 2)
                            for g in range(2):
                                P.tensor_tensor(wm[:, k, g, 0:c, :].rearrange("p c (q b) -> p c q b", q=2),
                                                      bc(M["w_bs"][:, 0:c, :, bass.ds(t, 1)].rearrange("p c (q h) t -> p c q (h t)", q=2)[:, :, :, g:g + 1], 128, c, 2, QB),
                                                      bc(own[:, :].unsqueeze(1).unsqueeze(1), 128, c, 2, QB), ALU.mult).then_inc(wm_ready, 1)
                        pool.wait_ge(w_in[k], (c * NC + 2 * i) * 16 + 32)
                        for g in range(2):
                            pool.wait_ge(yprod_ready, 2 * t + g + 1)
                            P.tensor_tensor(y_w[:, g, :], w_row[:, k, g * GW:(g + 1) * GW],
                                            hist_y[:, c, g * QB:(g + 1) * QB, :].rearrange("p b s -> p (b s)"), ALU.mult).then_inc(yw_ready, 1)
                        for g in range(2):
                            pool.wait_ge(h_ready, 2 * t + g + 1)
                            for a in range(2):
                                ins = P.tensor_tensor(prod[:, g, a, :].rearrange("p (c b s) -> p c b s", c=2, s=NC), chunk(hist_h, a, g, c),
                                                      bc(hist_h[:, a, c % 2, :, bass.ds(2 * i + k, 1)].rearrange("p (c b) s -> p c b s", c=2)[:, :, QB * g:QB * (g + 1), :], 128, 2, QB, NC), ALU.mult)
                            ins.then_inc(prod_ready, 1)
                            h = h_at(hist_h, g, c, 2 * i + k)
                            P.tensor_tensor(quads(hg[:, g, :]), h, quads(sg[:, g, :]), ALU.mult)
                            P.tensor_tensor(quads(hs[:, g, :]), h, quads(sg[:, g, :]), ALU.add).then_inc(pool_step, 1)
                            pool.wait_ge(pool_step, 2 * t + g + 1)
                            P.tensor_tensor(slope[:, g, :], hs[:, g, :], hg[:, g, :], ALU.subtract).then_inc(slope_ready, 1)
                        if not last:
                            pool.wait_ge(g_rows_in[1 - k], (c * NC // 2 + i + k) * 16 + 16)
                            for g in range(2):
                                P.tensor_tensor(z_prod[:, g, :, :].rearrange("p a (c x) -> p a c x", c=2), both(hist_dz, g, c),
                                                bc(g_row[:, 1 - k, :].rearrange("p (c x) -> p c x", c=2)[:, :, GW * g:GW * (g + 1)].unsqueeze(1), 128, 2, 2, GW), ALU.mult).then_inc(zprod_ready, 1)

                    with pool.Fori(0, NC // 2 - 1) as i:
                        for k in range(2):
                            one_step(i, k, False)
                    for k in range(2):
                        one_step(NC // 2 - 1, k, k == 1)
                    if 1 <= c < NCH - 1:
                        pool.wait_ge(dumped[(c - 1) % 2], 32 * ((c - 1) // 2 + 1))
                        pool.wait_ge(turned, 5 * c)
                        P.memset(hist_dz[:, :, (c + 1) % 2, :, :], 0.0).then_inc(zeroed, 1)

            @block.scalar
            def _(act):
                A = nc.scalar.activation

                def dump(c):
                    for n, x in (("h", hist_h), ("dz", hist_dz)):
                        nc.scalar.dma_start(M["hist_" + n][:, :, c, :, :], x[:, :, c % 2, :, :]).then_inc(dumped[c % 2], 16)

                act.wait_ge(ones_in, 48)
                for c in range(NCH):
                    if c >= 1:
                        n = 4 * (c - 1)
                        act.wait_ge(h_ready, 2 * c * NC)
                        for j, (src, parts, rest) in enumerate(split_work(c)):
                            if j == 1:
                                act.wait_ge(dz_ready, 2 * c * NC)
                                dump(c - 1)
                            elif j >= 2:
                                act.wait_ge(turned, 5 * (c - 1) + j + 2)
                            A(parts(0), src, ACT.Copy).then_inc(hi_ready, 1)
                        for j, (src, parts, rest) in enumerate(split_work(c)):
                            act.wait_ge(rest_ready, n + j + 1)
                            A(parts(1), rest, ACT.Copy).then_inc(mid_ready, 1)
                        act.wait_ge(base_done, c * (2 * NCH - 1 - c) // 2)
                    with act.Fori(0, NC // 2) as i:
                        for k in range(2):
                            for g in range(2):
                                act.wait_ge(z_ready, 2 * (c * NC + 2 * i + k) + g + 1)
                                A(sg[:, g, :], z[:, g, :], ACT.Sigmoid).then_inc(sg_ready, 1)
                        if c < NCH - 1:
                            A(g_mask[:, c:NCH - 1, :, bass.ds(i, 1), :].rearrange("p c q b t -> p c q (b t)"),
                              M["g_bs"][:, c, :, (c + 1) * NC:NT].rearrange("p q (c t) -> p c q t", t=NC), ACT.Copy,
                              scale=own[:, bass.ds(i, 1)]).then_inc(g_masked, 1)
                act.wait_ge(dz_ready, 2 * NT)
                dump(NCH - 1)

            @block.tensor
            def _(pe):
                MM, T = nc.tensor.matmul, nc.tensor.transpose
                pe.wait_ge(ones_in, 48)
                pe.wait_ge(split_ready, 1)
                for c in range(NCH):
                    if c >= 1:
                        pe.wait_ge(dz_ready, 2 * c * NC)
                        for n, x in ((2, hist_dz), (0, hist_h)):
                            for q in range(4):
                                for a in range(2):
                                    mm = T(ps[:, n + q // 2, (q % 2 * 2 + a) * 128:(q % 2 * 2 + a + 1) * 128],
                                           x[:, a, (c - 1) % 2, q * QB:(q + 1) * QB, :].rearrange("p b s -> p (b s)"), ident[:, :])
                                if q % 2 == 1:
                                    mm.then_inc(turned, 1)
                        for g in range(2):
                            mm = T(ps[:, 4, g * 128:(g + 1) * 128], hist_y[:, c - 1, g * QB:(g + 1) * QB, :].rearrange("p b s -> p (b s)"), ident[:, :])
                        mm.then_inc(turned, 1)
                        pe.wait_ge(dz_kept, 2 * c)
                        pe.wait_ge(g_masked, c * NC // 2)
                        for cc in range(c, NCH):
                            n = (c - 1) * (2 * NCH - c) // 2 + cc - c
                            if n >= 2:
                                pe.wait_ge(base_added, 2 * (n - 1))
                            for a in range(2):
                                for q in range(4):
                                    mm = MM(ps[:, base_bank(cc - c) + a, q * GW:(q + 1) * GW], dz_t[:, q, a * 128:(a + 1) * 128],
                                            g_mask[:, cc - 1, q, :, :].rearrange("p b t -> p (b t)"), start=True, stop=True)
                            mm.then_inc(base_done, 1)
                        pe.wait_ge(split_ready, c + 1)
                    with pe.Fori(0, NC) as i:
                        t = c * NC + i

                        def forward_scores(g):
                            now = lambda a, b2, m: h_now[:, g, m, (2 * a + b2) * QB:(2 * a + b2 + 1) * QB]
                            pe.wait_ge(parts_ready, 4 * t + g + 1)
                            for cc in range(c):
                                for b2 in range(2):
                                    for n, (a, (w, m)) in enumerate((a, p) for a in range(2) for p in PAIRS):
                                        MM(score_h(g)[:, cc, b2 * QB:(b2 + 1) * QB], h_f[:, cc, w, a, (2 * b2 + g) * GW:(2 * b2 + g + 1) * GW], now(a, b2, m),
                                           start=n == 0, stop=n == 11)
                            for n, (a, b2, (w, m)) in enumerate((a, b2, p) for a in range(2) for b2 in range(2) for p in PAIRS):
                                mm = MM(first_y(g), b0_f[:, w, a, b2, :], now(a, b2, m), start=n == 0, stop=n == 23)
                            mm.then_inc(scores_done, 1)
                            pe.wait_ge(prod_ready, 2 * t + g + 1)
                            for a in range(2):
                                for b2 in range(2):
                                    mm = MM(hh(g), cols[:, b2, :], prod[:, g, a, b2 * GW:(b2 + 1) * GW], start=a + b2 == 0, stop=a + b2 == 2)
                            mm.then_inc(hh_done, 1)

                        def forward_past(g):
                            if c >= 1:
                                pe.wait_ge(coef_ready, 4 * (t - NC) + g + 1)
                                for n, (cc, (w, m)) in enumerate((cc, p) for cc in range(c) for p in PAIRS):
                                    mm = MM(past_y(g), dy_t[:, cc, w, g, :], coef_y[:, g, m, cc, :], start=n == 0, stop=n == 6 * c - 1)
                                mm.then_inc(past_y_done, 1)

                        def backward_scores(g):
                            pe.wait_ge(parts_ready, 4 * t + 2 + g + 1)
                            for cc in range(c):
                                for n, (w, m) in enumerate(PAIRS):
                                    MM(score_y(g)[:, cc, :], dy_f[:, cc, w, g * GW:(g + 1) * GW], dy_now[:, g, m, :], start=n == 0, stop=n == 5)
                            for a in range(2):
                                for n, (w, m) in enumerate(PAIRS):
                                    mm = MM(first_h(g)[:, a * 2 * QB:(a + 1) * 2 * QB], b0_t[:, w, a * 128:(a + 1) * 128], dy_now[:, g, m, :], start=n == 0, stop=n == 5)
                            mm.then_inc(scores_done, 1)
                            pe.wait_ge(yprod_ready, 2 * t + g + 3)
                            for b2 in range(2):
                                mm = MM(yy(g)[:, b2 * GW:(b2 + 1) * GW], rows_[:, b2, :], y_prod[:, g, :], start=True, stop=True)
                            mm.then_inc(yy_done, 1)

                        def backward_past(g):
                            if c >= 1:
                                pe.wait_ge(coef_ready, 4 * (t - NC) + 2 + g + 1)
                            if c >= APART:
                                for a in range(2):
                                    for b2 in range(2):
                                        for cc in range(c):
                                            for w in range(3):
                                                mm = MM(past_h3(g)[:, 2 * a + b2, 0:3 - w, :], h_t[:, cc, w, 2 * b2 + g, a * 128:(a + 1) * 128],
                                                        coef_h[:, g, 0:3 - w, cc, b2 * QB:(b2 + 1) * QB], start=cc + w == 0, stop=True, skip_group_check=True)
                                mm.then_inc(past_h_done, 1)
                            elif c >= 1:
                                for a in range(2):
                                    for b2 in range(2):
                                        o = (2 * a + b2) * QB
                                        for n, (cc, (w, m)) in enumerate((cc, p) for cc in range(c) for p in PAIRS):
                                            mm = MM(past_h(g)[:, o:o + QB], h_t[:, cc, w, 2 * b2 + g, a * 128:(a + 1) * 128], coef_h[:, g, m, cc, b2 * QB:(b2 + 1) * QB],
                                                    start=n == 0, stop=n == 6 * c - 1)
                                mm.then_inc(past_h_done, 1)

                        forward_scores(0)
                        forward_past(0)
                        forward_scores(1)
                        backward_scores(0)
                        forward_past(1)
                        backward_past(0)
                        backward_scores(1)
                        backward_past(1)

            @block.vector
            def _(dve):
                V = nc.vector
                V.sem_inc(yprod_ready, 2)
                s = Steps(dve, step)
                for parts, x, left in ((lambda w: b0_f[:, w, :, :, :].rearrange("p a c m -> p (a c m)"), M["b0"][:, :, :, :].rearrange("p a c m -> p (a c m)"), room[:, 0:512]),
                                       (lambda w: b0_t[:, w, :], M["b0t"][:, :], room[:, 1024:1024 + FH])):
                    s.link(V.tensor_copy(parts(0), x))
                    V.tensor_tensor(parts(1), x, parts(0), ALU.subtract)
                    s.link(V.tensor_tensor(left, x, parts(0), ALU.subtract))
                    s.link(V.tensor_tensor(parts(2), left, parts(1), ALU.subtract))
                V.sem_inc(split_ready, 1)
                K0 = s.n
                dve.wait_ge(zeroed, 5)
                KS, KP, K1, KL = 38, 2, 10, 8

                for c in range(NCH):
                    base_at = lambda g, t: M["z_base"][:, :, :, bass.ds(t, 1)].rearrange("p a (c b) s -> p a c (b s)", c=2)[:, :, :, QB * g:QB * (g + 1)]

                    def hidden_before(s, g, t):
                        dve.wait_ge(zprod_ready, 2 * (t - c - 1) + g + 1)
                        s.link(V.reduce_sum(zsum[:, g, :], z_prod[:, g, :, :].rearrange("p a (b s) -> p (a b) s", s=NC), AX.X))
                        s.mark(V.tensor_tensor(quads(z_before[:, g, :]), quads(zsum[:, g, :]), base_at(g, t), ALU.add))

                    def hidden(s, g, t, i, k, turn):
                        dve.wait_ge(g_rows_in[k], turn * 16 + 16)
                        weight = g_row[:, k, :].rearrange("p (b s) -> p b s", s=NC)[:, :, bass.ds(i, 1)].rearrange("p (c b) s -> p c (b s)", c=2)[:, :, QB * g:QB * (g + 1)]
                        s.link(V.tensor_tensor(quads(zsum[:, g, :]), h_at(hist_dz, g, c, i), bc(weight.unsqueeze(1), 128, 2, 2, QB), ALU.mult))
                        V.tensor_tensor(z[:, g, :], z_before[:, g, :], zsum[:, g, :], ALU.add).then_inc(z_ready, 1)

                    def weigh_high(s, parts, score, g, k):
                        if c >= 1:
                            V.tensor_tensor(parts[:, g, 0, 0:c, :], score(g)[:, 0:c, :], wm[:, k, g, 0:c, :], ALU.mult)
                            s.mark(V.tensor_tensor(coef[:, g, 0:c, :], score(g)[:, 0:c, :], wm[:, k, g, 0:c, :], ALU.mult))

                    def weigh_middle(s, parts, g):
                        if c >= 1:
                            dve.wait_ge(step, s.base + s.n)
                            V.tensor_tensor(parts[:, g, 1, 0:c, :], coef[:, g, 0:c, :], parts[:, g, 0, 0:c, :], ALU.subtract)
                            s.mark(V.tensor_tensor(coef_rest[:, g, 0:c, :], coef[:, g, 0:c, :], parts[:, g, 0, 0:c, :], ALU.subtract))

                    def weigh_low(s, parts, g):
                        if c >= 1:
                            dve.wait_ge(step, s.base + s.n)
                            V.tensor_tensor(parts[:, g, 2, 0:c, :], coef_rest[:, g, 0:c, :], parts[:, g, 1, 0:c, :], ALU.subtract).then_inc(coef_ready, 1)

                    def silu(s, g, t, i):
                        dve.wait_ge(sg_ready, 2 * t + g + 1)
                        V.tensor_tensor(h_at(hist_h, g, c, i), quads(z[:, g, :]), quads(sg[:, g, :]), ALU.mult).then_inc(h_ready, 1)
                        hi, mid, lo = (h_now[:, g, w, :] for w in range(3))
                        s.link(V.tensor_tensor(hi, z[:, g, :], sg[:, g, :], ALU.mult))
                        dve.wait_ge(h_ready, 2 * t + g + 1)
                        V.tensor_tensor(quads(mid), h_at(hist_h, g, c, i), quads(hi), ALU.subtract)
                        s.link(V.tensor_tensor(quads(now_rest[:, g, :]), h_at(hist_h, g, c, i), quads(hi), ALU.subtract))
                        V.tensor_tensor(lo, now_rest[:, g, :], mid, ALU.subtract).then_inc(parts_ready, 1)

                    def output(s, g, t, k):
                        dve.wait_ge(scores_done, 4 * t + g + 1)
                        if c >= 1:
                            dve.wait_ge(wm_ready, 2 * (t - NC) + g + 1)
                        weigh_high(s, coef_y, score_h, g, k)
                        for b2 in range(2):
                            h, o = slice(b2 * DM, (b2 + 1) * DM), b2 * HB + g * QB
                            ins = V.scalar_tensor_tensor(pred[h, g, :], first_y(g)[h], 2.0 / DM, M["c_f"][h, o:o + QB, bass.ds(t, 1)].rearrange("p b s -> p (b s)"), ALU.mult, ALU.mult)
                        s.mark(ins)
                        weigh_middle(s, coef_y, g)
                        if c == 0:
                            dve.wait_ge(step, s.base + s.n)
                        s.mark(V.scalar_tensor_tensor(off[:, g, :], cols_at(M["v_y"], g, t), -2.0 / DM, pred[:, g, :], ALU.mult, ALU.add))
                        weigh_low(s, coef_y, g)
                        dve.wait_ge(hh_done, 2 * t + g + 1)
                        dve.wait_ge(yw_ready, 2 * t + g + 1)
                        s.link(V.tensor_tensor(y_prod[:, g, :], hh(g), y_w[:, g, :], ALU.mult))
                        s.link(V.reduce_sum(ysum[:, g, :], y_prod[:, g, :].rearrange("p (b s) -> p b s", s=NC), AX.X))

                    def output_end(s, g, t, i):
                        if c >= 1:
                            dve.wait_ge(past_y_done, 2 * (t - NC) + g + 1)
                            for b2 in range(2):
                                h = slice(b2 * DM, (b2 + 1) * DM)
                                ins = V.scalar_tensor_tensor(rest[h, g, :], past_y(g)[h, b2 * QB:(b2 + 1) * QB], 2.0 / DM, off[h, g, :], ALU.mult, ALU.add)
                        else:
                            ins = V.tensor_copy(rest[:, g, :], off[:, g, :])
                        s.link(ins)
                        for b2 in range(2):
                            h = slice(b2 * DM, (b2 + 1) * DM)
                            V.scalar_tensor_tensor(dy_pad[h, g, b2, :], ysum[h, g, :], 2.0 / DM, rest[h, g, :], ALU.mult, ALU.add)
                            V.scalar_tensor_tensor(dy_now[h, g, 0, b2 * QB:(b2 + 1) * QB], ysum[h, g, :], 2.0 / DM, rest[h, g, :], ALU.mult, ALU.add)
                        V.scalar_tensor_tensor(y_at(g, c, i), ysum[:, g, :], 2.0 / DM, rest[:, g, :], ALU.mult, ALU.add).then_inc(dy_ready, 1)
                        dve.wait_ge(dy_ready, 2 * t + g + 1)
                        full = dy_pad[:, g, :, :].rearrange("p c b -> p (c b)")
                        V.tensor_tensor(dy_now[:, g, 1, :], full, dy_now[:, g, 0, :], ALU.subtract)
                        s.mark(V.tensor_tensor(now_rest[:, g, 0:2 * QB], full, dy_now[:, g, 0, :], ALU.subtract))
                        V.tensor_tensor(y_prod[:, g, :].rearrange("p (b s) -> p b s", s=NC), y_w[:, g, :].rearrange("p (b s) -> p b s", s=NC),
                                        bc(hist_y[:, c, QB * g:QB * (g + 1), bass.ds(i, 1)], 128, QB, NC), ALU.mult).then_inc(yprod_ready, 1)
                        dve.wait_ge(step, s.base + s.n)
                        V.tensor_tensor(dy_now[:, g, 2, :], now_rest[:, g, 0:2 * QB], dy_now[:, g, 1, :], ALU.subtract).then_inc(parts_ready, 1)

                    def gradient_first(g, t):
                        cf = M["c_f"][:, :, bass.ds(t, 1)].rearrange("p (c b) s -> p c (b s)", c=2)[:, :, QB * g:QB * (g + 1)]
                        V.tensor_tensor(quads(first_part[:, g, :]), quads(first_h(g)), bc(cf.unsqueeze(1), 128, 2, 2, QB), ALU.mult)

                    def gradient_chunk(s, g, t):
                        dve.wait_ge(yy_done, 2 * t + g + 1)
                        s.link(V.tensor_tensor(prod[:, g, :, :].rearrange("p a (c x) -> p a c x", c=2), both(hist_h, g, c),
                                               bc(yy(g).rearrange("p (c x) -> p c x", c=2).unsqueeze(1), 128, 2, 2, GW), ALU.mult))
                        s.link(V.reduce_sum(dh[:, g, :], prod[:, g, :, :].rearrange("p a (b s) -> p (a b) s", s=NC), AX.X))

                    def add_first(s, g, t):
                        s.mark(V.tensor_tensor(dh2[:, g, :], dh[:, g, :], first_part[:, g, :], ALU.add))

                    def add_past(s, g, t):
                        if c >= 1:
                            dve.wait_ge(past_h_done, 2 * (t - NC) + g + 1)
                            if c >= APART:
                                V.reduce_sum(past_sum[:, g, :].rearrange("p (x b) -> p x b", x=4), past_h3(g).rearrange("p x m b -> p x b m"), AX.X).then_inc(summed, 1)
                                dve.wait_ge(summed, 2 * (t - APART * NC) + g + 1)
                            past = past_sum[:, g, :] if c >= APART else past_h(g)
                            s.mark(V.tensor_tensor(dh[:, g, :], dh2[:, g, :], past, ALU.add))

                    def gradient_end(s, g, t, i):
                        dve.wait_ge(slope_ready, 2 * t + g + 1)
                        dve.wait_ge(step, s.base + s.n)
                        d = dh if c >= 1 else dh2
                        V.tensor_tensor(h_at(hist_dz, g, c, i), quads(d[:, g, :]), quads(slope[:, g, :]), ALU.mult).then_inc(dz_ready, 1)

                    if c >= 1:
                        work = list(enumerate(split_work(c)))

                        def what_is_left(jobs):
                            for j, (src, parts, left) in jobs:
                                dve.wait_ge(hi_ready, 4 * (c - 1) + j + 1)
                                V.tensor_tensor(left, src, parts(0), ALU.subtract).then_inc(rest_ready, 1)

                        what_is_left(work[:2])
                        for n in range(2):
                            dve.wait_ge(turned, 5 * (c - 1) + 1 + n)
                            V.tensor_copy(dz_t[:, 2 * n:2 * n + 2, :].rearrange("p g f -> p (g f)"), ps[:, 2 + n, :]).then_inc(dz_kept, 1)
                        what_is_left(work[2:])

                        def add_base(cc):
                            m = (c - 1) * (2 * NCH - c) // 2 + cc - c
                            dve.wait_ge(base_done, m + 1)
                            for a in range(2):
                                part = M["z_base"][:, a, :, cc * NC:(cc + 1) * NC]
                                V.tensor_tensor(part, part, ps[:, base_bank(cc - c) + a, :].rearrange("p (b s) -> p b s", s=NC), ALU.add).then_inc(base_added, 1)
                            return 2 * m + 2

                        added = add_base(c)
                        for j, (src, parts, left) in work:
                            dve.wait_ge(mid_ready, 4 * (c - 1) + j + 1)
                            dve.wait_ge(rest_ready, 4 * (c - 1) + j + 1)
                            ins = V.tensor_tensor(parts(2), left, parts(1), ALU.subtract)
                        ins.then_inc(split_ready, 1)
                        dve.wait_ge(split_ready, c + 1)
                        for cc in range(c + 1, NCH):
                            added = add_base(cc)
                        dve.wait_ge(base_added, added)
                    if c >= 2:
                        dve.wait_ge(dumped[c % 2], 32 * (c // 2))
                        dve.wait_ge(zeroed, 5 + c - 1)
                    ks = KS if c >= 1 else KS - K1
                    start = K0 + (0 if c == 0 else NC * (KS - K1) - KL + KP + (c - 1) * (NC * KS - KL + KP))
                    s = Steps(dve, step, start)
                    for g in range(2):
                        V.tensor_copy(quads(z[:, g, :]), base_at(g, c * NC)).then_inc(z_ready, 1)
                    silu(s, 0, c * NC, 0)
                    assert s.n == KP, s.n

                    def one_step(turn, k, i, last):
                        t = c * NC + i
                        s = Steps(dve, step, start + KP + i * ks)
                        silu(s, 1, t, i)
                        output(s, 0, t, k)
                        output_end(s, 0, t, i)
                        if not last:
                            hidden_before(s, 0, t + 1)
                        output(s, 1, t, k)
                        dve.wait_ge(scores_done, 4 * t + 3)
                        weigh_high(s, coef_h, score_y, 0, k)
                        gradient_first(0, t)
                        weigh_middle(s, coef_h, 0)
                        weigh_low(s, coef_h, 0)
                        if not last:
                            hidden_before(s, 1, t + 1)
                        output_end(s, 1, t, i)
                        gradient_chunk(s, 0, t)
                        dve.wait_ge(scores_done, 4 * t + 4)
                        weigh_high(s, coef_h, score_y, 1, k)
                        gradient_first(1, t)
                        add_first(s, 0, t)
                        weigh_middle(s, coef_h, 1)
                        add_past(s, 0, t)
                        weigh_low(s, coef_h, 1)
                        gradient_end(s, 0, t, i)
                        if not last:
                            dve.wait_ge(dz_ready, 2 * t + 1)
                            hidden(s, 0, t + 1, i, 1 - k, turn + k)
                            silu(s, 0, t + 1, i + 1)
                        gradient_chunk(s, 1, t)
                        add_first(s, 1, t)
                        dve.wait_ge(step, s.base + s.n)
                        add_past(s, 1, t)
                        gradient_end(s, 1, t, i)
                        if not last:
                            dve.wait_ge(dz_ready, 2 * t + 2)
                            hidden(s, 1, t + 1, i, 1 - k, turn + k)
                        assert s.n == ks - (KL if last else 0), s.n

                    with dve.Fori(0, NC // 2 - 1) as j:
                        for k in range(2):
                            one_step(c * NC // 2 + j, k, 2 * j + k, False)
                    for k in range(2):
                        one_step(c * NC // 2 + NC // 2 - 1, k, NC - 2 + k, k == 1)
                    dve.wait_ge(dz_ready, 2 * (c + 1) * NC)


def memory_outputs(nc, M, H, hist_y, ident):
    NS = 4
    NR = HB // 2
    with ExitStack() as ctx:
        sb = lambda n, sh: ctx.enter_context(nc.sbuf_tensor("mo_" + n, sh, F32))
        sem = lambda n: ctx.enter_context(nc.semaphore("mo_" + n))
        hist_h, hist_dz = sb("hist_h", [128, 2, NCH, NB, NC]), sb("hist_dz", [128, 2, NCH, NB, NC])
        h_back, hist_in = sem("h_back"), [sem("hist_in0"), sem("hist_in1")]
        kq = sb("kq", [DM, 3, 2, NS, NT])
        w = sb("w", [NT, 2, NS, NT])
        cn = sb("cn", [128, 2, NS, NT])
        dz, hs = sb("dz", [128, 2, NS, 2, NT]), sb("hs", [128, 2, NS, 2, NT])
        dzt = sb("dzt", [NT, NS, FH])
        dy = sb("dy", [128, HB, NT])
        dyt = sb("dyt", [NT, HB, 128])
        s1, s2 = sb("s1", [NT, NS, NT]), sb("s2", [NT, NS, NT])
        sg, hq, hqc = (sb(n, [128, NS, 2, NT]) for n in ("sg", "hq", "hqc"))
        psA = ctx.enter_context(nc.psum_tensor("mo_psA", [128, NS, 512], F32))
        psB = ctx.enter_context(nc.psum_tensor("mo_psB", [128, NS, 512], F32))
        loaded = [sem("loaded0"), sem("loaded1")]
        dy_turned, dyt_ready, staged, dz_turned, dzt_ready = sem("dy_turned"), sem("dyt_ready"), sem("staged"), sem("dz_turned"), sem("dzt_ready")
        s1_done, s1_ready, z_done, sg_ready, hq_ready = sem("s1_done"), sem("s1_ready"), sem("z_done"), sem("sg_ready"), sem("hq_ready")
        hqc_ready, s2_done, s2_ready, out_done, added = sem("hqc_ready"), sem("s2_done"), sem("s2_ready"), sem("out_done"), sem("added")
        dy_rowed = sem("dy_rowed")
        LOADS = 16 * 10
        batch = lambda i, k: 2 * i + k // 2 + HB * (k % 2)
        zq = lambda k: psA[:, k, 256:256 + 2 * NT].rearrange("p (a t) -> p a t", a=2)
        with nc.Block() as block:
            @block.sync
            def _(sp):
                def load(i, r):
                    for h in range(2):
                        cols = bass.ds((2 * i + HB * h) * NT, 2 * NT)
                        two = lambda x: x.rearrange("p (q h) t -> p q h t", h=2)[:, :, h, :]
                        for dst, n in ((kq[:, 0, r], "k_t"), (kq[:, 1, r], "q_t"), (kq[:, 2, r], "qc_t"), (w[:, r], "w_t"), (cn[:, r], "c_now")):
                            sp.dma_start(two(dst), M[n][:, cols].rearrange("p (q t) -> p q t", q=2)).then_inc(loaded[r], 16)

                def past(n):
                    for x, name in ((hist_dz, "hist_dz"), (hist_h, "hist_h")):
                        for h in range(2):
                            o = slice(h * HB + n * HB // 2, h * HB + (n + 1) * HB // 2)
                            for a in range(2):
                                sp.dma_start(x[:, a, :, o, :], M[name][:, a, :, o, :]).then_inc(hist_in[n], 16)

                load(0, 0)
                past(0)
                load(1, 1)
                sp.dma_start(H[0:NT, :, :], M["h"]).then_inc(h_back, 16)
                past(1)
                with sp.Fori(1, NR // 2) as j:
                    for r in range(2):
                        sp.wait_ge(out_done, NS * (2 * j + r) - NS)
                        load(2 * j + r, r)

            @block.gpsimd
            def _(pool):
                P = nc.gpsimd
                P.tensor_copy(dy[:, :, :].rearrange("p b (c s) -> p c b s", s=NC), hist_y[:, :, :, :]).then_inc(dy_rowed, 1)

                def stage(i, r, k):
                    b = batch(i, k)
                    P.tensor_copy(dz[:, r, k, :, :].rearrange("p a (c s) -> p a c s", s=NC), hist_dz[:, :, :, bass.ds(b, 1), :].rearrange("p a c b s -> p a c (b s)"))
                    P.tensor_copy(hs[:, r, k, :, :].rearrange("p a (c s) -> p a c s", s=NC), hist_h[:, :, :, bass.ds(b, 1), :].rearrange("p a c b s -> p a c (b s)")).then_inc(staged, 1)

                def scale(i, r, k):
                    pool.wait_ge(hq_ready, NS * i + k + 1)
                    P.tensor_tensor(hqc[:, k, :, :], hq[:, k, :, :], bc(cn[:, r, k:k + 1, :], 128, 2, NT), ALU.mult).then_inc(hqc_ready, 1)

                pool.wait_ge(hist_in[0], 16 * 8)
                for r in range(2):
                    for k in range(NS):
                        stage(r, r, k)
                for first, last in ((0, 1), (1, NR // 2 - 1)):
                    with pool.Fori(first, last) as j:
                        for r in range(2):
                            for k in range(NS):
                                scale(2 * j + r, r, k)
                            for k in range(NS):
                                pool.wait_ge(s2_done, NS * (2 * j + r) + k + 1)
                                stage(2 * j + r + 2, r, k)
                    if first == 0:
                        pool.wait_ge(hist_in[1], 16 * 8)
                for r in range(2):
                    for k in range(NS):
                        scale(NR - 2 + r, r, k)

            @block.tensor
            def _(pe):
                T, MM = nc.tensor.transpose, nc.tensor.matmul
                pe.wait_ge(dy_rowed, 1)
                for b in range(HB):
                    mm = T(psA[0:NT, b // 4, b % 4 * 128:(b % 4 + 1) * 128], dy[:, b, :], ident[:, :])
                    if b % 4 == 3:
                        mm.then_inc(dy_turned, 1)
                pe.wait_ge(dyt_ready, 4)
                def one_round(turn, r):
                    i = 2 * turn + r
                    for k in range(NS):
                        pe.wait_ge(staged, NS * i + k + 1)
                        for a in range(2):
                            mm = T(psA[0:NT, k, a * 128:(a + 1) * 128], dz[:, r, k, a, :], ident[:, :])
                        mm.then_inc(dz_turned, 1)
                        pe.wait_ge(added, NS * i + k + 1)
                        pe.wait_ge(loaded[r], LOADS * turn + LOADS)
                        MM(psB[0:NT, k, 0:NT], kq[:, 0, r, k, :], kq[:, 1, r, k, :], start=True, stop=True).then_inc(s1_done, 1)
                    for k in range(NS):
                        pe.wait_ge(dzt_ready, NS * i + k + 1)
                        pe.wait_ge(s1_ready, NS * i + k + 1)
                        for a in range(2):
                            o = slice(a * 128, (a + 1) * 128)
                            MM(psA[:, k, 256 + a * NT:256 + (a + 1) * NT], dzt[:, k, o], s1[:, k, :], start=True, stop=False)
                            mm = MM(psA[:, k, 256 + a * NT:256 + (a + 1) * NT], M["a0"][:, o], kq[:, 2, r, k, :], start=False, stop=True)
                        mm.then_inc(z_done, 1)
                    for k in range(NS):
                        pe.wait_ge(hq_ready, NS * i + k + 1)
                        for a in range(2):
                            mm = MM(psB[0:NT, k, 128:128 + NT], hs[:, r, k, a, :], hq[:, k, a, :], start=a == 0, stop=a == 1)
                        mm.then_inc(s2_done, 1)
                    for k in range(NS):
                        pe.wait_ge(hqc_ready, NS * i + k + 1)
                        pe.wait_ge(s2_ready, NS * i + k + 1)
                        for a in range(2):
                            MM(psB[0:NT, k, 256:256 + DM], hqc[:, k, a, :], M["b0"][:, a, 0, 0:DM], start=a == 0, stop=False)
                        MM(psB[0:NT, k, 256:256 + DM], s2[:, k, :], dyt[:, bass.ds(2 * i + k // 2, 1), k % 2 * DM:(k % 2 + 1) * DM].rearrange("p b d -> p (b d)"),
                           start=False, stop=True).then_inc(out_done, 1)

                with pe.Fori(0, NR // 2) as j:
                    for r in range(2):
                        one_round(j, r)

            @block.scalar
            def _(act):
                with act.Fori(0, NR) as i:
                    for k in range(NS):
                        act.wait_ge(dz_turned, NS * i + k + 1)
                        nc.scalar.activation(dzt[:, k, :], psA[0:NT, k, 0:FH], ACT.Copy).then_inc(dzt_ready, 1)
                    for k in range(NS):
                        act.wait_ge(z_done, NS * i + k + 1)
                        nc.scalar.activation(sg[:, k, :, :], zq(k), ACT.Sigmoid).then_inc(sg_ready, 1)

            @block.vector
            def _(dve):
                V = nc.vector
                V.sem_inc(added, NS)
                dve.wait_ge(h_back, 16)
                for j in range(4):
                    dve.wait_ge(dy_turned, j + 1)
                    V.tensor_copy(dyt[:, 4 * j:4 * j + 4, :].rearrange("p b c -> p (b c)"), psA[0:NT, j, :]).then_inc(dyt_ready, 1)
                def one_round(turn, r):
                    i = 2 * turn + r
                    for k in range(NS):
                        dve.wait_ge(s1_done, NS * i + k + 1)
                        V.tensor_tensor(s1[:, k, :], psB[0:NT, k, 0:NT], w[:, r, k, :], ALU.mult).then_inc(s1_ready, 1)
                    for k in range(NS):
                        dve.wait_ge(sg_ready, NS * i + k + 1)
                        V.tensor_tensor(hq[:, k, :, :], zq(k), sg[:, k, :, :], ALU.mult).then_inc(hq_ready, 1)
                    for k in range(NS):
                        dve.wait_ge(s2_done, NS * i + k + 1)
                        V.tensor_tensor(s2[:, k, :], psB[0:NT, k, 128:128 + NT], w[:, r, k, :], ALU.mult).then_inc(s2_ready, 1)
                    for k in range(NS):
                        dve.wait_ge(out_done, NS * i + k + 1)
                        row = H[:, bass.ds(batch(i, k), 1), :].rearrange("t b d -> t (b d)")
                        V.tensor_tensor(row, row, psB[0:NT, k, 256:256 + DM], ALU.add).then_inc(added, 1)

                with dve.Fori(0, NR // 2) as j:
                    for r in range(2):
                        one_round(j, r)
                dve.wait_ge(added, NB + NS)


def early_fusion(nc, out, A):
    with ExitStack() as ctx:
        sb = lambda n, sh: ctx.enter_context(nc.sbuf_tensor(n, sh, F32))
        ident = sb("ident", [128, 128])
        moved = ctx.enter_context(nc.semaphore("moved"))
        image = nc.dram_tensor("image_rows", [NB, S, S], F32).ap()
        with nc.Block() as block:
            @block.sync
            def _(sp):
                sp.dma_start(ident[:, :], A["c_ident"]).then_inc(moved, 16)
                sp.wait_ge(moved, 16)

        t = lambda n: A["L0_tok_" + n]
        image_network(nc, A["x"], image, ident, {n: A["c_" + n] for n in ("d1", "d2", "e1", "e2")},
                      t("fc0_w"), t("fc0_b"), [t(f"sw{i}") for i in range(NL)], [t(f"cw{i}") for i in range(NL)],
                      [t(f"cb{i}") for i in range(NL)], t("fc1_w"), t("fc1_b"), t("fc2_w"), t("fc2_b"))

        H_room = sb("H", [128, NB, DM])
        H = H_room[0:NT]
        ln = layernorm_semaphores(nc, ctx)
        with nc.Block() as block:
            @block.sync
            def _(sp):
                sp.dma_start(H[0:S, :, :], image.rearrange("b t d -> t b d")).then_inc(moved, 16)
                sp.dma_start(H[S:NT, :, :], A["txt"].rearrange("b t d -> t b d")).then_inc(moved, 16)
                sp.wait_ge(moved, 48)

        def normed(tag, stage):
            XT = stage.enter_context(nc.sbuf_tensor("XT_" + tag, [DM, TOK], F32))
            with ExitStack() as own:
                XN, squares = (own.enter_context(nc.sbuf_tensor(n + tag, [NT, NB, DM], F32)) for n in ("XN_", "squares_"))
                layernorm_transposed(nc, ln, "abcd".index(tag), H, XN, squares, XT, ident)
            return XT

        with ExitStack() as stage:
            XT = normed("a", stage)
            linear_attention(nc, H, XT, ident, A["c_rows"], A["L0_attn_Q"], A["L0_attn_E"])
        with ExitStack() as stage:
            XT = normed("b", stage)
            f = lambda n: A["L0_ffn_" + n]
            top_two_experts(nc, H, XT, f("router_w1"), f("router_b1"), f("router_w2"), f("router_b2"), f("expert_w1"), f("expert_b1"),
                            f("expert_w2"), f("expert_b2"), f("expert_w3"), f("expert_b3"))
        with ExitStack() as mem:
            M = memory_tensors(nc, mem)
            m = lambda n: A["L1_attn_" + n]
            with ExitStack() as stage:
                XT = normed("c", stage)
                memory_setup(nc, M, H, XT, ident, A["c_inject"], m("W_fused"), m("W0"), m("W1"), m("P0"), m("P1"))
            msb = lambda n, sh: mem.enter_context(nc.sbuf_tensor(n, sh, F32))
            hist_y = msb("hist_y", [128, NCH, HB, NC])
            memory_scan(nc, M, H_room, hist_y, ident, A["c_cols"], A["c_rows"], A["c_own"])
            memory_outputs(nc, M, H, hist_y, ident)
        with ExitStack() as stage:
            XT = normed("d", stage)
            w = lambda n: A["L1_ffn_" + n]
            best_expert(nc, H, XT, ident, w("gate_w"), w("gate_b"), w("w1"), w("b1"), w("w2"), w("b2"))
        with nc.Block() as block:
            @block.sync
            def _(sp):
                sp.dma_start(out.rearrange("b t d -> t b d"), H[:, :, :]).then_inc(moved, 16)
                sp.wait_ge(moved, 64)


def shape_constants():
    half = np.zeros((128, 2, 128), np.float32)
    half[:, 0, 0:64] = 1.0
    half[:, 1, 64:128] = 1.0
    return dict(spectral_constants(), ident=np.eye(128, dtype=np.float32), inject=(-2 * MAX_LR * np.eye(NT)).astype(np.float32),
                cols=half, rows=np.ascontiguousarray(half.transpose(2, 1, 0)), own=np.repeat(np.eye(QB, dtype=np.float32), NC, axis=0))


_INS = ['x', 'txt', 'L0_tok_fc0_w', 'L0_tok_fc0_b', 'L0_tok_sw0', 'L0_tok_cw0', 'L0_tok_cb0', 'L0_tok_sw1', 'L0_tok_cw1', 'L0_tok_cb1',
        'L0_tok_sw2', 'L0_tok_cw2', 'L0_tok_cb2', 'L0_tok_sw3', 'L0_tok_cw3', 'L0_tok_cb3', 'L0_tok_fc1_w', 'L0_tok_fc1_b', 'L0_tok_fc2_w',
        'L0_tok_fc2_b', 'L0_attn_Q', 'L0_attn_E', 'L0_ffn_router_w1', 'L0_ffn_router_b1', 'L0_ffn_router_w2', 'L0_ffn_router_b2',
        'L0_ffn_expert_w1', 'L0_ffn_expert_b1', 'L0_ffn_expert_w2', 'L0_ffn_expert_b2', 'L0_ffn_expert_w3', 'L0_ffn_expert_b3',
        'L1_attn_W_fused', 'L1_attn_W0', 'L1_attn_W1', 'L1_attn_P0', 'L1_attn_P1', 'L1_ffn_gate_w', 'L1_ffn_gate_b', 'L1_ffn_w1',
        'L1_ffn_b1', 'L1_ffn_w2', 'L1_ffn_b2']


def kernel(**inputs):
    import concourse.bacc as bacc
    from concourse.bass_utils import run_bass_kernel_spmd

    nc = bacc.Bacc("TRN2", target_bir_lowering=False, num_devices=1)
    arrays, A = {}, {}
    for name, a in [*((n, inputs[n]) for n in _INS), *(("c_" + n, a) for n, a in shape_constants().items())]:
        a = np.ascontiguousarray(a)
        arrays[f"in_{name}_dram"] = a
        A[name] = nc.dram_tensor(f"in_{name}_dram", a.shape, mybir.dt.from_np(a.dtype), kind="ExternalInput").ap()
    out = nc.dram_tensor("out_0_dram", (NB, NT, DM), F32, kind="ExternalOutput").ap()
    early_fusion(nc, out, A)
    r = run_bass_kernel_spmd(nc, [arrays], core_ids=[0])
    return r.results[0]["out_0_dram"]
```
